# Optimizing a Trainium2 kernel written in Bass

```python
import numpy as np
import jax
import jax.numpy as jnp

def _softmax(x, axis=-1):
    return jax.nn.softmax(x, axis=axis)

def _gelu(x):
    return jax.nn.gelu(x, approximate=True)

def _silu(x):
    return jax.nn.silu(x)

def _sigmoid(x):
    return jax.nn.sigmoid(x)

def _layernorm(x, axis=-1, eps=1e-05):
    m = jnp.mean(x, axis=axis, keepdims=True)
    v = jnp.var(x, axis=axis, keepdims=True)
    return (x - m) / jnp.sqrt(v + eps)

def _scatter_add(tgt, idx, src, axis=0):
    return tgt.at[idx].add(src)

def _segment_sum(src, seg, n):
    return jax.ops.segment_sum(src, seg, n)
kernel_name = 'mk_vit_tower_d1_tok_img768_r4_9704a6'

def setup_inputs(seed: int=0):
    np.random.seed(seed)
    _w = jnp.asarray

    def _rec_inputs():
        import jax
        import jax.numpy as jnp
        _rk = jax.random.key(seed)
        x = -0.000596345 + 1.00056 * jax.random.normal(jax.random.fold_in(_rk, 1), (16, 3, 64, 64), jnp.float32)
        return x
    x = _rec_inputs()

    def _L0_tok_setup():
        import jax, jax.numpy as jnp
        import numpy as np
        B = 16
        IMG = 64
        CH = 3
        EMBED = 64
        GP = 16
        PRE = [1, 2, 4]
        N_LEVELS = 3
        FUSED = EMBED * N_LEVELS

        def hilbert_flat_indices(n):
            t = np.arange(n * n, dtype=np.int64)
            x = np.zeros(n * n, dtype=np.int64)
            y = np.zeros(n * n, dtype=np.int64)
            s = 1
            while s < n:
                rx = 1 & t // 2
                ry = 1 & (t ^ rx)
                swap = ry == 0
                flip = swap & (rx == 1)
                x = np.where(flip, s - 1 - x, x)
                y = np.where(flip, s - 1 - y, y)
                x2 = np.where(swap, y, x)
                y2 = np.where(swap, x, y)
                x, y = (x2, y2)
                x = x + s * rx
                y = y + s * ry
                t = t // 4
                s *= 2
            return y * n + x

        def _level(x, idx, W, b, p, gp):
            Bsz, C, H, _ = x.shape
            h = H // p
            t = x.reshape(Bsz, C, h, p, h, p).transpose(0, 2, 4, 3, 5, 1).reshape(Bsz, h * h, p * p * C)
            t = t[:, idx]
            t = t.reshape(Bsz, h * h // gp, gp * p * p * C)
            return t @ W.T + b

        def _interp_linear(x, n_out):
            L = x.shape[1]
            pos = (jnp.arange(n_out, dtype=jnp.float32) + 0.5) * (L / n_out) - 0.5
            pos = jnp.clip(pos, 0.0, L - 1)
            i0 = jnp.floor(pos).astype(jnp.int32)
            i1 = jnp.minimum(i0 + 1, L - 1)
            w = (pos - i0).astype(x.dtype)
            return x[:, i0] * (1.0 - w)[None, :, None] + x[:, i1] * w[None, :, None]
        key = jax.random.key(seed)
        ks = jax.random.split(key, 9)
        inp = {'x': jax.random.normal(ks[0], (B, CH, IMG, IMG), jnp.float32)}
        for i, p in enumerate(PRE):
            din = CH * p * p * GP
            inp[f'W{i}'] = jax.random.normal(ks[1 + 2 * i], (EMBED, din), jnp.float32) * din ** (-0.5)
            inp[f'b{i}'] = jax.random.normal(ks[2 + 2 * i], (EMBED,), jnp.float32) * 0.02
        inp['Wf'] = jax.random.normal(ks[7], (FUSED, FUSED), jnp.float32) * FUSED ** (-0.5)
        inp['bf'] = jax.random.normal(ks[8], (FUSED,), jnp.float32) * 0.02
        for i, p in enumerate(PRE):
            inp[f'idx{i}'] = jnp.asarray(hilbert_flat_indices(IMG // p), jnp.int32)
        return inp
    _L0_tok_all = _L0_tok_setup()
    _L0_tok_in = {k: v for k, v in _L0_tok_all.items() if k in ('W0', 'b0', 'W1', 'b1', 'W2', 'b2', 'Wf', 'bf', 'idx0', 'idx1', 'idx2')}
    del _L0_tok_all

    def _L0_attn_setup():
        import jax, jax.numpy as jnp
        import numpy as np
        L = 14
        H = 12
        HD = 64

        def rel_pos_embed(N, table_v, table_h):
            n = N - 1
            s = int(n ** 0.5)
            r = jnp.arange(n)
            dv = r[None, :] // s - r[:, None] // s
            dh = r[None, :] % s - r[:, None] % s
            iv = jnp.clip(dv, -L, L) + L + 1
            ih = jnp.clip(dh, -L, L) + L + 1
            iv = jnp.pad(iv, ((1, 0), (1, 0)))
            ih = jnp.pad(ih, ((1, 0), (1, 0)))
            return table_v[iv] + table_h[ih]
        key = jax.random.key(seed)
        ks = jax.random.split(key, 11)
        B, N, E = (64, 197, 192)
        T = 2 * L + 2
        std = 0.02
        return {'x': jax.random.normal(ks[0], (B, N, E), jnp.float32), 'wq': jax.random.normal(ks[1], (E, H * HD), jnp.float32) * std, 'wk': jax.random.normal(ks[2], (E, H * HD), jnp.float32) * std, 'wv': jax.random.normal(ks[3], (E, H * HD), jnp.float32) * std, 'wproj': jax.random.normal(ks[4], (H * HD, E), jnp.float32) * std, 'bproj': jnp.zeros((E,), jnp.float32), 'rk_v': jax.random.normal(ks[5], (T, HD), jnp.float32) * std, 'rk_h': jax.random.normal(ks[6], (T, HD), jnp.float32) * std, 'rv_v': jax.random.normal(ks[7], (T, HD), jnp.float32) * std, 'rv_h': jax.random.normal(ks[8], (T, HD), jnp.float32) * std}
    _L0_attn_all = _L0_attn_setup()
    _L0_attn_in = {k: v for k, v in _L0_attn_all.items() if k in ('wq', 'wk', 'wv', 'wproj', 'bproj', 'rk_v', 'rk_h', 'rv_v', 'rv_h')}
    del _L0_attn_all

    def _L0_ffn_setup():
        import math
        import jax, jax.numpy as jnp
        import numpy as np
        B, L, D = (8, 1024, 192)
        E = 16
        TOP_K = 2
        F_EXP = 4 * D
        F_SH = F_EXP * 2 // 4
        key = jax.random.key(seed)
        ks = jax.random.split(key, 8)
        s = lambda fan_in: 1.0 / math.sqrt(fan_in)
        return {'hidden_states': jax.random.normal(ks[0], (B, L, D), jnp.float32), 'gate_weight': jax.random.uniform(ks[1], (E, D), jnp.float32, -s(D), s(D)), 'Wg': jax.random.uniform(ks[2], (E, F_EXP, D), jnp.float32, -s(D), s(D)), 'Wu': jax.random.uniform(ks[3], (E, F_EXP, D), jnp.float32, -s(D), s(D)), 'Wd': jax.random.uniform(ks[4], (E, D, F_EXP), jnp.float32, -s(F_EXP), s(F_EXP)), 'Ws_g': jax.random.uniform(ks[5], (F_SH, D), jnp.float32, -s(D), s(D)), 'Ws_u': jax.random.uniform(ks[6], (F_SH, D), jnp.float32, -s(D), s(D)), 'Ws_d': jax.random.uniform(ks[7], (D, F_SH), jnp.float32, -s(F_SH), s(F_SH))}
    _L0_ffn_all = _L0_ffn_setup()
    _L0_ffn_in = {k: v for k, v in _L0_ffn_all.items() if k in ('gate_weight', 'Wg', 'Wu', 'Wd', 'Ws_g', 'Ws_u', 'Ws_d')}
    del _L0_ffn_all
    return {'x': x, 'L0_tok_W0': _L0_tok_in['W0'], 'L0_tok_b0': _L0_tok_in['b0'], 'L0_tok_W1': _L0_tok_in['W1'], 'L0_tok_b1': _L0_tok_in['b1'], 'L0_tok_W2': _L0_tok_in['W2'], 'L0_tok_b2': _L0_tok_in['b2'], 'L0_tok_Wf': _L0_tok_in['Wf'], 'L0_tok_bf': _L0_tok_in['bf'], 'L0_tok_idx0': _L0_tok_in['idx0'], 'L0_tok_idx1': _L0_tok_in['idx1'], 'L0_tok_idx2': _L0_tok_in['idx2'], 'L0_attn_wq': _L0_attn_in['wq'], 'L0_attn_wk': _L0_attn_in['wk'], 'L0_attn_wv': _L0_attn_in['wv'], 'L0_attn_wproj': _L0_attn_in['wproj'], 'L0_attn_bproj': _L0_attn_in['bproj'], 'L0_attn_rk_v': _L0_attn_in['rk_v'], 'L0_attn_rk_h': _L0_attn_in['rk_h'], 'L0_attn_rv_v': _L0_attn_in['rv_v'], 'L0_attn_rv_h': _L0_attn_in['rv_h'], 'L0_ffn_gate_weight': _L0_ffn_in['gate_weight'], 'L0_ffn_Wg': _L0_ffn_in['Wg'], 'L0_ffn_Wu': _L0_ffn_in['Wu'], 'L0_ffn_Wd': _L0_ffn_in['Wd'], 'L0_ffn_Ws_g': _L0_ffn_in['Ws_g'], 'L0_ffn_Ws_u': _L0_ffn_in['Ws_u'], 'L0_ffn_Ws_d': _L0_ffn_in['Ws_d']}

def reference(x, L0_tok_W0, L0_tok_b0, L0_tok_W1, L0_tok_b1, L0_tok_W2, L0_tok_b2, L0_tok_Wf, L0_tok_bf, L0_tok_idx0, L0_tok_idx1, L0_tok_idx2, L0_attn_wq, L0_attn_wk, L0_attn_wv, L0_attn_wproj, L0_attn_bproj, L0_attn_rk_v, L0_attn_rk_h, L0_attn_rv_v, L0_attn_rv_h, L0_ffn_gate_weight, L0_ffn_Wg, L0_ffn_Wu, L0_ffn_Wd, L0_ffn_Ws_g, L0_ffn_Ws_u, L0_ffn_Ws_d):
    import jax
    import jax.numpy as jnp

    def _L0_tok_ref(x, W0, b0, W1, b1, W2, b2, Wf, bf, idx0, idx1, idx2):
        import jax, jax.numpy as jnp
        import numpy as np
        B = 16
        IMG = 64
        CH = 3
        EMBED = 64
        GP = 16
        PRE = [1, 2, 4]
        N_LEVELS = 3
        FUSED = EMBED * N_LEVELS

        def hilbert_flat_indices(n):
            t = np.arange(n * n, dtype=np.int64)
            x = np.zeros(n * n, dtype=np.int64)
            y = np.zeros(n * n, dtype=np.int64)
            s = 1
            while s < n:
                rx = 1 & t // 2
                ry = 1 & (t ^ rx)
                swap = ry == 0
                flip = swap & (rx == 1)
                x = np.where(flip, s - 1 - x, x)
                y = np.where(flip, s - 1 - y, y)
                x2 = np.where(swap, y, x)
                y2 = np.where(swap, x, y)
                x, y = (x2, y2)
                x = x + s * rx
                y = y + s * ry
                t = t // 4
                s *= 2
            return y * n + x

        def _level(x, idx, W, b, p, gp):
            Bsz, C, H, _ = x.shape
            h = H // p
            t = x.reshape(Bsz, C, h, p, h, p).transpose(0, 2, 4, 3, 5, 1).reshape(Bsz, h * h, p * p * C)
            t = t[:, idx]
            t = t.reshape(Bsz, h * h // gp, gp * p * p * C)
            return t @ W.T + b

        def _interp_linear(x, n_out):
            L = x.shape[1]
            pos = (jnp.arange(n_out, dtype=jnp.float32) + 0.5) * (L / n_out) - 0.5
            pos = jnp.clip(pos, 0.0, L - 1)
            i0 = jnp.floor(pos).astype(jnp.int32)
            i1 = jnp.minimum(i0 + 1, L - 1)
            w = (pos - i0).astype(x.dtype)
            return x[:, i0] * (1.0 - w)[None, :, None] + x[:, i1] * w[None, :, None]
        Ws = [(idx0, W0, b0, PRE[0]), (idx1, W1, b1, PRE[1]), (idx2, W2, b2, PRE[2])]
        outs = [_level(x, idx, W, b, p, GP) for idx, W, b, p in Ws]
        n_tokens = outs[0].shape[1]
        outs = [outs[0]] + [_interp_linear(o, n_tokens) for o in outs[1:]]
        y = jnp.concatenate(outs, axis=-1)
        return y @ Wf.T + bf

    def _L0_attn_ref(x, wq, wk, wv, wproj, bproj, rk_v, rk_h, rv_v, rv_h):
        import jax, jax.numpy as jnp
        import numpy as np
        L = 14
        H = 12
        HD = 64

        def rel_pos_embed(N, table_v, table_h):
            n = N - 1
            s = int(n ** 0.5)
            r = jnp.arange(n)
            dv = r[None, :] // s - r[:, None] // s
            dh = r[None, :] % s - r[:, None] % s
            iv = jnp.clip(dv, -L, L) + L + 1
            ih = jnp.clip(dh, -L, L) + L + 1
            iv = jnp.pad(iv, ((1, 0), (1, 0)))
            ih = jnp.pad(ih, ((1, 0), (1, 0)))
            return table_v[iv] + table_h[ih]
        B, N, E = x.shape
        scale = HD ** (-0.5)
        q = (x @ wq).reshape(B, N, H, HD).transpose(0, 2, 1, 3)
        k = (x @ wk).reshape(B, N, H, HD).transpose(0, 2, 1, 3)
        v = (x @ wv).reshape(B, N, H, HD).transpose(0, 2, 1, 3)
        attn = jnp.einsum('bhid,bhjd->bhij', q, k) * scale
        rpk = rel_pos_embed(N, rk_v, rk_h)
        attn = attn + jnp.einsum('bhid,ijd->bhij', q, rpk) * scale
        attn = jax.nn.softmax(attn, axis=-1)
        out = jnp.einsum('bhij,bhjd->bhid', attn, v)
        rpv = rel_pos_embed(N, rv_v, rv_h)
        out = out + jnp.einsum('bhij,ijd->bhid', attn, rpv)
        out = out.transpose(0, 2, 1, 3).reshape(B, N, H * HD)
        return out @ wproj + bproj

    def _L0_ffn_ref(hidden_states, gate_weight, Wg, Wu, Wd, Ws_g, Ws_u, Ws_d):
        import math
        import jax, jax.numpy as jnp
        import numpy as np
        B, L, D = (8, 1024, 192)
        E = 16
        TOP_K = 2
        F_EXP = 4 * D
        F_SH = F_EXP * 2 // 4
        b, l, d = hidden_states.shape
        n = b * l
        x = hidden_states.reshape(n, d)
        scores = jax.nn.sigmoid(x @ gate_weight.T)
        capacity = math.ceil(n / E * TOP_K)
        topk_score, topk_ids = jax.lax.top_k(scores.T, capacity)
        xg = x[topk_ids]
        gate = jax.nn.silu(jnp.einsum('ecd,efd->ecf', xg, Wg))
        up = jnp.einsum('ecd,efd->ecf', xg, Wu)
        out = jnp.einsum('ecf,edf->ecd', gate * up, Wd)
        out = out * topk_score[..., None]
        y = jnp.zeros((n, d), x.dtype).at[topk_ids.reshape(-1)].add(out.reshape(-1, d))
        y = y.reshape(b, l, d)
        shared = jax.nn.silu(hidden_states @ Ws_g.T) * (hidden_states @ Ws_u.T) @ Ws_d.T
        return y + shared
    h = _L0_tok_ref(x, L0_tok_W0, L0_tok_b0, L0_tok_W1, L0_tok_b1, L0_tok_W2, L0_tok_b2, L0_tok_Wf, L0_tok_bf, L0_tok_idx0, L0_tok_idx1, L0_tok_idx2)
    h = h + _L0_attn_ref(_layernorm(h, axis=-1), L0_attn_wq, L0_attn_wk, L0_attn_wv, L0_attn_wproj, L0_attn_bproj, L0_attn_rk_v, L0_attn_rk_h, L0_attn_rv_v, L0_attn_rv_h)
    h = h + _L0_ffn_ref(_layernorm(h, axis=-1), L0_ffn_gate_weight, L0_ffn_Wg, L0_ffn_Wu, L0_ffn_Wd, L0_ffn_Ws_g, L0_ffn_Ws_u, L0_ffn_Ws_d)
    return h

_drawn_inputs = setup_inputs


def setup_inputs(seed=0):
    import zlib

    import numpy as np

    out = dict(_drawn_inputs(seed))
    spreads = {'L0_attn_bproj': (0.0, 0.1)}
    factors = {'L0_tok_b0': 4.159,
     'L0_tok_b1': 4.217,
     'L0_tok_b2': 3.758,
     'L0_attn_wq': 8.0,
     'L0_attn_wk': 8.0,
     'L0_attn_rk_v': 8.0,
     'L0_attn_rk_h': 8.0,
     'L0_attn_rv_v': 8.0,
     'L0_attn_rv_h': 8.0}
    for name, (base, spread) in spreads.items():
        noise = np.random.default_rng([zlib.crc32(name.encode()), seed]).standard_normal(out[name].shape)
        drawn = base * np.exp(spread * noise) if base else spread * noise
        out[name] = jnp.asarray(drawn.astype(out[name].dtype))
    for name, factor in factors.items():
        out[name] = (out[name] * factor).astype(out[name].dtype)
    return out
```

```python
from contextlib import ExitStack

import concourse.bass as bass
from concourse import mybir

F32 = mybir.dt.float32
F32R = mybir.dt.float32r
I32 = mybir.dt.int32
U32 = mybir.dt.uint32
ALU = mybir.AluOpType
ACT = mybir.ActivationFunctionType
AX = mybir.AxisListType

B, IMG, CH = 16, 64, 3
GP = 16
EMB = 64
D = 192
NT = 256
T = B * NT
NTILE = T // 128
H, HD = 12, 64
SIDE = 15
ROWS = (NT - 1) // SIDE
EPS = 1e-5
E, CAP, FE, FS = 16, 512, 768, 384


class Mem:

    def __init__(self, nc, ctx, phase):
        self.nc, self.ctx, self.phase = nc, ctx, phase
        self.sems = []
        ctx.callback(self.clear)

    def clear(self):
        if self.sems:
            self.nc.clear_and_free_semaphores(self.sems)
            self.nc.all_engine_barrier()

    def sb(self, name, shape, dt=F32):
        return self.ctx.enter_context(self.nc.sbuf_tensor(f"{self.phase}_{name}", shape, dt))

    def psum(self, name, shape):
        return self.ctx.enter_context(self.nc.psum_tensor(f"{self.phase}_{name}", shape, F32))

    def sem(self, name):
        self.sems.append(self.nc.alloc_semaphore(name=f"{self.phase}_{name}"))
        return self.sems[-1]


def norm_stats(dve, h, stat, raw, t, last, s_hf, s_bn, s_agg, tile=lambda k: k):
    for k in ([t] if t + 1 < last else [t, t + 1, t + 2]):
        if 1 <= k <= last:
            dve.wait_ge(s_hf, k)
            if k >= 3:
                dve.wait_ge(s_agg, k - 2)
            dve.bn_stats(raw[:, (k - 1) % 2, :], h[:, tile(k - 1), :]).then_inc(s_bn, 1)
        if 2 <= k:
            dve.wait_ge(s_bn, k - 1)
            dve.bn_aggr(stat[:, tile(k - 2), 0:2], raw[:, k % 2, :]).then_inc(s_agg, 1)


def tokenize(nc, A, h, ident, stat):
    with ExitStack() as ctx:
        m = Mem(nc, ctx, "tokenize")
        idx0 = m.sb("idx0", [128, 2 * GP], I32)
        idx1 = m.sb("idx1", [64, GP], I32)
        idx2 = m.sb("idx2", [128, 2], I32)
        w0 = m.sb("w0", [48, EMB])
        w1a = m.sb("w1a", [128, EMB])
        w1b = m.sb("w1b", [64, EMB])
        w2 = m.sb("w2", [48, GP, EMB])
        wfa = m.sb("wfa", [128, D])
        wfb = m.sb("wfb", [64, D])
        bias = m.sb("bias", [64, 3])
        bf = m.sb("bf", [128, D])
        g0 = m.sb("g0", [128, 2, GP, B * CH])
        g0r = m.sb("g0r", [128, 2, B, GP * CH])
        g1 = m.sb("g1", [64, GP, B * 12])
        g1r = m.sb("g1r", [64, B, GP * 12])
        g2 = m.sb("g2", [128, 2, B * 48])
        t0 = m.sb("t0", [48, B, 2, 128])
        t1a = m.sb("t1a", [128, B, 64])
        t1b = m.sb("t1b", [64, B, 64])
        t2 = m.sb("t2", [48, 2 * B, 8, GP])
        o1 = m.sb("o1", [64, B, 66])
        o2 = m.sb("o2", [64, B, 18])
        part = m.sb("part", [64, B, 64])
        ct = m.sb("ct", [128, B, NT])
        ct2 = m.sb("ct2", [64, B, NT])
        raw = m.sb("tok_bn", [128, 2, 6])
        ps = m.psum("ps_tok", [128, 8, 512])

        s_idx = m.sem("idx_loaded")
        s_w = m.sem("tok_weights_loaded")
        s_g2, s_g1 = m.sem("g2_gathered"), m.sem("g1_gathered")
        s_g0 = [m.sem(f"g0_gathered{i}") for i in range(2)]
        s_reord, s_reord0 = m.sem("g1_reordered"), m.sem("g0_reordered")
        s_pe = m.sem("tok_pe_done")
        s_ev = m.sem("tok_bank_read")
        s_dv = m.sem("tok_dve")
        s_ct = m.sem("ct_ready")
        s_wf = m.sem("fused")
        s_hf = m.sem("h_written")
        s_bn = m.sem("bn_stats_done")
        s_agg = m.sem("bn_aggregated")

        N2, N1, N0, NJ = 8, 8 + 1 + 4, 8 + 1 + 4 + 2, 8 + 1 + 4 + 2 + 16

        def tile(n):
            return 2 * (n % B) + n // B


        with nc.Block() as block:

            @block.sync
            def _(sp):
                sp.dma_start(idx2[:, :], A["idx2t"]).then_inc(s_idx, 16)
                sp.dma_start(idx1[:, :], A["idx1t"]).then_inc(s_idx, 16)
                sp.dma_start(idx0[:, :], A["idx0t"]).then_inc(s_idx, 16)
                sp.dma_start(ident[:, :], A["ident"]).then_inc(s_w, 16)
                sp.dma_start(w0[:, :], A["w0t"]).then_inc(s_w, 16)
                sp.dma_start(w1a[:, :], A["w1t"][0:128, :]).then_inc(s_w, 16)
                sp.dma_start(w1b[:, :], A["w1t"][128:192, :]).then_inc(s_w, 16)
                sp.dma_start(w2[:, :, :], A["w2t"]).then_inc(s_w, 16)
                sp.dma_start(wfa[:, :], A["wft"][0:128, :]).then_inc(s_w, 16)
                sp.dma_start(wfb[:, :], A["wft"][128:192, :]).then_inc(s_w, 16)
                sp.dma_start(bias[:, :], A["tokb"]).then_inc(s_w, 16)
                sp.dma_start(bf[:, :], A["bf"].partition_broadcast(128)).then_inc(s_w, 16)

            @block.gpsimd
            def _(pool):
                def gather(dst, table, index, done):
                    pool.indirect_dma_start(
                        out=dst, out_offset=None, in_=table,
                        in_offset=bass.IndirectOffsetOnAxis(ap=index.bitcast(U32), axis=0)).then_inc(done, 16)

                pool.wait_ge(s_idx, 48)
                for i in range(2):
                    gather(g2[:, i, :], A["x2"], idx2[:, i:i + 1], s_g2)
                for s in range(GP):
                    gather(g1[:, s, :], A["x1"], idx1[:, s:s + 1], s_g1)
                for i in range(2):
                    for s in range(GP):
                        gather(g0[:, i, s, :], A["x0"], idx0[:, i * GP + s:i * GP + s + 1], s_g0[i])

            @block.vector
            def _(dve):
                dve.wait_ge(s_g1, 16 * GP)
                dve.tensor_copy(g1r[:, :, :].rearrange("p b (s f) -> p b s f", s=GP),
                                g1[:, :, :].rearrange("p s (b f) -> p b s f", b=B)).then_inc(s_reord, 1)
                done = 0

                def step(ins):
                    nonlocal done
                    done += 1
                    ins.then_inc(s_dv, 1)
                    dve.wait_ge(s_dv, done)

                def interpolate(o, n, dst):
                    step(dve.tensor_copy(o[:, :, 0:1], o[:, :, 1:2]))
                    step(dve.tensor_copy(o[:, :, n + 1:n + 2], o[:, :, n:n + 1]))
                    r = NT // n
                    out = dst.rearrange("p b (k r) -> p b k r", r=r)
                    for i in range(r):
                        f = (i + 0.5) / r - 0.5
                        low = 0 if f < 0 else 1
                        wt = f + 1 if f < 0 else f
                        step(dve.tensor_scalar(part[:, :, 0:n], o[:, :, low:low + n], 1.0 - wt, None, ALU.mult))
                        ins = dve.scalar_tensor_tensor(out[:, :, :, i], o[:, :, low + 1:low + 1 + n], wt,
                                                       part[:, :, 0:n], ALU.mult, ALU.add)
                        step(ins)

                dve.wait_ge(s_ev, N2 + 1)
                interpolate(o2, 16, ct2[:, :, :])
                dve.wait_ge(s_ev, N1 + 2)
                interpolate(o1, 64, ct[64:128, :, :])
                dve.tensor_copy(part[0:1, 0, 0:1], o1[0:1, 0, 0:1]).then_inc(s_ct, 1)
                dve.wait_ge(s_w, 16 * 9)
                for n in range(NTILE):
                    dve.wait_ge(s_wf, n + 1)
                    dve.tensor_tensor(h[:, tile(n), :], ps[:, n % 8, 0:D], bf[:, :], ALU.add).then_inc(s_hf, 1)
                    norm_stats(dve, h, stat, raw, n, NTILE, s_hf, s_bn, s_agg, tile)

            @block.scalar
            def _(act):
                n = 0

                def evac(dst, src, bias_col=None):
                    nonlocal n
                    act.wait_ge(s_pe, n + 1)
                    if bias_col is None:
                        act.activation(dst, src, ACT.Copy).then_inc(s_ev, 1)
                    else:
                        act.activation(dst, src, ACT.Identity, bias=bias[:, bias_col:bias_col + 1]).then_inc(s_ev, 1)
                    n += 1

                act.wait_ge(s_w, 16 * 9)
                for j in range(8):
                    evac(t2[:, 4 * j:4 * j + 4, :, :].rearrange("p a g s -> p (a g s)"), ps[0:48, n % 8, :])
                evac(o2[:, :, 1:17], ps[0:64, n % 8, 0:256].rearrange("p (b g) -> p b g", b=B), 2)
                for j in range(2):
                    evac(t1a[:, 8 * j:8 * j + 8, :].rearrange("p b g -> p (b g)"), ps[:, n % 8, :])
                    evac(t1b[:, 8 * j:8 * j + 8, :].rearrange("p b g -> p (b g)"), ps[0:64, n % 8, :])
                for j in range(2):
                    evac(o1[:, 8 * j:8 * j + 8, 1:65], ps[0:64, n % 8, :].rearrange("p (b g) -> p b g", b=8), 1)
                for i in range(2):
                    act.wait_ge(s_g0[i], 16 * GP)
                    act.activation(g0r[:, i, :, :].rearrange("p b (s f) -> p b s f", s=GP),
                                   g0[:, i, :, :].rearrange("p s (b f) -> p b s f", b=B), ACT.Copy).then_inc(s_reord0, 1)
                    for j in range(4):
                        evac(t0[:, 4 * j:4 * j + 4, i, :], ps[0:48, n % 8, :].rearrange("p (b g) -> p b g", b=4))
                    for j in range(4):
                        evac(ct[0:64, 4 * j:4 * j + 4, 128 * i:128 * i + 128],
                             ps[0:64, n % 8, :].rearrange("p (b g) -> p b g", b=4), 0)
                assert n == NJ

            @block.tensor
            def _(pe):
                n = 0

                def bank():
                    if n >= 8:
                        pe.wait_ge(s_ev, n - 7)
                    return n % 8

                pe.wait_ge(s_w, 16 * 9)
                pe.wait_ge(s_g2, 32)
                for j in range(8):
                    k = bank()
                    for q in range(4):
                        b, i = 2 * j + q // 2, q % 2
                        last = pe.transpose(ps[0:48, k, 128 * q:128 * q + 128], g2[:, i, 48 * b:48 * b + 48], ident[:, :])
                    last.then_inc(s_pe, 1)
                    n += 1
                k = bank()
                pe.wait_ge(s_ev, 8)
                for s in range(GP):
                    last = pe.matmul(ps[0:64, k, 0:256], w2[:, s, :], t2[:, :, :, s], start=(s == 0), stop=(s == GP - 1))
                last.then_inc(s_pe, 1)
                n += 1
                pe.wait_ge(s_reord, 1)
                for j in range(2):
                    for lo, wide in ((0, 128), (128, 64)):
                        k = bank()
                        for q in range(8):
                            last = pe.transpose(ps[0:wide, k, 64 * q:64 * q + 64], g1r[:, 8 * j + q, lo:lo + wide],
                                                ident[0:64, 0:64])
                        last.then_inc(s_pe, 1)
                        n += 1
                pe.wait_ge(s_ev, N1)
                for j in range(2):
                    k = bank()
                    pe.matmul(ps[0:64, k, :], w1a[:, :], t1a[:, 8 * j:8 * j + 8, :].rearrange("p b g -> p (b g)"), start=True, stop=False)
                    pe.matmul(ps[0:64, k, :], w1b[:, :], t1b[:, 8 * j:8 * j + 8, :].rearrange("p b g -> p (b g)"),
                              start=False, stop=True).then_inc(s_pe, 1)
                    n += 1
                for i in range(2):
                    if i:
                        pe.wait_ge(s_hf, B)
                    pe.wait_ge(s_reord0, 1 + i)
                    for j in range(4):
                        k = bank()
                        for q in range(4):
                            last = pe.transpose(ps[0:48, k, 128 * q:128 * q + 128], g0r[:, i, 4 * j + q, :], ident[:, :])
                        last.then_inc(s_pe, 1)
                        n += 1
                    pe.wait_ge(s_ev, N0 + 8 * i + 4)
                    for j in range(4):
                        k = bank()
                        pe.matmul(ps[0:64, k, :], w0[:, :], t0[:, 4 * j:4 * j + 4, i, :], start=True, stop=True).then_inc(s_pe, 1)
                        n += 1
                    pe.wait_ge(s_ct, 1)
                    pe.wait_ge(s_ev, N0 + 8 * i + 8)
                    for b in range(B):
                        t = B * i + b
                        if b >= 8:
                            pe.wait_ge(s_hf, t - 7)
                        pe.matmul(ps[:, t % 8, 0:D], ct[:, b, 128 * i:128 * i + 128], wfa[:, :], start=True, stop=False)
                        pe.matmul(ps[:, t % 8, 0:D], ct2[:, b, 128 * i:128 * i + 128], wfb[:, :], start=False, stop=True).then_inc(s_wf, 1)


def five_passes(pe, out, w, x, x_stationary=False):
    pairs = [(w[0], x[0]), (w[0], x[1]), (w[1], x[0]), (w[2], x[2]), (w[3], x[2])]
    for i, (a, b) in enumerate(pairs):
        if x_stationary:
            a, b = b, a
        last = pe.matmul(out, a, b, start=(i == 0), stop=(i == len(pairs) - 1))
    return last


def group_pairs(eng, body):
    G = T // 512
    with eng.Fori(0, G // 2 - 1) as i:
        for u in range(2):
            body(2 * i + u, i, u, True)
    for u in range(2):
        body(G - 2 + u, G // 2 - 1, u, u == 0)


def normalize_group(dve, h, stat, xn, g, u, done):
    for t in range(4):
        tile = bass.ds(4 * g + t, 1)
        for lo, n, c in ((0, D, 0), (D, 64, 128)):
            ins = dve.tensor_scalar(xn[:, u, t:t + 1, lo:lo + n], h[:, tile, c:c + n],
                                    stat[:, tile, 0], stat[:, tile, 1], ALU.subtract, ALU.mult)
    ins.then_inc(done, 1)


def transpose_group(pe, ps, xn, u, ident, done, bank=0):
    for k in range(2):
        for t in range(4):
            last = pe.transpose(ps[:, bank + k, 128 * t:128 * t + 128], xn[:, u, t, 128 * k:128 * k + 128], ident[:, :])
    last.then_inc(done, 1)


def project(nc, A, S, h, ident, stat, epsc):
    G = T // 512
    WQ = H * HD
    with ExitStack() as ctx:
        m = Mem(nc, ctx, "project")
        xhi = m.sb("xhi", [128, B, NT], F32R)
        xlo = m.sb("xlo", [128, B, NT], F32R)
        xmix = m.sb("xmix", [128, B, NT], F32R)
        vhi = m.sb("vhi", [128, 2, 512], F32R)
        vlo = m.sb("vlo", [128, 2, 512], F32R)
        vmix = m.sb("vmix", [128, 2, 512], F32R)
        whi, wlo = m.sb("whi", [128, 3 * WQ], F32R), m.sb("wlo", [128, 3 * WQ], F32R)
        w2hi, w2lo = m.sb("w2hi", [128, 3 * WQ], F32R), m.sb("w2lo", [128, 3 * WQ], F32R)
        cq = [m.sb(f"cq{i}", [128, 3, 128, 4], F32R) for i in range(4)]
        krow = m.sb("krow", [128, 2])
        vrow = m.sb("vrow", [1, 2, WQ])
        rk = m.sb("rk", [HD, 128])
        rk0 = m.sb("rk0", [HD, 32])
        std = m.sb("std", [128, NTILE])
        ps = m.psum("ps_proj", [128, 8, 512])

        s_w, s_c = m.sem("proj_weights_loaded"), m.sem("proj_tables_loaded")
        s_std, s_rstd = m.sem("std_ready"), m.sem("rstd_ready")
        s_rk = m.sem("tables_ready")
        s_cp, s_chi, s_clo = m.sem("composed"), m.sem("composed_hi"), m.sem("composed_lo")
        s_whi, s_wlo = m.sem("w_hi_made"), m.sem("w_lo_made")
        s_xn, s_tr = m.sem("normed"), m.sem("x_transposed")
        s_hi, s_lo = m.sem("x_hi_made"), m.sem("x_lo_made")
        s_vx = [m.sem(f"v_operand_copied{i}") for i in range(2)]
        s_vused = m.sem("v_operand_used")
        s_q, s_k, s_v = m.sem("q_product"), m.sem("k_product"), m.sem("v_product")
        s_qe, s_ke, s_ve = m.sem("q_read"), m.sem("k_read"), m.sem("v_read")
        s_k0, s_v0 = m.sem("key0_done"), m.sem("value0_done")
        s_qst = [m.sem(f"q_stored{i}") for i in range(2)]
        s_kst = [m.sem(f"k_stored{i}") for i in range(2)]
        s_vst = [m.sem(f"v_stored{i}") for i in range(4)]
        s_f, s_fa, s_fd = m.sem("f_product"), m.sem("f_read_act"), m.sem("f_read_dve")
        s_fz = m.sem("f_zeroed")
        s_fst = [m.sem(f"f_stored{i}") for i in range(2)]

        with ExitStack() as raw_ctx:
            r = Mem(nc, raw_ctx, "project")
            rawa, rawb = r.sb("w_raw_a", [128, 3 * WQ]), r.sb("w_raw_b", [128, 3 * WQ])
            wqt = r.sb("wqt", [HD, H, 256])
        fbuf = [m.sb(f"f_{k}", [128, B, NT]) for k in "ac"]
        xn = m.sb("xn", [128, 2, 4, 256])
        qst, kst = m.sb("q_stage", [128, 2, 512]), m.sb("k_stage", [128, 2, 512])
        vst = fbuf[1][:, :, :].rearrange("p b t -> p (b t)")[:, 0:4 * WQ].rearrange("p (s n) -> p s n", s=4)

        blocks = [(0, 1, 1, 96, 0)]
        blocks += [(1 + SIDE * a, SIDE, 1, 16 - a, 0) for a in range(ROWS)]
        blocks += [(1 + c, ROWS, SIDE, 48 + 14 - c, 1) for c in range(SIDE)]
        NB = len(blocks)

        def pair_of_images(ap):
            return ap.rearrange("p (b t) -> p b t", b=2)

        def store_feature_waits(n_blocks):
            return (n_blocks + 1) // 2, n_blocks // 2

        def read_feature(eng, n, done):
            q, (first, count, step, _, k) = n // NB, blocks[n % NB]
            if q:
                eng.wait_ge(s_fst[k], 16 * q)
            eng.wait_ge(s_f, n + 1)
            dst = fbuf[k][:, :, first:first + (count - 1) * step + 1:step].rearrange("p b t -> p t b")
            src = ps[:, n % 8, 0:count * B].rearrange("p (t b) -> p t b", b=B)
            if done is s_fa:
                eng.activation(dst, src, ACT.Copy).then_inc(done, 1)
            else:
                eng.tensor_copy(dst, src).then_inc(done, 1)

        with nc.Block() as block:

            @block.sync
            def _(sp):
                sp.dma_start(rk[:, :], A["rk"]).then_inc(s_c, 16)
                sp.dma_start(rk0[:, :], A["rk0"]).then_inc(s_c, 16)
                sp.dma_start(wqt[:, :, :], A["wqt"]).then_inc(s_c, 16)
                sp.dma_start(krow[:, :], A["krow"]).then_inc(s_c, 16)
                sp.dma_start(vrow[:, :, :], A["vrow"].rearrange("(o r) n -> o r n", o=1)).then_inc(s_c, 16)
                sp.dma_start(rawa[:, :], A["wqkv_a"]).then_inc(s_w, 16)
                sp.dma_start(rawb[:, :], A["wqkv_b"]).then_inc(s_w, 16)

                def group(g, r, u, more):
                    sp.wait_ge(s_vused, g + 1)
                    sp.wait_ge(s_hi, 2 * g + 2)
                    sp.wait_ge(s_lo, 2 * g + 2)
                    for dst, src in ((vhi, xhi), (vlo, xlo), (vmix, xmix)):
                        sp.dma_start(pair_of_images(dst[:, u, :]).bitcast(F32), src[:, bass.ds(2 * g, 2), :].bitcast(F32)).then_inc(s_vx[u], 16)
                    for j in range(6):
                        sp.wait_ge(s_qe, 6 * g + j + 3)
                        sp.dma_start(S["q"][128 * j:128 * j + 128, bass.ds(g * 512, 512)], qst[:, j % 2, :])\
                            .then_inc(s_qst[j % 2], 16)
                        sp.wait_ge(s_k0, 6 * g + j + 1)
                        sp.dma_start(S["k"][128 * j:128 * j + 128, bass.ds(g * 512, 512)], kst[:, j % 2, :])\
                            .then_inc(s_kst[j % 2], 16)
                    for t in range(4):
                        if t % 2 == 0:
                            sp.wait_ge(s_v0, 2 * g + t // 2 + 1)
                        else:
                            sp.wait_ge(s_ve, 8 * g + 2 * t + 4)
                        sp.dma_start(S["v"][bass.ds(g * 512 + 128 * t, 128), :], vst[:, t, :]).then_inc(s_vst[t], 16)

                group_pairs(sp, group)
                for q in range(3):
                    for k in range(2):
                        na, nd = store_feature_waits(NB * q + (NB if k else 1 + ROWS))
                        sp.wait_ge(s_fa, na)
                        sp.wait_ge(s_fd, nd)
                        if k:
                            sp.wait_ge(s_fz, 1)
                        sp.dma_start(S["f"][q, 128 * k:128 * k + 128, :], fbuf[k][:, :, :].rearrange("p b t -> p (b t)"))\
                            .then_inc(s_fst[k], 16)
                for q in s_fst:
                    sp.wait_ge(q, 48)

            @block.vector
            def _(dve):
                dve.sem_inc(s_ke, 2)
                for q in s_kst:
                    dve.sem_inc(q, 16)
                dve.wait_ge(s_std, 1)
                dve.reciprocal(stat[:, :, 1], std[:, :]).then_inc(s_rstd, 1)
                dve.wait_ge(s_c, 80)
                dve.tensor_tensor(rk[:, 96:128], rk[:, 96:128], rk0[:, :], ALU.add).then_inc(s_rk, 1)
                dve.tensor_tensor(krow[:, 0:1], krow[:, 0:1], krow[:, 1:2], ALU.add).then_inc(s_rk, 1)
                dve.tensor_tensor(vrow[:, 0, :], vrow[:, 0, :], vrow[:, 1, :], ALU.add).then_inc(s_rk, 1)
                dve.wait_ge(s_rstd, 1)
                normalize_group(dve, h, stat, xn, 0, 0, s_xn)
                for j in range(6):
                    q, half = divmod(j, 2)
                    dve.wait_ge(s_chi, j + 1)
                    dve.tensor_tensor(cq[2 * half + 1][:, q, :, :].rearrange("p t h -> p h t"),
                                      ps[:, j, :].rearrange("p (h t) -> p h t", h=4),
                                      cq[2 * half][:, q, :, :].rearrange("p t h -> p h t").bitcast(F32),
                                      ALU.subtract).then_inc(s_clo, 1)
                for k, (lo, hi, raw) in enumerate(((wlo, whi, rawa), (w2lo, w2hi, rawb))):
                    dve.wait_ge(s_whi, k + 1)
                    dve.tensor_tensor(lo[:, :], raw[:, :], hi[:, :].bitcast(F32), ALU.subtract).then_inc(s_wlo, 1)
                dve.wait_ge(s_rk, 3)

                def lo_parts(g):
                    cols = bass.ds(2 * g, 2)
                    dve.wait_ge(s_hi, 2 * g + 1)
                    dve.tensor_tensor(xlo[:, cols, :], pair_of_images(ps[:, 0, :]), xhi[:, cols, :].bitcast(F32),
                                      ALU.subtract).then_inc(s_lo, 1)
                    dve.wait_ge(s_hi, 2 * g + 2)
                    dve.tensor_tensor(xmix[64:128, cols, :], pair_of_images(ps[64:128, 1, :]),
                                      xmix[64:128, cols, :].bitcast(F32), ALU.subtract).then_inc(s_lo, 1)

                lo_parts(0)

                def group(g, r, u, more):
                    if more:
                        dve.wait_ge(s_tr, g + 1)
                        normalize_group(dve, h, stat, xn, g + 1, 1 - u, s_xn)
                    for j in range(6):
                        if j == 3 and more:
                            lo_parts(g + 1)
                        dve.wait_ge(s_k, 6 * g + j + 1)
                        dve.wait_ge(s_kst[j % 2], 16 * (3 * g + j // 2) + 16)
                        dve.tensor_copy(kst[:, j % 2, :], ps[:, 4 + j % 2, :]).then_inc(s_ke, 1)
                        dve.wait_ge(s_ke, 6 * g + j + 3)
                        k0 = pair_of_images(kst[:, j % 2, :])[:, :, 0]
                        dve.tensor_scalar(k0, k0, krow[:, 0:1], None, ALU.add).then_inc(s_k0, 1)
                    for t in (0, 2):
                        dve.wait_ge(s_ve, 8 * g + 2 * t + 4)
                        dve.tensor_tensor(vst[0:1, t, :], vst[0:1, t, :], vrow[:, 0, :], ALU.add).then_inc(s_v0, 1)

                group_pairs(dve, group)
                dve.wait_ge(s_wlo, 2)
                for q in s_vst:
                    dve.wait_ge(q, 16 + 16 * G)
                dve.memset(fbuf[1][:, :, 0], 0.0).then_inc(s_fz, 1)
                for n in range(1, 3 * NB, 2):
                    read_feature(dve, n, s_fd)

            @block.scalar
            def _(act):
                act.sem_inc(s_qe, 2)
                act.sem_inc(s_ve, 2)
                for q in s_qst + s_vst:
                    act.sem_inc(q, 16)
                act.activation(std[:, :], stat[:, :, 1], ACT.Sqrt, bias=epsc[:, 0:1]).then_inc(s_std, 1)
                for j in range(6):
                    q, half = divmod(j, 2)
                    act.wait_ge(s_cp, j + 1)
                    act.activation(cq[2 * half][:, q, :, :].rearrange("p t h -> p h t"),
                                   ps[:, j, :].rearrange("p (h t) -> p h t", h=4), ACT.Copy).then_inc(s_chi, 1)
                act.wait_ge(s_w, 32)
                act.activation(whi[:, :], rawa[:, :], ACT.Copy).then_inc(s_whi, 1)
                act.activation(w2hi[:, :], rawb[:, :], ACT.Copy).then_inc(s_whi, 1)

                def hi_parts(g):
                    cols = bass.ds(2 * g, 2)
                    act.wait_ge(s_tr, g + 1)
                    act.activation(xhi[:, cols, :], pair_of_images(ps[:, 0, :]), ACT.Copy).then_inc(s_hi, 1)
                    act.activation(xmix[:, cols, :], pair_of_images(ps[:, 1, :]), ACT.Copy).then_inc(s_hi, 1)

                hi_parts(0)

                def group(g, r, u, more):
                    for j in range(6):
                        if j == 3 and more:
                            hi_parts(g + 1)
                        act.wait_ge(s_q, 6 * g + j + 1)
                        act.wait_ge(s_qst[j % 2], 16 * (3 * g + j // 2) + 16)
                        act.activation(qst[:, j % 2, :], ps[:, 2 + j % 2, :], ACT.Copy).then_inc(s_qe, 1)
                    for t in range(4):
                        act.wait_ge(s_vst[t], 16 * g + 16)
                        for half in range(2):
                            act.wait_ge(s_v, 8 * g + 2 * t + half + 1)
                            act.activation(vst[:, t, 384 * half:384 * half + 384], ps[:, 6 + half, 0:384],
                                           ACT.Copy).then_inc(s_ve, 1)

                group_pairs(act, group)
                act.wait_ge(s_wlo, 2)
                for q in s_vst:
                    act.wait_ge(q, 16 + 16 * G)
                for n in range(0, 3 * NB, 2):
                    read_feature(act, n, s_fa)

            @block.tensor
            def _(pe):
                pe.wait_ge(s_c, 80)
                pe.wait_ge(s_rk, 1)
                for j in range(6):
                    q, half = divmod(j, 2)
                    for i in range(4):
                        last = pe.matmul(ps[:, j, 128 * i:128 * i + 128], wqt[:, 4 * q + i, 128 * half:128 * half + 128],
                                         rk[:, :], start=True, stop=True)
                    last.then_inc(s_cp, 1)
                pe.wait_ge(s_clo, 6)
                pe.wait_ge(s_xn, 1)
                transpose_group(pe, ps, xn, 0, ident, s_tr)
                pe.wait_ge(s_wlo, 2)

                def group(g, r, u, more):
                    cols = bass.ds(2 * g, 2)
                    x = (xhi[:, cols, :], xlo[:, cols, :], xmix[:, cols, :])
                    pe.wait_ge(s_hi, 2 * g + 2)
                    pe.wait_ge(s_lo, 2 * g + 2)
                    for j in range(6):
                        if j == 2 and more:
                            pe.wait_ge(s_xn, g + 2)
                            transpose_group(pe, ps, xn, 1 - u, ident, s_tr)
                        for read, done, bank, off in ((s_qe, s_q, 2, 0), (s_ke, s_k, 4, WQ)):
                            pe.wait_ge(read, 6 * g + j + 1)
                            c = slice(off + 128 * j, off + 128 * j + 128)
                            five_passes(pe, ps[:, bank + j % 2, :], (whi[:, c], wlo[:, c], w2hi[:, c], w2lo[:, c]),
                                        x).then_inc(done, 1)
                    pe.wait_ge(s_vx[u], 48 * (r + 1))
                    for t in range(4):
                        tok = slice(128 * t, 128 * t + 128)
                        for half in range(2):
                            pe.wait_ge(s_ve, 8 * g + 2 * t + half + 1)
                            c = slice(2 * WQ + 384 * half, 2 * WQ + 384 * half + 384)
                            last = five_passes(pe, ps[:, 6 + half, 0:384], (whi[:, c], wlo[:, c], w2hi[:, c], w2lo[:, c]),
                                               (vhi[:, u, tok], vlo[:, u, tok], vmix[:, u, tok]), x_stationary=True)
                            last.then_inc(s_v, 1)
                    pe.sem_inc(s_vused, 1)

                pe.sem_inc(s_vused, 2)
                group_pairs(pe, group)
                for s, n in ((s_qe, 6 * G + 2), (s_ke, 6 * G + 2), (s_ve, 8 * G + 2), (s_lo, 2 * G)):
                    pe.wait_ge(s, n)
                for n in range(3 * NB):
                    q, (first, count, step, window, _) = n // NB, blocks[n % NB]
                    if n >= 8:
                        pe.wait_ge(s_fd if n % 2 else s_fa, (n - 8) // 2 + 1)
                    tok = slice(first, first + (count - 1) * step + 1, step)
                    rows = [c[:, q, window:window + 32, :].rearrange("p t h -> p (t h)") for c in cq]
                    five_passes(pe, ps[:, n % 8, 0:count * B], rows,
                                [x[:, :, tok].rearrange("p b t -> p t b") for x in (xhi, xlo, xmix)]).then_inc(s_f, 1)


def attend(nc, A, S, h, ident):
    SCALE = HD ** -0.5
    N = B * H
    with ExitStack() as ctx:
        m = Mem(nc, ctx, "attend")
        qf = m.sb("qf", [128, H, NT])
        kf = m.sb("kf", [128, H, NT])
        vg = m.sb("vg", [128, 2, H, 128])
        prob = m.sb("prob", [128, 3, 2, NT])
        probt = m.sb("probt", [128, 2, 2, NT])
        otp = m.sb("otp", [128, 2, NT])
        wst = m.sb("w_stage", [128, 3, 4, NT])
        wp = m.sb("wp", [128, 6, D])
        mx, nm = m.sb("mx", [128, 2, 2]), m.sb("neg_max", [128, 2, 2])
        den, rden = m.sb("den", [128, 2, 2]), m.sb("rden", [128, 2, 2])
        ps_s = m.psum("ps_scores", [128, 2, 512])
        ps_t = m.psum("ps_probt", [128, 2, 512])
        ps_o = m.psum("ps_out", [128, 2, 512])
        ps_y = m.psum("ps_y", [128, 2, 512])

        s_c, s_cp = m.sem("att_consts_loaded"), m.sem("att_weights_loaded")
        s_ld = [m.sem(f"quad_loaded{q}") for q in range(3)]
        s_s = m.sem("scores")
        s_mx, s_nm = m.sem("max_done"), m.sem("neg_max_done")
        s_e = m.sem("exp_done")
        s_r = m.sem("rden_done")
        s_p0, s_p1 = m.sem("prob_tile0_done"), m.sem("prob_tile1_done")
        s_t = m.sem("prob_transposed")
        s_pt = m.sem("probt_copied")
        s_o = m.sem("head_out")
        s_oe = m.sem("head_out_read")
        s_pr = m.sem("pair_projected")
        s_y = m.sem("y_added")
        s_wst = [m.sem(f"w_stored{q}") for q in range(3)]

        def lagged(b, hd, lag):
            n = 12 * b + hd - lag
            if hd - lag < 0:
                return b - 1, hd - lag + H, n
            if hd - lag >= H:
                return b + 1, hd - lag - H, n
            return b, hd - lag, n

        def steps(eng, step):
            for hd in range(H):
                step(0, hd, lambda lag, hd=hd: hd - lag >= 0)
            with eng.Fori(1, B) as b:
                for hd in range(H):
                    step(b, hd, lambda lag: True)
            for hd in range(H, H + 5):
                step(B - 1, hd, lambda lag, hd=hd: hd - lag < H)

        with nc.Block() as block:

            @block.sync
            def _(sp):
                sp.dma_start(kf[64:128, :, :], A["ind"].rearrange("f (o t) -> f o t", o=1).to_broadcast([64, H, NT])).then_inc(s_c, 16)
                for j in range(2):
                    sp.dma_start(vg[:, j, :, 64:128], A["indt"][:, j:j + 1, :].to_broadcast([128, H, 64])).then_inc(s_c, 16)

                def image(b):
                    cols = bass.ds(b * NT, NT)
                    for q in range(3):
                        sp.wait_ge(s_o, 12 * b + 4 * q + 4)
                        sp.dma_start(qf[0:64, 4 * q:4 * q + 4, :],
                                     S["q"][256 * q:256 * q + 256, cols].rearrange("(h d) t -> d h t", h=4)).then_inc(s_ld[q], 16)
                        sp.dma_start(kf[0:64, 4 * q:4 * q + 4, :],
                                     S["k"][256 * q:256 * q + 256, cols].rearrange("(h d) t -> d h t", h=4)).then_inc(s_ld[q], 16)
                        sp.dma_start(qf[64:128, 4 * q:4 * q + 4, :],
                                     S["f"][q, :, cols].rearrange("(r h) t -> r h t", h=4)).then_inc(s_ld[q], 16)
                        for j in range(2):
                            sp.dma_start(vg[:, j, 4 * q:4 * q + 4, 0:64],
                                         S["v"][bass.ds(b * NT + 128 * j, 128), 256 * q:256 * q + 256]
                                         .rearrange("p (h d) -> p h d", h=4)).then_inc(s_ld[q], 16)

                image(0)
                sp.dma_start(wp[:, :, :], A["wproj"].rearrange("(m p) n -> p m n", p=128)).then_inc(s_cp, 16)
                with sp.Fori(1, B) as b:
                    image(b)

            @block.vector
            def _(dve):
                dve.sem_inc(s_pt, 2)
                dve.sem_inc(s_y, 2)

                def step(b, hd, live):
                    if live(1) and hd - 1 < H:
                        _, g, n = lagged(b, hd, 1)
                        dve.wait_ge(s_e, n + 3)
                        dve.reciprocal(rden[:, g % 2, :], den[:, g % 2, :]).then_inc(s_r, 1)
                        dve.wait_ge(s_r, n + 1)
                        dve.tensor_scalar(prob[:, g % 3, 0, :], prob[:, g % 3, 0, :], rden[:, g % 2, 0:1], None,
                                          ALU.mult).then_inc(s_p0, 1)
                    if hd < H:
                        _, _, n = lagged(b, hd, 0)
                        dve.wait_ge(s_s, n + 1)
                        dve.tensor_reduce(mx[:, hd % 2, :], ps_s[:, hd % 2, :].rearrange("p (i j) -> p i j", i=2),
                                          AX.X, ALU.max).then_inc(s_mx, 1)
                        dve.wait_ge(s_mx, n + 1)
                        dve.tensor_scalar(nm[:, hd % 2, :], mx[:, hd % 2, :], -SCALE, None, ALU.mult).then_inc(s_nm, 1)
                    if live(2) and hd - 2 < H:
                        _, g, n = lagged(b, hd, 2)
                        dve.wait_ge(s_t, n + 4)
                        dve.tensor_copy(probt[:, g % 2, :, :].rearrange("p j i -> p (j i)"), ps_t[:, g % 2, :]).then_inc(s_pt, 1)
                    if hd == 5 and live(6):
                        add_y(b - 1)

                def add_y(b):
                    for it in range(2):
                        dve.wait_ge(s_pr, 6 * b + 8)
                        tile = h[:, bass.ds(2 * b + it, 1), :]
                        dve.tensor_tensor(tile, ps_y[:, it, 0:D].rearrange("p (o n) -> p o n", o=1), tile, ALU.add).then_inc(s_y, 1)

                steps(dve, step)
                add_y(B - 1)

            @block.scalar
            def _(act):
                act.sem_inc(s_e, 2)
                act.sem_inc(s_oe, 2)
                for q in s_wst:
                    act.sem_inc(q, 16)

                def step(b, hd, live):
                    if live(1) and hd - 1 < H:
                        _, g, n = lagged(b, hd, 1)
                        act.wait_ge(s_r, n + 1)
                        act.activation(prob[:, g % 3, 1, :], prob[:, g % 3, 1, :], ACT.Copy,
                                       scale=rden[:, g % 2, 1:2]).then_inc(s_p1, 1)
                    if hd < H:
                        _, _, n = lagged(b, hd, 0)
                        act.wait_ge(s_nm, n + 1)
                        act.wait_ge(s_t, n + 1)
                        for it in range(2):
                            ins = act.activation(prob[:, hd % 3, it, :], ps_s[:, hd % 2, NT * it:NT * it + NT], ACT.Exp,
                                                 bias=nm[:, hd % 2, it:it + 1], scale=SCALE,
                                                 accum_out=den[:, hd % 2, it:it + 1])
                        ins.then_inc(s_e, 1)
                    if live(3) and hd - 3 < H:
                        gb, g, n = lagged(b, hd, 3)
                        act.wait_ge(s_o, n + 1 + H)
                        act.wait_ge(s_pr, 6 * gb + g // 2 + 1)
                        half = 64 * (g % 2)
                        act.activation(otp[half:half + 64, (g // 2) % 2, :], ps_o[0:64, g % 2, 0:NT], ACT.Copy)
                        q = g // 4
                        if g % 4 == 0:
                            act.wait_ge(s_wst[q], 16 * gb + 16)
                        act.activation(wst[64:128, q, g % 4, :], ps_o[64:128, g % 2, 0:NT], ACT.Copy).then_inc(s_oe, 1)
                        if g % 4 == 3:
                            act.wait_ge(s_oe, n + 3)
                            act.dma_start(S["w"][q, :, bass.ds(gb * NT, NT)].rearrange("(r h) t -> r h t", h=4),
                                          wst[64:128, q, :, :]).then_inc(s_wst[q], 16)

                steps(act, step)
                for q in s_wst:
                    act.wait_ge(q, 16 * B + 16)

            @block.tensor
            def _(pe):
                pe.sem_inc(s_t, 3)
                pe.sem_inc(s_o, H)
                pe.sem_inc(s_pr, 2)
                pe.wait_ge(s_c, 48)

                def step(b, hd, live):
                    if hd < H:
                        _, _, n = lagged(b, hd, 0)
                        if hd % 4 == 0:
                            pe.wait_ge(s_ld[hd // 4], 80 * b + 80)
                        pe.wait_ge(s_e, n + 1)
                        for it in range(2):
                            last = pe.matmul(ps_s[:, hd % 2, NT * it:NT * it + NT], qf[:, hd, 128 * it:128 * it + 128],
                                             kf[:, hd, :], start=True, stop=True)
                        last.then_inc(s_s, 1)
                    if live(2) and hd - 2 < H:
                        _, g, n = lagged(b, hd, 2)
                        pe.wait_ge(s_p0, n + 1)
                        pe.wait_ge(s_p1, n + 1)
                        pe.wait_ge(s_pt, n + 1)
                        for jt in range(2):
                            for it in range(2):
                                last = pe.transpose(ps_t[:, g % 2, NT * jt + 128 * it:NT * jt + 128 * it + 128],
                                                    prob[:, g % 3, it, 128 * jt:128 * jt + 128], ident[:, :])
                        last.then_inc(s_t, 1)
                    if live(3) and hd - 3 < H:
                        _, g, n = lagged(b, hd, 3)
                        pe.wait_ge(s_pt, n + 3)
                        pe.wait_ge(s_oe, n + 1)
                        for jt in range(2):
                            last = pe.matmul(ps_o[:, g % 2, 0:NT], vg[:, jt, g, :], probt[:, g % 2, jt, :],
                                             start=(jt == 0), stop=(jt == 1))
                        last.then_inc(s_o, 1)
                    if live(4) and hd - 4 < H and hd % 2 == 1:
                        gb, g, n = lagged(b, hd, 4)
                        p = g // 2
                        if p == 0:
                            pe.wait_ge(s_cp, 16)
                            pe.wait_ge(s_y, 2 * gb + 2)
                        pe.wait_ge(s_oe, n + 3)
                        for it in range(2):
                            last = pe.matmul(ps_y[:, it, 0:D], otp[:, p % 2, 128 * it:128 * it + 128], wp[:, p, :],
                                             start=(p == 0), stop=(p == 5))
                        last.then_inc(s_pr, 1)

                steps(pe, step)


def relative(nc, A, S, h, ident, stat):
    with ExitStack() as ctx:
        m = Mem(nc, ctx, "relative")
        K = 4 * 32
        w = m.sb("block_sums", [K, 2, 3, B, NT])
        yt = m.sb("yt", [128, B, NT])
        yt2 = m.sb("yt2", [64, B, NT])
        rv, rv0 = m.sb("rv", [HD, 128]), m.sb("rv0", [HD, 32])
        wh = m.sb("wproj_h", [HD, H, D])
        rw = m.sb("rw_stage", [128, 6, 2 * D])
        win = m.sb("rw_window", [K, 4, 3, D])
        bias, bias2 = m.sb("bias", [128, 1]), m.sb("bias2", [64, 1])
        raw = m.sb("rel_bn", [128, 2, 6])
        ps = m.psum("ps_rel", [128, 8, 512])

        s_c = m.sem("rel_consts_loaded")
        s_w = [m.sem(f"block_sums_loaded{k}") for k in range(2)]
        s_rv = m.sem("rv_ready")
        s_rw, s_rwe, s_rws = m.sem("rw_product"), m.sem("rw_read"), m.sem("rw_stored")
        s_win = [m.sem(f"window_loaded{i}") for i in range(4)]
        s_y, s_ya, s_yc = m.sem("y_product"), m.sem("y_rows_read"), m.sem("y_columns_added")
        s_t, s_h = m.sem("y_transposed"), m.sem("h_updated")
        s_bn, s_agg = m.sem("bn2_stats_done"), m.sem("bn2_aggregated")

        blocks = [(0, 1, 1, 96, 0)]
        blocks += [(1 + SIDE * a, SIDE, 1, 16 - a, 0) for a in range(ROWS)]
        blocks += [(1 + c, ROWS, SIDE, 48 + 14 - c, 1) for c in range(SIDE)]
        NA = 1 + ROWS

        def tokens(ap, n):
            first, count, step, _, _ = blocks[n]
            return ap[:, :, first:first + (count - 1) * step + 1:step]

        def product(n, part):
            lo, rows = ((0, 128), (1, 64))[part]
            count = blocks[n][1]
            return ps[0:rows, 2 * (n % 4) + lo, 0:B * count].rearrange("p (b t) -> p b t", b=B)

        with nc.Block() as block:

            @block.sync
            def _(sp):
                sp.dma_start(rv[:, :], A["rv"]).then_inc(s_c, 16)
                sp.dma_start(rv0[:, :], A["rv0"]).then_inc(s_c, 16)
                sp.dma_start(wh[:, :, :], A["wproj_h"]).then_inc(s_c, 16)
                sp.dma_start(bias[:, :], A["bproj"][0:128].rearrange("(p o) -> p o", o=1)).then_inc(s_c, 16)
                sp.dma_start(bias2[:, :], A["bproj"][128:192].rearrange("(p o) -> p o", o=1)).then_inc(s_c, 16)
                for k in range(2):
                    for q in range(3):
                        if k:
                            sp.wait_ge(s_y, 2 + 4 * q)
                        sp.dma_start(w[:, k, q, :, :].rearrange("p b t -> p (b t)"),
                                     S["w"][q, 128 * k:128 * k + K, :]).then_inc(s_w[k], 16)

            @block.scalar
            def _(act):
                for j in range(6):
                    act.wait_ge(s_rw, j + 1)
                    act.activation(rw[:, j, :], ps[:, j, 0:2 * D], ACT.Copy).then_inc(s_rwe, 1)
                act.wait_ge(s_rwe, 6)
                act.dma_start(S["rw"].rearrange("t h n -> t (h n)"), rw[:, :, :].rearrange("p j n -> p (j n)")).then_inc(s_rws, 16)
                act.wait_ge(s_rws, 16)
                rows = S["rw"].rearrange("t (h q) n -> (t h) q n", q=3)

                def load_window(n):
                    f = 4 * blocks[n][3]
                    act.dma_start(win[:, n % 4, :, :], rows[f:f + K, :, :]).then_inc(s_win[n % 4], 16)

                for n in range(4):
                    load_window(n)
                act.wait_ge(s_c, 80)
                for n in range(len(blocks)):
                    act.wait_ge(s_y, n + 1)
                    if n + 4 < len(blocks):
                        load_window(n + 4)
                    if n < NA:
                        act.activation(tokens(yt, n), product(n, 0), ACT.Identity, bias=bias[:, 0:1])
                        act.activation(tokens(yt2, n), product(n, 1), ACT.Identity, bias=bias2[:, 0:1]).then_inc(s_ya, 1)

            @block.vector
            def _(dve):
                dve.wait_ge(s_c, 80)
                dve.tensor_tensor(rv[:, 96:128], rv[:, 96:128], rv0[:, :], ALU.add).then_inc(s_rv, 1)
                dve.wait_ge(s_ya, NA)
                for n in range(NA, len(blocks)):
                    dve.wait_ge(s_y, n + 1)
                    dve.tensor_tensor(tokens(yt, n), product(n, 0), tokens(yt, n), ALU.add)
                    dve.tensor_tensor(tokens(yt2, n), product(n, 1), tokens(yt2, n), ALU.add).then_inc(s_yc, 1)
                for t in range(NTILE):
                    dve.wait_ge(s_t, t + 1)
                    dve.tensor_tensor(h[:, t, :], ps[:, t % 8, 0:D], h[:, t, :], ALU.add).then_inc(s_h, 1)
                    norm_stats(dve, h, stat, raw, t, NTILE, s_h, s_bn, s_agg)

            @block.tensor
            def _(pe):
                pe.wait_ge(s_rv, 1)
                for j in range(6):
                    pe.matmul(ps[:, j, 0:2 * D], rv[:, :], wh[:, 2 * j:2 * j + 2, :].rearrange("p h n -> p (h n)"),
                              start=True, stop=True).then_inc(s_rw, 1)
                pe.wait_ge(s_rwe, 6)
                pe.wait_ge(s_w[0], 48)
                for n in range(len(blocks)):
                    if n == NA:
                        pe.wait_ge(s_w[1], 48)
                    if n >= 4:
                        if n - 4 < NA:
                            pe.wait_ge(s_ya, n - 3)
                        else:
                            pe.wait_ge(s_yc, n - 3 - NA)
                    pe.wait_ge(s_win[n % 4], 16 * (n // 4 + 1))
                    for part, c in ((0, slice(0, 128)), (1, slice(128, D))):
                        for q in range(3):
                            last = pe.matmul(product(n, part), win[:, n % 4, q, c], tokens(w[:, blocks[n][4], q], n),
                                             start=(q == 0), stop=(q == 2))
                    last.then_inc(s_y, 1)
                pe.wait_ge(s_yc, SIDE)
                for t in range(NTILE):
                    if t >= 8:
                        pe.wait_ge(s_h, t - 7)
                    b, i = t // 2, t % 2
                    pe.transpose(ps[:, t % 8, 0:128], yt[:, b, 128 * i:128 * i + 128], ident[:, :])
                    pe.transpose(ps[:, t % 8, 128:D], yt2[:, b, 128 * i:128 * i + 128], ident[0:64, 0:64]).then_inc(s_t, 1)


def pipeline(eng, n, body):
    for u in range(2):
        body(u, 0, u, u > 0, True)
    with eng.Fori(1, n // 2 - 1) as i:
        for u in range(2):
            body(2 * i + u, i, u, True, True)
    for u in range(2):
        body(n - 2 + u, n // 2 - 1, u, True, u == 0)


ROW = 256 + E


def score(nc, A, S, h, ident, stat, epsc, x, scores):
    G = T // 512
    xhi, xlo, xmix = x
    with ExitStack() as ctx:
        m = Mem(nc, ctx, "score")
        rawa, rawb = m.sb("raw_a", [128, E]), m.sb("raw_b", [128, E])
        whi, wlo = m.sb("w_hi", [128, E], F32R), m.sb("w_lo", [128, E], F32R)
        w2hi, w2lo = m.sb("w2_hi", [128, E], F32R), m.sb("w2_lo", [128, E], F32R)
        std = m.sb("std", [128, NTILE])
        xn = m.sb("xn", [128, 2, 4, 256])
        rsc = m.sb("token_scores", [128, 2, 4, E])
        sct = m.sb("scores_t", [E, 2, 512])
        ps = m.psum("ps", [128, 8, 512])

        s_w = m.sem("weights_loaded")
        s_std, s_rstd = m.sem("std_ready"), m.sem("rstd_ready")
        s_whi, s_wlo = m.sem("w_hi_made"), m.sem("w_lo_made")
        s_xn, s_tr = m.sem("normed"), m.sem("x_transposed")
        s_hi, s_lo = m.sem("x_hi_made"), m.sem("x_lo_made")
        s_gt, s_sc = m.sem("gate_product"), m.sem("scores_ready")
        s_st, s_row = m.sem("scores_transposed"), m.sem("row_ready")
        s_go = m.sem("pe_wait_passed")
        s_xd = [m.sem(f"row_stored{i}") for i in range(2)]
        s_rd = [m.sem(f"row_scores_stored{i}") for i in range(2)]
        s_sd = [m.sem(f"scores_stored{i}") for i in range(2)]

        with nc.Block() as block:

            @block.sync
            def _(sp):
                sp.dma_start(rawa[:, :], A["gate"][0:128, :]).then_inc(s_w, 16)
                for half in (0, 64):
                    sp.dma_start(rawb[half:half + 64, :], A["gate"][128:192, :]).then_inc(s_w, 16)

                def store_scores(g, u):
                    sp.wait_ge(s_sc, g + 1)
                    sp.dma_start(S["scores"][bass.ds(16 * g, 16), :], sct[:, u, :]).then_inc(s_sd[u], 16)
                    sp.wait_ge(s_row, g + 1)
                    sp.dma_start(rows(g)[:, :, 256:ROW], rsc[:, u, :, :]).then_inc(s_rd[u], 16)

                def rows(g):
                    return S["rows"][bass.ds(g * 512, 512), :].rearrange("(t p) c -> p t c", p=128)

                def body(g, r, u, before, after):
                    sp.wait_ge(s_xn, g + 1)
                    sp.dma_start(rows(g)[:, :, 0:256], xn[:, u, :, :]).then_inc(s_xd[u], 16)
                    if before:
                        store_scores(g - 1, 1 - u)
                    if not after:
                        store_scores(g, u)

                pipeline(sp, G, body)
                for u in range(2):
                    sp.wait_ge(s_sd[u], 16 + 16 * G // 2)
                    sp.wait_ge(s_xd[u], 16 + 16 * G // 2)
                    sp.wait_ge(s_rd[u], 16 + 16 * G // 2)
                sp.dma_start(scores[:, :], S["scores"]).then_inc(s_w, 16)
                sp.wait_ge(s_w, 16 * 4)

            @block.vector
            def _(dve):
                dve.wait_ge(s_std, 1)
                dve.reciprocal(stat[:, :, 1], std[:, :]).then_inc(s_rstd, 1)
                dve.wait_ge(s_rstd, 1)
                dve.wait_ge(s_xd[0], 16)
                normalize_group(dve, h, stat, xn, 0, 0, s_xn)
                for k, (lo, hi, raw) in enumerate(((wlo, whi, rawa), (w2lo, w2hi, rawb))):
                    dve.wait_ge(s_whi, k + 1)
                    dve.tensor_tensor(lo[:, :], raw[:, :], hi[:, :].bitcast(F32), ALU.subtract).then_inc(s_wlo, 1)

                def body(g, r, u, before, after):
                    if after:
                        dve.wait_ge(s_xd[1 - u], 16 * (r + u) + 16)
                        if before:
                            dve.wait_ge(s_tr, g)
                        normalize_group(dve, h, stat, xn, g + 1, 1 - u, s_xn)
                    cols = bass.ds(g * 512, 512)
                    dve.wait_ge(s_hi, 2 * g + 1)
                    dve.tensor_tensor(xlo[:, cols], ps[:, 2 * u, :], xhi[:, cols].bitcast(F32), ALU.subtract).then_inc(s_lo, 1)
                    dve.wait_ge(s_hi, 2 * g + 2)
                    dve.tensor_tensor(xmix[64:128, cols], ps[64:128, 2 * u + 1, :], xmix[64:128, cols].bitcast(F32),
                                      ALU.subtract).then_inc(s_lo, 1)

                pipeline(dve, G, body)

            @block.scalar
            def _(act):
                for q in s_xd + s_sd + s_rd:
                    act.sem_inc(q, 16)
                act.activation(std[:, :], stat[:, :, 1], ACT.Sqrt, bias=epsc[:, 0:1]).then_inc(s_std, 1)
                act.wait_ge(s_w, 16 * 3)
                for hi, raw in ((whi, rawa), (w2hi, rawb)):
                    act.activation(hi[:, :], raw[:, :], ACT.Copy).then_inc(s_whi, 1)

                def finish(g, r, u):
                    act.wait_ge(s_gt, g + 1)
                    act.wait_ge(s_sd[u], 16 * r + 16)
                    act.activation(sct[:, u, :], ps[0:E, 4 + u, :], ACT.Sigmoid).then_inc(s_sc, 1)
                    act.wait_ge(s_st, g + 1)
                    act.wait_ge(s_rd[u], 16 * r + 16)
                    act.activation(rsc[:, u, :, :], ps[:, 6 + u, 0:4 * E].rearrange("p (t e) -> p t e", t=4),
                                   ACT.Copy).then_inc(s_row, 1)

                def body(g, r, u, before, after):
                    cols = bass.ds(g * 512, 512)
                    act.wait_ge(s_tr, g + 1)
                    act.activation(xhi[:, cols], ps[:, 2 * u, :], ACT.Copy).then_inc(s_hi, 1)
                    act.activation(xmix[:, cols], ps[:, 2 * u + 1, :], ACT.Copy).then_inc(s_hi, 1)
                    if before:
                        finish(g - 1, r + u - 1, 1 - u)
                    if not after:
                        finish(g, r, u)

                pipeline(act, G, body)

            @block.tensor
            def _(pe):
                pe.wait_ge(s_wlo, 2)

                def finish(g, r, u):
                    pe.wait_ge(s_lo, 2 * g + 2)
                    cols = bass.ds(g * 512, 512)
                    five_passes(pe, ps[0:E, 4 + u, :], (whi[:, :], wlo[:, :], w2hi[:, :], w2lo[:, :]),
                                (xhi[:, cols], xlo[:, cols], xmix[:, cols])).then_inc(s_gt, 1)

                def turn(g, u):
                    pe.wait_ge(s_sc, g + 1)
                    pe.sem_inc(s_go, 1)
                    for t in range(4):
                        last = pe.transpose(ps[:, 6 + u, E * t:E * t + E], sct[:, u, 128 * t:128 * t + 128], ident[0:E, 0:E])
                    last.then_inc(s_st, 1)

                def body(g, r, u, before, after):
                    if before and not (isinstance(g, int) and g < 2):
                        pe.wait_ge(s_lo, 2 * g - 2)
                        pe.wait_ge(s_row, g - 1)
                    pe.wait_ge(s_xn, g + 1)
                    transpose_group(pe, ps, xn, u, ident, s_tr, 2 * u)
                    if before:
                        finish(g - 1, r, 1 - u)
                        turn(g - 1, 1 - u)
                    if not after:
                        finish(g, r, u)
                        turn(g, u)

                pipeline(pe, G, body)


def share(nc, A, S, out, h, x, scores, limit):
    G = T // 512
    W = 2 * FS
    NF = FS // 128
    PER_GROUP = 4
    xhi, xlo, xmix = x
    with ExitStack() as ctx:
        m = Mem(nc, ctx, "share")
        rawa, rawb, rawd = m.sb("raw_a", [128, W]), m.sb("raw_b", [128, W]), m.sb("raw_d", [128, NF, D])
        whi, wlo = m.sb("w_hi", [128, W], F32R), m.sb("w_lo", [128, W], F32R)
        w2hi, w2lo = m.sb("w2_hi", [128, W], F32R), m.sb("w2_lo", [128, W], F32R)
        wdhi, wdlo = m.sb("wd_hi", [128, NF, D], F32R), m.sb("wd_lo", [128, NF, D], F32R)
        sg = m.sb("silu", [128, 2, 512])
        a = m.sb("act", [128, 2, 512])
        ahi, alo = m.sb("act_hi", [128, 2, NF, 512], F32R), m.sb("act_lo", [128, 2, NF, 512], F32R)
        ost = m.sb("out_stage", [128, 2, 4, D])
        same = m.sb("same_expert", [128, 128])
        bits = m.sb("bits", [128, PER_GROUP * G], I32)
        cand, cnt, keep = m.sb("candidate", [128, 1], I32), m.sb("partial_count", [128, 1]), m.sb("kept_candidate", [128, 1])
        mask = m.sb("mask", [128, 512])
        ps = m.psum("ps", [128, 8, 512])

        s_w, s_c = m.sem("weights_loaded"), m.sem("consts_loaded")
        s_whi, s_wlo = m.sem("w_hi_made"), m.sem("w_lo_made")
        s_gu, s_sg = m.sem("gate_up_product"), m.sem("silu_done")
        s_a, s_ahi, s_alo = m.sem("act_made"), m.sem("act_hi_made"), m.sem("act_lo_made")
        s_d, s_o = m.sem("down_product"), m.sem("out_made")
        s_os = [m.sem(f"out_stored{i}") for i in range(2)]
        s_v, s_n, s_tot = m.sem("bit_step"), m.sem("counted"), m.sem("total_ready")

        with nc.Block() as block:

            @block.sync
            def _(sp):
                sp.dma_start(rawa[:, :], A["wsgu_a"]).then_inc(s_w, 16)
                sp.dma_start(rawb[:, :], A["wsgu_b"]).then_inc(s_w, 16)
                sp.dma_start(rawd[:, :, :], A["wsd"]).then_inc(s_w, 16)
                sp.dma_start(same[:, :], A["same_expert"]).then_inc(s_c, 16)
                sp.dma_start(bits[:, :], A["bits"]).then_inc(s_c, 16)

                def store_out(g, u):
                    sp.wait_ge(s_o, 4 * g + 6)
                    sp.dma_start(out[bass.ds(g * 512, 512), :].rearrange("(t p) c -> p t c", p=128),
                                 ost[:, u, :, :]).then_inc(s_os[u], 16)

                pipeline(sp, G, lambda g, r, u, before, after: store_out(g, u))
                for u in range(2):
                    sp.wait_ge(s_os[u], 16 + 16 * G // 2)

            @block.vector
            def _(dve):
                dve.sem_inc(s_o, 2)
                dve.memset(limit[:, :], 0).then_inc(s_v, 1)
                for k, (lo, hi, raw) in enumerate(((wlo, whi, rawa), (w2lo, w2hi, rawb), (wdlo, wdhi, rawd))):
                    dve.wait_ge(s_whi, k + 1)
                    ix = (slice(None),) * len(raw.shape)
                    dve.tensor_tensor(lo[ix], raw[ix], hi[ix].bitcast(F32), ALU.subtract).then_inc(s_wlo, 1)
                dve.wait_ge(s_c, 32)

                def guess(i):
                    dve.wait_ge(s_v, 3 * i + 1)
                    dve.tensor_tensor(cand[:, :], bits[:, bass.ds(i, 1)], limit[:, :], ALU.bitwise_or).then_inc(s_v, 1)
                    dve.wait_ge(s_v, 3 * i + 2)
                    dve.tensor_scalar(mask[:, :], scores[:, :], cand[:, 0:1].bitcast(F32), 0.0, ALU.is_ge, ALU.add,
                                      accum_out=cnt[:, 0:1]).then_inc(s_n, 1)

                def settle(i):
                    dve.wait_ge(s_tot, i + 1)
                    dve.tensor_scalar(keep[:, :], ps[:, 0, 0:1], float(CAP), cand[:, 0:1].bitcast(F32), ALU.is_ge,
                                      ALU.mult).then_inc(s_v, 1)
                    dve.wait_ge(s_v, 3 * i + 3)
                    dve.tensor_tensor(limit[:, :].bitcast(F32), limit[:, :].bitcast(F32), keep[:, :], ALU.max).then_inc(s_v, 1)

                def add_shared(g, u, tiles):
                    for t in tiles:
                        if t == 0:
                            dve.wait_ge(s_os[u], 8 * (g - u) + 16)
                        dve.wait_ge(s_d, 4 * g + t + 1)
                        dve.tensor_tensor(ost[:, u, t:t + 1, :], ps[:, 6 + t % 2, 0:D].rearrange("p (o n) -> p o n", o=1),
                                          h[:, bass.ds(4 * g + t, 1), :], ALU.add).then_inc(s_o, 1)

                def body(g, r, u, before, after):
                    bit = PER_GROUP * g
                    for j in range(NF):
                        k = (u + j) % 2
                        dve.wait_ge(s_sg, NF * g + j + 1)
                        dve.tensor_tensor(a[:, k, :], sg[:, k, :], ps[:, 4 + k, :], ALU.mult).then_inc(s_a, 1)
                        if j > 0 or before:
                            settle(bit + j if j else bit - 1)
                        guess(bit + (j + 1 if j else 0))
                        dve.wait_ge(s_ahi, NF * g + j + 1)
                        dve.tensor_tensor(alo[:, u, j, :], a[:, k, :], ahi[:, u, j, :].bitcast(F32), ALU.subtract)\
                            .then_inc(s_alo, 1)
                        if j == 0:
                            if before:
                                add_shared(g - 1, 1 - u, (0, 1))
                            settle(bit)
                            guess(bit + 1)
                            if before:
                                add_shared(g - 1, 1 - u, (2, 3))
                    if not after:
                        settle(bit + 3)
                        add_shared(g, u, range(4))

                pipeline(dve, G, body)

            @block.scalar
            def _(act):
                for q in s_os:
                    act.sem_inc(q, 16)
                act.wait_ge(s_w, 16 * 3)
                for hi, raw in ((whi, rawa), (w2hi, rawb), (wdhi, rawd)):
                    ix = (slice(None),) * len(raw.shape)
                    act.activation(hi[ix], raw[ix], ACT.Copy).then_inc(s_whi, 1)

                def body(g, r, u, before, after):
                    for j in range(NF):
                        k = (u + j) % 2
                        act.wait_ge(s_gu, NF * g + j + 1)
                        act.activation(sg[:, k, :], ps[:, 2 + k, :], ACT.Silu).then_inc(s_sg, 1)
                        act.wait_ge(s_a, NF * g + j + 1)
                        act.activation(ahi[:, u, j, :], a[:, k, :], ACT.Copy).then_inc(s_ahi, 1)

                pipeline(act, G, body)

            @block.tensor
            def _(pe):
                pe.wait_ge(s_c, 32)
                pe.wait_ge(s_wlo, 3)

                def total(i):
                    pe.wait_ge(s_n, i + 1)
                    pe.matmul(ps[:, 0, 0:1], same[:, :], cnt[:, :], start=True, stop=True).then_inc(s_tot, 1)

                def down(g, u, tiles):
                    pe.wait_ge(s_alo, NF * g + NF)
                    for t in tiles:
                        tok = slice(128 * t, 128 * t + 128)
                        pe.wait_ge(s_o, 4 * g + t + 1)
                        n = 0
                        for f in range(NF):
                            for v, w in ((ahi, wdhi), (ahi, wdlo), (alo, wdhi)):
                                last = pe.matmul(ps[:, 6 + t % 2, 0:D], v[:, u, f, tok], w[:, f, :],
                                                 start=(n == 0), stop=(n == 3 * NF - 1))
                                n += 1
                        last.then_inc(s_d, 1)

                def body(g, r, u, before, after):
                    cols = bass.ds(g * 512, 512)
                    v = (xhi[:, cols], xlo[:, cols], xmix[:, cols])
                    bit = PER_GROUP * g
                    for j in range(NF):
                        k = (u + j) % 2
                        if not (isinstance(g, int) and NF * g + j < 2):
                            pe.wait_ge(s_a, NF * g + j - 1)
                        for bank, c in ((2, 128 * j), (4, FS + 128 * j)):
                            c = slice(c, c + 128)
                            last = five_passes(pe, ps[:, bank + k, :], (whi[:, c], wlo[:, c], w2hi[:, c], w2lo[:, c]), v)
                        last.then_inc(s_gu, 1)
                        if j > 0 or before:
                            total(bit + j if j else bit - 1)
                        if j == 0:
                            if before:
                                down(g - 1, 1 - u, (0, 1))
                            total(bit)
                            if before:
                                down(g - 1, 1 - u, (2, 3))
                    if not after:
                        total(bit + 3)
                        down(g, u, range(4))

                pipeline(pe, G, body)


def select(nc, A, S, ident, scores, limit, weights):
    CH_N = 512
    BF16 = mybir.dt.bfloat16
    with ExitStack() as ctx:
        m = Mem(nc, ctx, "select")
        same, earlier = m.sb("same_expert", [128, 128]), m.sb("earlier_chunk", [128, 128])
        count = m.sb("count", [128, 32])
        part, tile_no = m.sb("partition", [128, 1]), m.sb("tile_number", [128, 32])
        cnt = m.sb("partial_count", [128, 2])
        mask = m.sb("mask", [128, CH_N])
        gt, eq, rank, sel, place = (m.sb(n, [128, CH_N]) for n in ("above", "equal", "rank", "chosen", "place"))
        room = m.sb("room", [128, 1])
        pl, hi, lo = (m.sb(n, [128, CH_N], I32) for n in ("place_int", "place_hi", "place_lo"))
        hif, lof = m.sb("place_hi_f", [128, CH_N]), m.sb("place_lo_f", [128, CH_N])
        hit, lot = m.sb("place_hi_t", [128, E, 32]), m.sb("place_lo_t", [128, E, 32])
        hot = m.sb("one_hot_hi", [128, 2, 32, 32], BF16)
        low = m.sb("one_hot_lo", [128, 2, 32, 16], BF16)
        val = m.sb("values", [128, 2, 2, 32, 16], BF16)
        ids = m.sb("ids", [32, E, 16], I32)
        idf = m.sb("tile_part", [32, E, 16])
        ps_c = m.psum("ps_count", [128, 512])
        ps_t = m.psum("ps_places", [128, 2, 512])
        ps_i = m.psum("ps_ids", [128, 512])

        s_c = m.sem("select_consts_loaded")
        s_w = m.sem("first_weights_loaded")
        s_v = m.sem("select_step")
        s_n, s_tot = m.sem("counted"), m.sem("total_ready")
        s_pf, s_tr, s_te = m.sem("places_ready"), m.sem("places_transposed"), m.sem("places_read")
        s_hot, s_low = m.sem("hi_ready"), m.sem("lo_ready")
        s_vp, s_vt = m.sem("partition_values_ready"), m.sem("tile_values_ready")
        s_id = m.sem("ids_product")
        s_out, s_st = m.sem("ids_ready"), m.sem("ids_stored")

        with nc.Block() as block:

            @block.sync
            def _(sp):
                for dst, name in ((same, "same_expert"), (earlier, "earlier_chunk"), (count, "count"),
                                  (part, "partition"), (tile_no, "tile_number")):
                    sp.dma_start(dst[:, :], A[name]).then_inc(s_c, 16)
                for e in range(2):
                    load_gate_up(sp, A, weights, e, e, s_w)
                    load_down(sp, A, weights, e, e, s_w)
                sp.wait_ge(s_w, 2 * 4 * 16)
                sp.wait_ge(s_out, 1)
                sp.dma_start(S["ids"].rearrange("e (a b) -> a e b", b=16), ids[:, :, :]).then_inc(s_st, 16)
                sp.wait_ge(s_st, 16)

            @block.vector
            def _(dve):
                dve.sem_inc(s_id, 2)
                dve.wait_ge(s_c, 80)
                n = 0

                def step(ins):
                    nonlocal n
                    n += 1
                    ins.then_inc(s_v, 1)
                    dve.wait_ge(s_v, n)

                least = limit[:, 0:1].bitcast(F32)
                dve.tensor_scalar(gt[:, :], scores[:, :], least, 0.0, ALU.is_gt, ALU.add, accum_out=cnt[:, 0:1])
                dve.tensor_scalar(eq[:, :], scores[:, :], least, 0.0, ALU.is_equal, ALU.add, accum_out=cnt[:, 1:2]).then_inc(s_n, 1)
                dve.wait_ge(s_n, 1)
                step(dve.tensor_tensor_scan(rank[:, :], eq[:, :], eq[:, :], 0.0, ALU.add, ALU.max))
                dve.wait_ge(s_tot, 1)
                step(dve.tensor_scalar(room[:, :], ps_c[:, 0:1], -1.0, float(CAP), ALU.mult, ALU.add))
                step(dve.scalar_tensor_tensor(mask[:, :], rank[:, :], room[:, 0:1], eq[:, :], ALU.is_le, ALU.mult))
                step(dve.tensor_tensor(sel[:, :], mask[:, :], gt[:, :], ALU.add))
                dve.tensor_tensor_scan(rank[:, :], sel[:, :], sel[:, :], 0.0, ALU.add, ALU.max).then_inc(s_n, 1)
                dve.wait_ge(s_tot, 2)
                step(dve.scalar_tensor_tensor(place[:, :], rank[:, :], ps_c[:, 0:1], sel[:, :], ALU.add, ALU.mult))
                step(dve.tensor_scalar(pl[:, :], place[:, :], -1.0, None, ALU.add))
                dve.tensor_scalar(hi[:, :], pl[:, :], 4, None, ALU.arith_shift_right)
                step(dve.tensor_scalar(lo[:, :], pl[:, :], 15, None, ALU.bitwise_and))
                dve.tensor_copy(hif[:, :], hi[:, :])
                dve.tensor_copy(lof[:, :], lo[:, :]).then_inc(s_pf, 1)
                dve.wait_ge(s_te, 2)

                def pattern(n):
                    return count[:, 0:n].rearrange("p (o n) -> p o n", o=1).to_broadcast([128, 32, n])

                with dve.Fori(0, E // 2) as r:
                    for u in range(2):
                        e = 2 * r + u
                        col = bass.ds(e, 1)
                        dve.wait_ge(s_id, e + 1)
                        dve.tensor_tensor(low[:, u, :, :], lot[:, col, :].rearrange("p o q -> p q o").to_broadcast([128, 32, 16]),
                                          pattern(16), ALU.is_equal).then_inc(s_low, 1)
                        dve.tensor_tensor(hot[:, u, :, :], hit[:, col, :].rearrange("p o q -> p q o").to_broadcast([128, 32, 32]),
                                          pattern(32), ALU.is_equal).then_inc(s_hot, 1)
                dve.wait_ge(s_id, E + 2)
                both = ps_i[0:32, :].rearrange("p (e k b) -> p e k b", k=2, b=16)
                step(dve.tensor_copy(idf[:, :, :], both[:, :, 0, :]))
                dve.scalar_tensor_tensor(ids[:, :, :], both[:, :, 1, :], 128.0, idf[:, :, :], ALU.mult, ALU.add).then_inc(s_out, 1)

            @block.gpsimd
            def _(pool):
                with pool.Fori(0, E // 2) as r:
                    for u in range(2):
                        pool.wait_ge(s_low, 2 * r + u + 1)
                        pool.tensor_tensor(val[:, u, 1, :, :], low[:, u, :, :],
                                           tile_no[:, :].rearrange("p (q o) -> p q o", o=1).to_broadcast([128, 32, 16]),
                                           ALU.mult).then_inc(s_vt, 1)

            @block.scalar
            def _(act):
                for k, (dst, n) in enumerate(((hit, 0), (lot, 1))):
                    act.wait_ge(s_tr, k + 1)
                    act.activation(dst[:, :, :].rearrange("p e (j c) -> p j c e", j=4),
                                   ps_t[:, n, :].rearrange("p (j c e) -> p j c e", j=4, c=8), ACT.Copy).then_inc(s_te, 1)
                with act.Fori(0, E // 2) as r:
                    for u in range(2):
                        act.wait_ge(s_low, 2 * r + u + 1)
                        act.activation(val[:, u, 0, :, :], low[:, u, :, :], ACT.Copy, scale=part[:, 0:1]).then_inc(s_vp, 1)

            @block.tensor
            def _(pe):
                pe.wait_ge(s_n, 1)
                pe.matmul(ps_c[:, 0:1], same[:, :], cnt[:, 0:1], start=True, stop=False)
                pe.matmul(ps_c[:, 0:1], earlier[:, :], cnt[:, 1:2], start=False, stop=True).then_inc(s_tot, 1)
                pe.wait_ge(s_n, 2)
                pe.matmul(ps_c[:, 0:1], earlier[:, :], rank[:, CH_N - 1:CH_N], start=True, stop=True).then_inc(s_tot, 1)
                pe.wait_ge(s_pf, 1)
                for n, src in ((0, hif), (1, lof)):
                    for j in range(4):
                        last = pe.transpose(ps_t[:, n, 128 * j:128 * j + 128], src[:, 128 * j:128 * j + 128], ident[:, :])
                    last.then_inc(s_tr, 1)
                with pe.Fori(0, E // 2) as r:
                    for u in range(2):
                        e = 2 * r + u
                        pe.wait_ge(s_hot, e + 1)
                        pe.wait_ge(s_vp, e + 1)
                        pe.wait_ge(s_vt, e + 1)
                        for q in range(32):
                            last = pe.matmul(ps_i[0:32, bass.ds(32 * e, 32)], hot[:, u, q, :], val[:, u, :, q, :],
                                             start=(q == 0), stop=(q == 31))
                        last.then_inc(s_id, 1)


def load_gate_up(sp, A, weights, e, u, done):
    one = bass.ds(e, 1)
    rawa, rawb, _ = weights
    sp.dma_start(rawa[:, u:u + 1, :], A["wgu"][one, 0:128, :].rearrange("o p f -> p o f")).then_inc(done, 16)
    for half in (0, 64):
        sp.dma_start(rawb[half:half + 64, u:u + 1, :], A["wgu"][one, 128:192, :].rearrange("o p f -> p o f")).then_inc(done, 16)


def load_down(sp, A, weights, e, u, done):
    one = bass.ds(e, 1)
    sp.dma_start(weights[2][:, u:u + 1, :, :], A["wd"][one, :, :, :].rearrange("o p k n -> p o k n")).then_inc(done, 16)


def experts(nc, A, S, out, ident, weights):
    NF = FE // 128
    W = 2 * FE
    NT4 = CAP // 128
    with ExitStack() as ctx:
        m = Mem(nc, ctx, "experts")
        rawa, rawb, rawd = weights
        whi, wlo = m.sb("ewhi", [128, 2, W], F32R), m.sb("ewlo", [128, 2, W], F32R)
        w2hi, w2lo = m.sb("ew2hi", [128, 2, W], F32R), m.sb("ew2lo", [128, 2, W], F32R)
        wdhi, wdlo = m.sb("ewdhi", [128, 2, NF, D], F32R), m.sb("ewdlo", [128, 2, NF, D], F32R)
        idx = m.sb("token_numbers", [128, 2, NT4], I32)
        kept = m.sb("kept_numbers", [128, 2, NT4], I32)
        xg = m.sb("gathered", [128, 2, NT4, ROW])
        xhi, xlo, xmix = (m.sb(n, [128, 2, 512], F32R) for n in ("xghi", "xglo", "xgmix"))
        sc = m.sb("chosen_scores", [128, 2, NT4, 1])
        sg = m.sb("e_silu", [128, 2, 512])
        a = m.sb("e_act", [128, 2, 512])
        ahi, alo = m.sb("e_act_hi", [128, 2, NF, 512], F32R), m.sb("e_act_lo", [128, 2, NF, 512], F32R)
        y = m.sb("y_stage", [128, 2, NT4, D])
        ps = m.psum("ps_experts", [128, 8, 512])

        s_w = [m.sem(f"expert_weights_loaded{i}") for i in range(2)]
        s_wd = [m.sem(f"down_weights_loaded{i}") for i in range(2)]
        s_ix = [m.sem(f"numbers_loaded{i}") for i in range(2)]
        s_g = [m.sem(f"tokens_gathered{i}") for i in range(2)]
        s_whi, s_wlo = m.sem("expert_hi_made"), m.sem("expert_lo_made")
        s_w2lo = m.sem("expert_lo2_made")
        s_wdhi, s_wdlo = m.sem("down_hi_made"), m.sem("down_lo_made")
        s_tr, s_hi, s_lo = m.sem("xg_transposed"), m.sem("xg_hi_made"), m.sem("xg_lo_made")
        s_gu, s_sg = m.sem("e_gate_up_product"), m.sem("e_silu_done")
        s_a, s_ahi, s_alo = m.sem("e_act_made"), m.sem("e_act_hi_made"), m.sem("e_act_lo_made")
        s_sc = m.sem("chosen_scores_ready")
        s_d, s_y = m.sem("e_down_product"), m.sem("y_ready")
        s_kept = m.sem("numbers_kept")
        s_sct = m.sem("y_scattered")
        s_go = m.sem("pool_waits_passed")

        with nc.Block() as block:

            @block.sync
            def _(sp):
                def body(e, r, u, before, after):
                    one = bass.ds(e, 1)
                    if not opening(r):
                        sp.wait_ge(s_g[u], 64 * r)
                        sp.wait_ge(s_kept, e - 1)
                    sp.dma_start(idx[:, u, :].rearrange("p (o k) -> p o k", o=1),
                                 S["ids"][one, :].rearrange("o (p k) -> p o k", p=128)).then_inc(s_ix[u], 16)
                    if not opening(r):
                        sp.wait_ge(s_w2lo, e - 1)
                        sp.wait_ge(s_wlo, e - 1)
                        load_gate_up(sp, A, weights, e, u, s_w[u])
                        sp.wait_ge(s_wdlo, e - 1)
                        load_down(sp, A, weights, e, u, s_wd[u])

                pipeline(sp, E, body)

            @block.gpsimd
            def _(pool):
                def gather(u):
                    for k in range(NT4):
                        pool.indirect_dma_start(
                            out=xg[:, u, k, :], out_offset=None, in_=S["rows"],
                            in_offset=bass.IndirectOffsetOnAxis(ap=idx[:, u, k:k + 1].bitcast(U32), axis=0)).then_inc(s_g[u], 16)

                def scatter(e, u):
                    pool.wait_ge(s_y, NT4 * e + NT4 + 2)
                    if not (isinstance(e, int) and e == 0):
                        pool.wait_ge(s_sct, 64 * e)
                    pool.sem_inc(s_go, 1)
                    for k in range(NT4):
                        pool.indirect_dma_start(
                            out=out, in_=y[:, u, k, :], in_offset=None, compute_op=ALU.add,
                            out_offset=bass.IndirectOffsetOnAxis(ap=kept[:, u, k:k + 1].bitcast(U32), axis=0)).then_inc(s_sct, 16)

                def body(e, r, u, before, after):
                    if after:
                        pool.wait_ge(s_whi, 2 * e + 4)
                        pool.sem_inc(s_go, 1)
                        weights_lo(1 - u, rawb, w2hi, w2lo, s_w2lo)
                    if before:
                        scatter(e - 1, 1 - u)
                    if not opening(r):
                        pool.wait_ge(s_sct, 64 * e - 64)
                    pool.sem_inc(s_go, 1)
                    pool.tensor_copy(kept[:, u, :], idx[:, u, :]).then_inc(s_kept, 1)
                    if not isinstance(e, int) or e + 2 < E:
                        pool.wait_ge(s_ix[u], 16 * r + 32)
                        pool.wait_ge(s_tr, e + 1)
                        pool.wait_ge(s_sc, e + 1)
                        pool.sem_inc(s_go, 1)
                        gather(u)
                    if after:
                        pool.wait_ge(s_wdhi, e + 2)
                        pool.sem_inc(s_go, 1)
                        weights_lo(1 - u, rawd, wdhi, wdlo, s_wdlo)
                    pool.wait_ge(s_kept, e + 1)
                    if not after:
                        pool.sem_inc(s_go, 1)
                        scatter(e, u)

                def weights_lo(u, raw, hi, lo, done):
                    ix = (slice(None), u) + (slice(None),) * (len(raw.shape) - 2)
                    pool.tensor_tensor(lo[ix], raw[ix], hi[ix].bitcast(F32), ALU.subtract).then_inc(done, 1)

                for u in range(2):
                    pool.wait_ge(s_ix[u], 16)
                    gather(u)
                pool.wait_ge(s_whi, 2)
                weights_lo(0, rawb, w2hi, w2lo, s_w2lo)
                pool.wait_ge(s_wdhi, 1)
                weights_lo(0, rawd, wdhi, wdlo, s_wdlo)
                pipeline(pool, E, body)
                pool.wait_ge(s_sct, 64 * E)

            @block.scalar
            def _(act):
                def weights_hi(u, n, part):
                    if part < 2:
                        if not (isinstance(n, int) and n == 0):
                            act.wait_ge(s_w[u], n * 48)
                        raw, hi = ((rawa, whi), (rawb, w2hi))[part]
                        act.activation(hi[:, u, :], raw[:, u, :], ACT.Copy).then_inc(s_whi, 1)
                    else:
                        if not (isinstance(n, int) and n == 0):
                            act.wait_ge(s_wd[u], n * 16)
                        act.activation(wdhi[:, u, :, :], rawd[:, u, :, :], ACT.Copy).then_inc(s_wdhi, 1)

                def hi_parts(e, u):
                    act.wait_ge(s_tr, e + 1)
                    act.activation(xhi[:, u, :], ps[:, 0, :], ACT.Copy).then_inc(s_hi, 1)
                    act.activation(xmix[:, u, :], ps[:, 1, :], ACT.Copy).then_inc(s_hi, 1)

                weights_hi(0, 0, 0)
                weights_hi(0, 0, 1)
                hi_parts(0, 0)
                weights_hi(0, 0, 2)

                def body(e, r, u, before, after):
                    for j in range(NF):
                        act.wait_ge(s_gu, NF * e + j + 1)
                        act.activation(sg[:, j % 2, :], ps[:, 2 + j % 2, :], ACT.Silu).then_inc(s_sg, 1)
                        act.wait_ge(s_a, NF * e + j + 1)
                        act.activation(ahi[:, u, j, :], a[:, j % 2, :], ACT.Copy).then_inc(s_ahi, 1)
                        if after and j == 1:
                            weights_hi(1 - u, r + u, 0)
                            weights_hi(1 - u, r + u, 1)
                        if after and j == 2:
                            if before:
                                act.wait_ge(s_d, NT4 * e)
                            weights_hi(1 - u, r + u, 2)
                        if after and j == 3:
                            hi_parts(e + 1, 1 - u)

                pipeline(act, E, body)

            @block.vector
            def _(dve):
                dve.sem_inc(s_y, 2)

                def weights_lo(e, u):
                    dve.wait_ge(s_whi, 2 * e + 1)
                    dve.tensor_tensor(wlo[:, u, :], rawa[:, u, :], whi[:, u, :].bitcast(F32), ALU.subtract).then_inc(s_wlo, 1)

                def lo_parts(e, u, n):
                    dve.wait_ge(s_hi, 2 * e + 1)
                    dve.tensor_tensor(xlo[:, u, :], ps[:, 0, :], xhi[:, u, :].bitcast(F32), ALU.subtract).then_inc(s_lo, 1)
                    dve.wait_ge(s_hi, 2 * e + 2)
                    dve.tensor_tensor(xmix[64:128, u, :], ps[64:128, 1, :], xmix[64:128, u, :].bitcast(F32),
                                      ALU.subtract).then_inc(s_lo, 1)
                    dve.wait_ge(s_g[u], 64 * n)
                    dve.tensor_copy(sc[:, u, :, :], xg[:, u, :, bass.ds(256 + e, 1)]).then_inc(s_sc, 1)

                def weigh(e, u):
                    dve.wait_ge(s_sc, e + 1)
                    if not (isinstance(e, int) and e < 2):
                        dve.wait_ge(s_sct, 64 * e - 64)
                    for t in range(NT4):
                        dve.wait_ge(s_d, NT4 * e + t + 1)
                        dve.tensor_scalar(y[:, u, t, :], ps[:, 6 + t % 2, 0:D], sc[:, u, t, 0:1], None,
                                          ALU.mult).then_inc(s_y, 1)

                weights_lo(0, 0)
                lo_parts(0, 0, 1)

                def body(e, r, u, before, after):
                    for j in range(NF):
                        dve.wait_ge(s_sg, NF * e + j + 1)
                        dve.tensor_tensor(a[:, j % 2, :], sg[:, j % 2, :], ps[:, 4 + j % 2, :], ALU.mult).then_inc(s_a, 1)
                        dve.wait_ge(s_ahi, NF * e + j + 1)
                        dve.tensor_tensor(alo[:, u, j, :], a[:, j % 2, :], ahi[:, u, j, :].bitcast(F32), ALU.subtract)\
                            .then_inc(s_alo, 1)
                        if j == 1 and before:
                            weigh(e - 1, 1 - u)
                        if after and j == 1:
                            weights_lo(e + 1, 1 - u)
                        if after and j == 3:
                            lo_parts(e + 1, 1 - u, r + u + 1)
                    if not after:
                        weigh(e, u)

                pipeline(dve, E, body)

            @block.tensor
            def _(pe):
                pe.wait_ge(s_g[0], 64)
                transpose_group(pe, ps, xg, 0, ident, s_tr)

                def down(e, u):
                    pe.wait_ge(s_alo, NF * e + NF)
                    pe.wait_ge(s_wdlo, e + 1)
                    for t in range(NT4):
                        tok = slice(128 * t, 128 * t + 128)
                        pe.wait_ge(s_y, NT4 * e + t + 1)
                        n = 0
                        for f in range(NF):
                            for x, w in ((ahi, wdhi), (ahi, wdlo), (alo, wdhi)):
                                last = pe.matmul(ps[:, 6 + t % 2, 0:D], x[:, u, f, tok], w[:, u, f, :],
                                                 start=(n == 0), stop=(n == 3 * NF - 1))
                                n += 1
                        last.then_inc(s_d, 1)

                def body(e, r, u, before, after):
                    x = (xhi[:, u, :], xlo[:, u, :], xmix[:, u, :])
                    pe.wait_ge(s_wlo, e + 1)
                    pe.wait_ge(s_w2lo, e + 1)
                    pe.wait_ge(s_hi, 2 * e + 2)
                    pe.wait_ge(s_lo, 2 * e + 2)
                    for j in range(NF):
                        if before or j >= 2:
                            pe.wait_ge(s_a, NF * e + j - 1)
                        for bank, c in ((2, 128 * j), (4, FE + 128 * j)):
                            c = slice(c, c + 128)
                            last = five_passes(pe, ps[:, bank + j % 2, :],
                                               (whi[:, u, c], wlo[:, u, c], w2hi[:, u, c], w2lo[:, u, c]), x)
                        last.then_inc(s_gu, 1)
                        if j == 1 and before:
                            down(e - 1, 1 - u)
                        if j == 3 and after:
                            pe.wait_ge(s_g[1 - u], 64 * (r + u) + 64)
                            transpose_group(pe, ps, xg, 1 - u, ident, s_tr)
                    if not after:
                        down(e, u)

                pipeline(pe, E, body)


def opening(r):
    return isinstance(r, int) and r == 0


def vit_block(nc, A, out):
    def scratch(name, *shape, dt=F32):
        return nc.dram_tensor(name, shape, dt, kind="Internal").ap()

    S = {"q": scratch("q_scratch", H * HD, T), "k": scratch("k_scratch", H * HD, T), "v": scratch("v_scratch", T, H * HD),
         "f": scratch("feature_scratch", 3, 256, T), "w": scratch("block_sum_scratch", 3, 256, T),
         "rw": scratch("value_table_scratch", 128, H, D), "scores": scratch("score_scratch", 128, T // 8),
         "rows": scratch("row_scratch", T, ROW), "ids": scratch("chosen_scratch", E, CAP, dt=I32)}
    with ExitStack() as ctx:
        m = Mem(nc, ctx, "all")
        ident = m.sb("ident", [128, 128])
        epsc = m.sb("eps", [128, 1])
        scores = m.sb("scores", [128, T // 8])
        limit = m.sb("lowest_chosen", [128, 1], I32)
        s_eps = m.sem("eps_ready")
        with ExitStack() as residual:
            r = Mem(nc, residual, "all")
            h = r.sb("h", [128, NTILE, D])
            stat = r.sb("stat", [128, NTILE, 2])
            with nc.Block() as block:
                @block.vector
                def _(dve):
                    dve.memset(epsc[:, :], EPS).then_inc(s_eps, 1)
            tokenize(nc, A, h, ident, stat)
            project(nc, A, S, h, ident, stat, epsc)
            attend(nc, A, S, h, ident)
            relative(nc, A, S, h, ident, stat)
            x = tuple(r.sb(name, [128, T], F32R) for name in ("x_hi", "x_lo", "x_mixed"))
            score(nc, A, S, h, ident, stat, epsc, x, scores)
            share(nc, A, S, out, h, x, scores, limit)
        weights = (m.sb("gate_up_a", [128, 2, 2 * FE]), m.sb("gate_up_b", [128, 2, 2 * FE]),
                   m.sb("down", [128, 2, FE // 128, D]))
        select(nc, A, S, ident, scores, limit, weights)
        experts(nc, A, S, out, ident, weights)


def _layouts(x, L0_tok_W0, L0_tok_b0, L0_tok_W1, L0_tok_b1, L0_tok_W2, L0_tok_b2, L0_tok_Wf, L0_tok_bf,
             L0_tok_idx0, L0_tok_idx1, L0_tok_idx2, L0_attn_wq, L0_attn_wk, L0_attn_wv, L0_attn_wproj,
             L0_attn_bproj, L0_attn_rk_v, L0_attn_rk_h, L0_attn_rv_v, L0_attn_rv_h, L0_ffn_gate_weight,
             L0_ffn_Wg, L0_ffn_Wu, L0_ffn_Wd, L0_ffn_Ws_g, L0_ffn_Ws_u, L0_ffn_Ws_d):
    import numpy as np

    a = {k: np.asarray(v) for k, v in locals().items() if k != "np"}
    x = a["x"]

    def patches(p):
        n = IMG // p
        t = x.reshape(B, CH, n, p, n, p).transpose(2, 4, 0, 3, 5, 1)
        return t.reshape(n * n, B * p * p * CH)

    def rel(tv, th):
        z = np.zeros((HD, 128), np.float32)
        z0 = np.zeros((HD, 32), np.float32)
        for i in range(33):
            z[:, i] = tv[min(max(i - 16, -14), 14) + 15]
        for i in range(29):
            z[:, 48 + i] = th[i + 1]
        for i in range(ROWS):
            z[:, 96 + i] = tv[0]
            z0[:, i] = th[0]
        return z, z0

    rk, rk0 = rel(a["L0_attn_rk_v"], a["L0_attn_rk_h"])
    rv, rv0 = rel(a["L0_attn_rv_v"], a["L0_attn_rv_h"])
    row0 = np.stack([a["L0_attn_rk_v"][0], a["L0_attn_rk_h"][0]])
    rv_row0 = np.stack([np.tile(a["L0_attn_rv_v"][0], H), np.tile(a["L0_attn_rv_h"][0], H)])
    ind = np.zeros((64, NT), np.float32)
    for j in range(1, NT):
        ra, rc = divmod(j - 1, SIDE)
        ind[ra, j] = 1.0
        ind[32 + rc, j] = 1.0

    def rows128(w):
        return w[0:128], np.concatenate([w[128:192], w[128:192]])

    wqkv = np.concatenate([a["L0_attn_wq"], a["L0_attn_wk"], a["L0_attn_wv"]], axis=1)
    wqkv_a, wqkv_b = rows128(wqkv)
    wqt = a["L0_attn_wq"].T.reshape(H, HD, D).transpose(1, 0, 2)
    wqt = np.concatenate([wqt, wqt[:, :, 128:192]], axis=2)
    wsgu = np.concatenate([a["L0_ffn_Ws_g"].T, a["L0_ffn_Ws_u"].T], axis=1)
    wsgu_a, wsgu_b = rows128(wsgu)
    wgu = np.concatenate([a["L0_ffn_Wg"], a["L0_ffn_Wu"]], axis=1).transpose(0, 2, 1)
    gt = a["L0_ffn_gate_weight"].T
    out = {
        "x0": patches(1), "x1": patches(2), "x2": patches(4),
        "idx0t": a["L0_tok_idx0"].reshape(2, 128, GP).transpose(1, 0, 2).reshape(128, 2 * GP),
        "idx1t": a["L0_tok_idx1"].reshape(64, GP),
        "idx2t": a["L0_tok_idx2"].reshape(2, 128).T,
        "w0t": a["L0_tok_W0"].T, "w1t": a["L0_tok_W1"].T,
        "w2t": a["L0_tok_W2"].reshape(EMB, GP, 48).transpose(2, 1, 0),
        "wft": a["L0_tok_Wf"].T,
        "tokb": np.stack([a["L0_tok_b0"], a["L0_tok_b1"], a["L0_tok_b2"]], axis=1),
        "bf": a["L0_tok_bf"],
        "ident": np.eye(128, dtype=np.float32),
        "wqkv_a": wqkv_a, "wqkv_b": wqkv_b, "wqt": wqt,
        "rk": rk, "rk0": rk0, "rv": rv, "rv0": rv0,
        "krow": np.concatenate([row0, row0], axis=1).T,
        "vrow": rv_row0,
        "ind": ind,
        "indt": ind.T.reshape(2, 128, 64).transpose(1, 0, 2),
        "wproj": a["L0_attn_wproj"],
        "wproj_h": a["L0_attn_wproj"].reshape(3, 4, HD, D).transpose(2, 1, 0, 3).reshape(HD, H, D),
        "bproj": a["L0_attn_bproj"],
        "wsgu_a": wsgu_a, "wsgu_b": wsgu_b,
        "wsd": a["L0_ffn_Ws_d"].T.reshape(3, 128, D).transpose(1, 0, 2),
        "wgu": wgu,
        "wd": a["L0_ffn_Wd"].transpose(0, 2, 1).reshape(E, 6, 128, D).transpose(0, 2, 1, 3),
        "gate": gt,
        "same_expert": np.tile(np.eye(E, dtype=np.float32), (8, 8)),
        "earlier_chunk": np.kron(np.triu(np.ones((8, 8), np.float32), 1), np.eye(E, dtype=np.float32)),
        "bits": np.broadcast_to(np.append(1 << np.arange(29, -1, -1), [0, 0]).astype(np.int32), (128, 32)),
        "count": np.broadcast_to(np.arange(32, dtype=np.float32), (128, 32)),
        "partition": np.arange(128, dtype=np.float32)[:, None],
        "tile_number": np.broadcast_to((4 * np.arange(8)[None, :] + np.arange(4)[:, None]).astype(np.float32).reshape(32), (128, 32)),
    }
    return {k: np.ascontiguousarray(v) for k, v in out.items()}


def kernel(**inputs):
    import concourse.bacc as bacc
    from concourse.bass_utils import run_bass_kernel_spmd

    nc = bacc.Bacc("TRN2", target_bir_lowering=False, num_devices=1)
    arrays = _layouts(**inputs)
    A = {k: nc.dram_tensor(f"in_{k}", v.shape, mybir.dt.from_np(v.dtype), kind="ExternalInput").ap()
         for k, v in arrays.items()}
    out = nc.dram_tensor("out_h", (T, D), F32, kind="ExternalOutput").ap()
    vit_block(nc, A, out)
    r = run_bass_kernel_spmd(nc, [{f"in_{k}": v for k, v in arrays.items()}], core_ids=[0])
    return r.results[0]["out_h"].reshape(B, NT, D)
```

```python
from contextlib import ExitStack

import concourse.bass as bass
from concourse import mybir

F32 = mybir.dt.float32
F32R = mybir.dt.float32r
I32 = mybir.dt.int32
U32 = mybir.dt.uint32
ALU = mybir.AluOpType
ACT = mybir.ActivationFunctionType
AX = mybir.AxisListType

B, IMG, CH = 16, 64, 3
GP = 16
EMB = 64
D = 192
NT = 256
T = B * NT
NTILE = T // 128
H, HD = 12, 64
SIDE = 15
ROWS = (NT - 1) // SIDE
EPS = 1e-5
E, CAP, FE, FS = 16, 512, 768, 384


class Mem:

    spent = []

    def __init__(self, nc, ctx, phase):
        self.nc, self.ctx, self.phase = nc, ctx, phase

    @classmethod
    def reclaim(cls, nc):
        nc.clear_and_free_semaphores(cls.spent)
        nc.all_engine_barrier()
        cls.spent.clear()

    def sb(self, name, shape, dt=F32):
        return self.ctx.enter_context(self.nc.sbuf_tensor(f"{self.phase}_{name}", shape, dt))

    def psum(self, name, shape):
        return self.ctx.enter_context(self.nc.psum_tensor(f"{self.phase}_{name}", shape, F32))

    def sem(self, name):
        self.spent.append(self.nc.alloc_semaphore(name=f"{self.phase}_{name}"))
        return self.spent[-1]


def norm_stats(dve, h, stat, raw, t, last, s_hf, s_bn, s_agg, tile=lambda k: k):
    for k in ([t] if t + 1 < last else [t, t + 1, t + 2]):
        if 1 <= k <= last:
            dve.wait_ge(s_hf, k)
            if k >= 3:
                dve.wait_ge(s_agg, k - 2)
            dve.bn_stats(raw[:, (k - 1) % 2, :], h[:, tile(k - 1), :]).then_inc(s_bn, 1)
        if 2 <= k:
            dve.wait_ge(s_bn, k - 1)
            dve.bn_aggr(stat[:, tile(k - 2), 0:2], raw[:, k % 2, :]).then_inc(s_agg, 1)


def tokenize(nc, A, S, h, ident, stat, qkv):
    with ExitStack() as ctx:
        m = Mem(nc, ctx, "tokenize")
        idx0 = m.sb("idx0", [128, 2 * GP], I32)
        idx1 = m.sb("idx1", [64, GP], I32)
        idx2 = m.sb("idx2", [128, 2], I32)
        w0 = m.sb("w0", [48, EMB])
        w1a = m.sb("w1a", [128, EMB])
        w1b = m.sb("w1b", [64, EMB])
        w2 = m.sb("w2", [48, GP, EMB])
        wfa = m.sb("wfa", [128, D])
        wfb = m.sb("wfb", [64, D])
        bias = m.sb("bias", [64, 3])
        bf = m.sb("bf", [128, D])
        g0 = m.sb("g0", [128, 2, GP, B * CH])
        g0r = m.sb("g0r", [128, 2, B, GP * CH])
        g1 = m.sb("g1", [64, GP, B * 12])
        g1r = m.sb("g1r", [64, B, GP * 12])
        g2 = m.sb("g2", [128, 2, B * 48])
        t0 = m.sb("t0", [48, B, 2, 128])
        t1a = m.sb("t1a", [128, B, 64])
        t1b = m.sb("t1b", [64, B, 64])
        t2 = m.sb("t2", [48, 2 * B, 8, GP])
        o1 = m.sb("o1", [64, B, 66])
        o2 = m.sb("o2", [64, B, 18])
        part = m.sb("part", [64, B, 64])
        ct = m.sb("ct", [128, B, NT])
        ct2 = m.sb("ct2", [64, B, NT])
        raw = m.sb("tok_bn", [128, 2, 6])
        rv, rv0 = m.sb("rv", [HD, 128]), m.sb("rv0", [HD, 32])
        wh = g1[:, 0:H, :]
        rw = m.sb("rw_stage", [128, 6, 2 * D])
        ps = m.psum("ps_tok", [128, 8, 512])

        s_idx = m.sem("idx_loaded")
        s_w = m.sem("tok_weights_loaded")
        s_g2, s_g1 = m.sem("g2_gathered"), m.sem("g1_gathered")
        s_g0 = [m.sem(f"g0_gathered{i}") for i in range(2)]
        s_reord, s_reord0 = m.sem("g1_reordered"), m.sem("g0_reordered")
        s_pe = m.sem("tok_pe_done")
        s_ev = m.sem("tok_bank_read")
        s_dv = m.sem("tok_dve")
        s_ct = m.sem("ct_ready")
        s_wf = m.sem("fused")
        s_hf = m.sem("h_written")
        s_rl, s_wh = m.sem("rv_loaded"), m.sem("wproj_loaded")
        s_rv, s_rws = m.sem("rv_ready"), m.sem("rw_stored_and_qkv_loaded")
        s_bn = m.sem("bn_stats_done")
        s_agg = m.sem("bn_aggregated")

        N2, N1, N0, NJ = 8, 8 + 1 + 4, 8 + 1 + 4 + 2 + 6, 8 + 1 + 4 + 2 + 6 + 16

        def tile(n):
            return 2 * (n % B) + n // B


        with nc.Block() as block:

            @block.sync
            def _(sp):
                sp.dma_start(idx2[:, :], A["idx2t"]).then_inc(s_idx, 16)
                sp.dma_start(idx1[:, :], A["idx1t"]).then_inc(s_idx, 16)
                sp.dma_start(idx0[:, :], A["idx0t"]).then_inc(s_idx, 16)
                sp.dma_start(ident[:, :], A["ident"]).then_inc(s_w, 16)
                sp.dma_start(w0[:, :], A["w0t"]).then_inc(s_w, 16)
                sp.dma_start(w1a[:, :], A["w1t"][0:128, :]).then_inc(s_w, 16)
                sp.dma_start(w1b[:, :], A["w1t"][128:192, :]).then_inc(s_w, 16)
                sp.dma_start(w2[:, :, :], A["w2t"]).then_inc(s_w, 16)
                sp.dma_start(wfa[:, :], A["wft"][0:128, :]).then_inc(s_w, 16)
                sp.dma_start(wfb[:, :], A["wft"][128:192, :]).then_inc(s_w, 16)
                sp.dma_start(bias[:, :], A["tokb"]).then_inc(s_w, 16)
                sp.dma_start(bf[:, :], A["bf"].partition_broadcast(128)).then_inc(s_w, 16)
                sp.dma_start(rv[:, :], A["rv"]).then_inc(s_rl, 16)
                sp.dma_start(rv0[:, :], A["rv0"]).then_inc(s_rl, 16)
                for dst, name in zip(qkv, ("wqkv_a", "wqkv_b")):
                    sp.dma_start(dst, A[name]).then_inc(s_rws, 16)
                sp.wait_ge(s_reord, 1)
                sp.dma_start(wh, A["wproj_h"]).then_inc(s_wh, 16)
                sp.wait_ge(s_ev, N0)
                sp.dma_start(S["rw"].rearrange("t h n -> t (h n)"), rw[:, :, :].rearrange("p j n -> p (j n)")).then_inc(s_rws, 16)
                sp.wait_ge(s_rws, 48)

            @block.gpsimd
            def _(pool):
                def gather(dst, table, index, done):
                    pool.indirect_dma_start(
                        out=dst, out_offset=None, in_=table,
                        in_offset=bass.IndirectOffsetOnAxis(ap=index.bitcast(U32), axis=0)).then_inc(done, 16)

                pool.wait_ge(s_idx, 48)
                for i in range(2):
                    gather(g2[:, i, :], A["x2"], idx2[:, i:i + 1], s_g2)
                for s in range(GP):
                    gather(g1[:, s, :], A["x1"], idx1[:, s:s + 1], s_g1)
                for i in range(2):
                    for s in range(GP):
                        gather(g0[:, i, s, :], A["x0"], idx0[:, i * GP + s:i * GP + s + 1], s_g0[i])

            @block.vector
            def _(dve):
                dve.wait_ge(s_rl, 32)
                dve.tensor_tensor(rv[:, 96:128], rv[:, 96:128], rv0[:, :], ALU.add).then_inc(s_rv, 1)
                dve.wait_ge(s_g1, 16 * GP)
                dve.tensor_copy(g1r[:, :, :].rearrange("p b (s f) -> p b s f", s=GP),
                                g1[:, :, :].rearrange("p s (b f) -> p b s f", b=B)).then_inc(s_reord, 1)
                done = 0

                def step(ins):
                    nonlocal done
                    done += 1
                    ins.then_inc(s_dv, 1)
                    dve.wait_ge(s_dv, done)

                def interpolate(o, n, dst):
                    step(dve.tensor_copy(o[:, :, 0:1], o[:, :, 1:2]))
                    step(dve.tensor_copy(o[:, :, n + 1:n + 2], o[:, :, n:n + 1]))
                    r = NT // n
                    out = dst.rearrange("p b (k r) -> p b k r", r=r)
                    for i in range(r):
                        f = (i + 0.5) / r - 0.5
                        low = 0 if f < 0 else 1
                        wt = f + 1 if f < 0 else f
                        step(dve.tensor_scalar(part[:, :, 0:n], o[:, :, low:low + n], 1.0 - wt, None, ALU.mult))
                        ins = dve.scalar_tensor_tensor(out[:, :, :, i], o[:, :, low + 1:low + 1 + n], wt,
                                                       part[:, :, 0:n], ALU.mult, ALU.add)
                        step(ins)

                dve.wait_ge(s_ev, N2 + 1)
                interpolate(o2, 16, ct2[:, :, :])
                dve.wait_ge(s_ev, N1 + 2)
                interpolate(o1, 64, ct[64:128, :, :])
                dve.tensor_copy(part[0:1, 0, 0:1], o1[0:1, 0, 0:1]).then_inc(s_ct, 1)
                dve.wait_ge(s_w, 16 * 9)
                for n in range(NTILE):
                    dve.wait_ge(s_wf, n + 1)
                    dve.tensor_tensor(h[:, tile(n), :], ps[:, n % 8, 0:D], bf[:, :], ALU.add).then_inc(s_hf, 1)
                    norm_stats(dve, h, stat, raw, n, NTILE, s_hf, s_bn, s_agg, tile)

            @block.scalar
            def _(act):
                n = 0

                def evac(dst, src, bias_col=None):
                    nonlocal n
                    act.wait_ge(s_pe, n + 1)
                    if bias_col is None:
                        act.activation(dst, src, ACT.Copy).then_inc(s_ev, 1)
                    else:
                        act.activation(dst, src, ACT.Identity, bias=bias[:, bias_col:bias_col + 1]).then_inc(s_ev, 1)
                    n += 1

                act.wait_ge(s_w, 16 * 9)
                for j in range(8):
                    evac(t2[:, 4 * j:4 * j + 4, :, :].rearrange("p a g s -> p (a g s)"), ps[0:48, n % 8, :])
                evac(o2[:, :, 1:17], ps[0:64, n % 8, 0:256].rearrange("p (b g) -> p b g", b=B), 2)
                for j in range(2):
                    evac(t1a[:, 8 * j:8 * j + 8, :].rearrange("p b g -> p (b g)"), ps[:, n % 8, :])
                    evac(t1b[:, 8 * j:8 * j + 8, :].rearrange("p b g -> p (b g)"), ps[0:64, n % 8, :])
                for j in range(2):
                    evac(o1[:, 8 * j:8 * j + 8, 1:65], ps[0:64, n % 8, :].rearrange("p (b g) -> p b g", b=8), 1)
                for j in range(6):
                    evac(rw[:, j, :], ps[:, n % 8, 0:2 * D])
                for i in range(2):
                    act.wait_ge(s_g0[i], 16 * GP)
                    act.activation(g0r[:, i, :, :].rearrange("p b (s f) -> p b s f", s=GP),
                                   g0[:, i, :, :].rearrange("p s (b f) -> p b s f", b=B), ACT.Copy).then_inc(s_reord0, 1)
                    for j in range(4):
                        evac(t0[:, 4 * j:4 * j + 4, i, :], ps[0:48, n % 8, :].rearrange("p (b g) -> p b g", b=4))
                    for j in range(4):
                        evac(ct[0:64, 4 * j:4 * j + 4, 128 * i:128 * i + 128],
                             ps[0:64, n % 8, :].rearrange("p (b g) -> p b g", b=4), 0)
                assert n == NJ

            @block.tensor
            def _(pe):
                n = 0

                def bank():
                    if n >= 8:
                        pe.wait_ge(s_ev, n - 7)
                    return n % 8

                pe.wait_ge(s_w, 16 * 9)
                pe.wait_ge(s_g2, 32)
                for j in range(8):
                    k = bank()
                    for q in range(4):
                        b, i = 2 * j + q // 2, q % 2
                        last = pe.transpose(ps[0:48, k, 128 * q:128 * q + 128], g2[:, i, 48 * b:48 * b + 48], ident[:, :])
                    last.then_inc(s_pe, 1)
                    n += 1
                k = bank()
                pe.wait_ge(s_ev, 8)
                for s in range(GP):
                    last = pe.matmul(ps[0:64, k, 0:256], w2[:, s, :], t2[:, :, :, s], start=(s == 0), stop=(s == GP - 1))
                last.then_inc(s_pe, 1)
                n += 1
                pe.wait_ge(s_reord, 1)
                for j in range(2):
                    for lo, wide in ((0, 128), (128, 64)):
                        k = bank()
                        for q in range(8):
                            last = pe.transpose(ps[0:wide, k, 64 * q:64 * q + 64], g1r[:, 8 * j + q, lo:lo + wide],
                                                ident[0:64, 0:64])
                        last.then_inc(s_pe, 1)
                        n += 1
                pe.wait_ge(s_ev, N1)
                for j in range(2):
                    k = bank()
                    pe.matmul(ps[0:64, k, :], w1a[:, :], t1a[:, 8 * j:8 * j + 8, :].rearrange("p b g -> p (b g)"), start=True, stop=False)
                    pe.matmul(ps[0:64, k, :], w1b[:, :], t1b[:, 8 * j:8 * j + 8, :].rearrange("p b g -> p (b g)"),
                              start=False, stop=True).then_inc(s_pe, 1)
                    n += 1
                pe.wait_ge(s_rv, 1)
                pe.wait_ge(s_wh, 16)
                for j in range(6):
                    k = bank()
                    pe.matmul(ps[:, k, 0:2 * D], rv[:, :], wh[:, 2 * j:2 * j + 2, :].rearrange("p h n -> p (h n)"),
                              start=True, stop=True).then_inc(s_pe, 1)
                    n += 1
                for i in range(2):
                    if i:
                        pe.wait_ge(s_hf, B)
                    pe.wait_ge(s_reord0, 1 + i)
                    for j in range(4):
                        k = bank()
                        for q in range(4):
                            last = pe.transpose(ps[0:48, k, 128 * q:128 * q + 128], g0r[:, i, 4 * j + q, :], ident[:, :])
                        last.then_inc(s_pe, 1)
                        n += 1
                    pe.wait_ge(s_ev, N0 + 8 * i + 4)
                    for j in range(4):
                        k = bank()
                        pe.matmul(ps[0:64, k, :], w0[:, :], t0[:, 4 * j:4 * j + 4, i, :], start=True, stop=True).then_inc(s_pe, 1)
                        n += 1
                    pe.wait_ge(s_ct, 1)
                    pe.wait_ge(s_ev, N0 + 8 * i + 8)
                    for b in range(B):
                        t = B * i + b
                        if b >= 8:
                            pe.wait_ge(s_hf, t - 7)
                        pe.matmul(ps[:, t % 8, 0:D], ct[:, b, 128 * i:128 * i + 128], wfa[:, :], start=True, stop=False)
                        pe.matmul(ps[:, t % 8, 0:D], ct2[:, b, 128 * i:128 * i + 128], wfb[:, :], start=False, stop=True).then_inc(s_wf, 1)


def five_passes(pe, out, w, x, x_stationary=False):
    pairs = [(w[0], x[0]), (w[0], x[1]), (w[1], x[0]), (w[2], x[2]), (w[3], x[2])]
    for i, (a, b) in enumerate(pairs):
        if x_stationary:
            a, b = b, a
        last = pe.matmul(out, a, b, start=(i == 0), stop=(i == len(pairs) - 1))
    return last


def group_pairs(eng, body):
    G = T // 512
    with eng.Fori(0, G // 2 - 1) as i:
        for u in range(2):
            body(2 * i + u, i, u, True)
    for u in range(2):
        body(G - 2 + u, G // 2 - 1, u, u == 0)


def normalize_group(dve, h, stat, xn, g, u, done):
    for t in range(4):
        tile = bass.ds(4 * g + t, 1)
        for lo, n, c in ((0, D, 0), (D, 64, 128)):
            ins = dve.tensor_scalar(xn[:, u, t:t + 1, lo:lo + n], h[:, tile, c:c + n],
                                    stat[:, tile, 0], stat[:, tile, 1], ALU.subtract, ALU.mult)
    ins.then_inc(done, 1)


def transpose_group(pe, ps, xn, u, ident, done, bank=0):
    for k in range(2):
        for t in range(4):
            last = pe.transpose(ps[:, bank + k, 128 * t:128 * t + 128], xn[:, u, t, 128 * k:128 * k + 128], ident[:, :])
    last.then_inc(done, 1)


def raw_weights(fbuf):
    return [f[:, :, :].rearrange("p b t -> p (b t)")[:, 0:3 * H * HD] for f in fbuf]


def project(nc, A, S, h, ident, stat, epsc, fbuf):
    G = T // 512
    WQ = H * HD
    with ExitStack() as ctx:
        m = Mem(nc, ctx, "project")
        xhi = m.sb("xhi", [128, B, NT], F32R)
        xlo = m.sb("xlo", [128, B, NT], F32R)
        xmix = m.sb("xmix", [128, B, NT], F32R)
        vhi = m.sb("vhi", [128, 2, 512], F32R)
        vlo = m.sb("vlo", [128, 2, 512], F32R)
        vmix = m.sb("vmix", [128, 2, 512], F32R)
        whi, wlo = m.sb("whi", [128, 3 * WQ], F32R), m.sb("wlo", [128, 3 * WQ], F32R)
        w2hi, w2lo = m.sb("w2hi", [128, 3 * WQ], F32R), m.sb("w2lo", [128, 3 * WQ], F32R)
        cq = [m.sb(f"cq{i}", [128, 3, 128, 4], F32R) for i in range(4)]
        krow = m.sb("krow", [128, 2])
        vrow = m.sb("vrow", [1, 2, WQ])
        rk = m.sb("rk", [HD, 128])
        rk0 = m.sb("rk0", [HD, 32])
        std = m.sb("std", [128, NTILE])
        ps = m.psum("ps_proj", [128, 8, 512])

        s_c, s_wq = m.sem("proj_tables_loaded"), m.sem("wqt_loaded")
        s_std, s_rstd = m.sem("std_ready"), m.sem("rstd_ready")
        s_rk = m.sem("tables_ready")
        s_cp, s_chi, s_clo = m.sem("composed"), m.sem("composed_hi"), m.sem("composed_lo")
        s_whi, s_wlo = m.sem("w_hi_made"), m.sem("w_lo_made")
        s_xn, s_tr = m.sem("normed"), m.sem("x_transposed")
        s_hi, s_lo = m.sem("x_hi_made"), m.sem("x_lo_made")
        s_vx = [m.sem(f"v_operand_copied{i}") for i in range(2)]
        s_vused = m.sem("v_operand_used")
        s_q, s_k, s_v = m.sem("q_product"), m.sem("k_product"), m.sem("v_product")
        s_qe, s_ke, s_ve = m.sem("q_read"), m.sem("k_read"), m.sem("v_read")
        s_k0, s_v0 = m.sem("key0_done"), m.sem("value0_done")
        s_qst = [m.sem(f"q_stored{i}") for i in range(2)]
        s_kst = [m.sem(f"k_stored{i}") for i in range(2)]
        s_vst = [m.sem(f"v_stored{i}") for i in range(4)]
        s_f, s_fa, s_fd = m.sem("f_product"), m.sem("f_read_act"), m.sem("f_read_dve")
        s_fz = m.sem("f_zeroed")
        s_fst = [m.sem(f"f_stored{i}") for i in range(2)]

        rawa, rawb = raw_weights(fbuf)
        wqt = fbuf[0][0:HD, :, :].rearrange("p b t -> p (b t)")[:, 0:H * 256].rearrange("p (h n) -> p h n", h=H)
        vst = fbuf[1][:, :, :].rearrange("p b t -> p (b t)")[:, 0:4 * WQ].rearrange("p (s n) -> p s n", s=4)
        xn = m.sb("xn", [128, 2, 4, 256])
        qst, kst = m.sb("q_stage", [128, 2, 512]), m.sb("k_stage", [128, 2, 512])

        blocks = [(0, 1, 1, 96, 0)]
        blocks += [(1 + SIDE * a, SIDE, 1, 16 - a, 0) for a in range(ROWS)]
        blocks += [(1 + c, ROWS, SIDE, 48 + 14 - c, 1) for c in range(SIDE)]
        NB = len(blocks)

        def pair_of_images(ap):
            return ap.rearrange("p (b t) -> p b t", b=2)

        def store_feature_waits(n_blocks):
            return (n_blocks + 1) // 2, n_blocks // 2

        def read_feature(eng, n, done):
            q, (first, count, step, _, k) = n // NB, blocks[n % NB]
            if q:
                eng.wait_ge(s_fst[k], 16 * q)
            eng.wait_ge(s_f, n + 1)
            dst = fbuf[k][:, :, first:first + (count - 1) * step + 1:step].rearrange("p b t -> p t b")
            src = ps[:, n % 8, 0:count * B].rearrange("p (t b) -> p t b", b=B)
            if done is s_fa:
                eng.activation(dst, src, ACT.Copy).then_inc(done, 1)
            else:
                eng.tensor_copy(dst, src).then_inc(done, 1)

        with nc.Block() as block:

            @block.sync
            def _(sp):
                sp.dma_start(rk[:, :], A["rk"]).then_inc(s_c, 16)
                sp.dma_start(rk0[:, :], A["rk0"]).then_inc(s_c, 16)
                sp.dma_start(krow[:, :], A["krow"]).then_inc(s_c, 16)
                sp.dma_start(vrow[:, :, :], A["vrow"].rearrange("(o r) n -> o r n", o=1)).then_inc(s_c, 16)
                sp.wait_ge(s_wlo, 2)
                sp.dma_start(wqt[:, :, :], A["wqt"]).then_inc(s_wq, 16)

                def group(g, r, u, more):
                    sp.wait_ge(s_vused, g + 1)
                    sp.wait_ge(s_hi, 2 * g + 2)
                    sp.wait_ge(s_lo, 2 * g + 2)
                    for dst, src in ((vhi, xhi), (vlo, xlo), (vmix, xmix)):
                        sp.dma_start(pair_of_images(dst[:, u, :]).bitcast(F32), src[:, bass.ds(2 * g, 2), :].bitcast(F32)).then_inc(s_vx[u], 16)
                    for j in range(6):
                        sp.wait_ge(s_qe, 6 * g + j + 3)
                        sp.dma_start(S["q"][128 * j:128 * j + 128, bass.ds(g * 512, 512)], qst[:, j % 2, :])\
                            .then_inc(s_qst[j % 2], 16)
                        sp.wait_ge(s_k0, 6 * g + j + 1)
                        sp.dma_start(S["k"][128 * j:128 * j + 128, bass.ds(g * 512, 512)], kst[:, j % 2, :])\
                            .then_inc(s_kst[j % 2], 16)
                    for t in range(4):
                        if t % 2 == 0:
                            sp.wait_ge(s_v0, 2 * g + t // 2 + 1)
                        else:
                            sp.wait_ge(s_ve, 8 * g + 2 * t + 4)
                        sp.dma_start(S["v"][bass.ds(g * 512 + 128 * t, 128), :], vst[:, t, :]).then_inc(s_vst[t], 16)

                group_pairs(sp, group)
                for q in range(3):
                    for k in range(2):
                        na, nd = store_feature_waits(NB * q + (NB if k else 1 + ROWS))
                        sp.wait_ge(s_fa, na)
                        sp.wait_ge(s_fd, nd)
                        if k:
                            sp.wait_ge(s_fz, 1)
                        sp.dma_start(S["f"][q, k], fbuf[k][0:4 * ROWS, :, :].rearrange("p b t -> p (b t)"))\
                            .then_inc(s_fst[k], 16)
                for q in s_fst:
                    sp.wait_ge(q, 48)

            @block.vector
            def _(dve):
                dve.sem_inc(s_ke, 2)
                for q in s_kst:
                    dve.sem_inc(q, 16)
                dve.wait_ge(s_std, 1)
                dve.reciprocal(stat[:, :, 1], std[:, :]).then_inc(s_rstd, 1)
                dve.wait_ge(s_rstd, 1)
                normalize_group(dve, h, stat, xn, 0, 0, s_xn)
                dve.wait_ge(s_c, 64)
                dve.tensor_tensor(rk[:, 96:128], rk[:, 96:128], rk0[:, :], ALU.add).then_inc(s_rk, 1)
                dve.tensor_tensor(krow[:, 0:1], krow[:, 0:1], krow[:, 1:2], ALU.add).then_inc(s_rk, 1)
                dve.tensor_tensor(vrow[:, 0, :], vrow[:, 0, :], vrow[:, 1, :], ALU.add).then_inc(s_rk, 1)
                for k, (lo, hi, raw) in enumerate(((wlo, whi, rawa), (w2lo, w2hi, rawb))):
                    dve.wait_ge(s_whi, k + 1)
                    dve.tensor_tensor(lo[:, :], raw[:, :], hi[:, :].bitcast(F32), ALU.subtract).then_inc(s_wlo, 1)
                dve.wait_ge(s_rk, 3)

                def composed_lo(j):
                    q, half = divmod(j, 2)
                    dve.wait_ge(s_chi, j + 1)
                    dve.tensor_tensor(cq[2 * half + 1][:, q, :, :].rearrange("p t h -> p h t"),
                                      ps[:, j % 2, :].rearrange("p (h t) -> p h t", h=4),
                                      cq[2 * half][:, q, :, :].rearrange("p t h -> p h t").bitcast(F32),
                                      ALU.subtract).then_inc(s_clo, 1)

                def lo_parts(g):
                    cols = bass.ds(2 * g, 2)
                    dve.wait_ge(s_hi, 2 * g + 1)
                    dve.tensor_tensor(xlo[:, cols, :], pair_of_images(ps[:, 0, :]), xhi[:, cols, :].bitcast(F32),
                                      ALU.subtract).then_inc(s_lo, 1)
                    dve.wait_ge(s_hi, 2 * g + 2)
                    dve.tensor_tensor(xmix[64:128, cols, :], pair_of_images(ps[64:128, 1, :]),
                                      xmix[64:128, cols, :].bitcast(F32), ALU.subtract).then_inc(s_lo, 1)

                lo_parts(0)

                def group(g, r, u, more):
                    if more:
                        dve.wait_ge(s_tr, g + 1)
                        normalize_group(dve, h, stat, xn, g + 1, 1 - u, s_xn)
                    for j in range(6):
                        if j == 3 and more:
                            lo_parts(g + 1)
                        dve.wait_ge(s_k, 6 * g + j + 1)
                        dve.wait_ge(s_kst[j % 2], 16 * (3 * g + j // 2) + 16)
                        dve.tensor_copy(kst[:, j % 2, :], ps[:, 4 + j % 2, :]).then_inc(s_ke, 1)
                        dve.wait_ge(s_ke, 6 * g + j + 3)
                        k0 = pair_of_images(kst[:, j % 2, :])[:, :, 0]
                        dve.tensor_scalar(k0, k0, krow[:, 0:1], None, ALU.add).then_inc(s_k0, 1)
                        if not more:
                            composed_lo(j)
                    for t in (0, 2):
                        dve.wait_ge(s_ve, 8 * g + 2 * t + 4)
                        dve.tensor_tensor(vst[0:1, t, :], vst[0:1, t, :], vrow[:, 0, :], ALU.add).then_inc(s_v0, 1)

                group_pairs(dve, group)
                dve.wait_ge(s_wlo, 2)
                for q in s_vst:
                    dve.wait_ge(q, 16 + 16 * G)
                dve.memset(fbuf[1][:, :, 0], 0.0).then_inc(s_fz, 1)
                for n in range(1, 3 * NB, 2):
                    read_feature(dve, n, s_fd)

            @block.scalar
            def _(act):
                act.sem_inc(s_qe, 2)
                act.sem_inc(s_ve, 2)
                for q in s_qst + s_vst:
                    act.sem_inc(q, 16)
                act.activation(std[:, :], stat[:, :, 1], ACT.Sqrt, bias=epsc[:, 0:1]).then_inc(s_std, 1)
                act.activation(whi[:, :], rawa[:, :], ACT.Copy).then_inc(s_whi, 1)
                act.activation(w2hi[:, :], rawb[:, :], ACT.Copy).then_inc(s_whi, 1)

                def composed_hi(j):
                    q, half = divmod(j, 2)
                    act.wait_ge(s_cp, j + 1)
                    act.activation(cq[2 * half][:, q, :, :].rearrange("p t h -> p h t"),
                                   ps[:, j % 2, :].rearrange("p (h t) -> p h t", h=4), ACT.Copy).then_inc(s_chi, 1)

                def hi_parts(g):
                    cols = bass.ds(2 * g, 2)
                    act.wait_ge(s_tr, g + 1)
                    act.activation(xhi[:, cols, :], pair_of_images(ps[:, 0, :]), ACT.Copy).then_inc(s_hi, 1)
                    act.activation(xmix[:, cols, :], pair_of_images(ps[:, 1, :]), ACT.Copy).then_inc(s_hi, 1)

                hi_parts(0)

                def group(g, r, u, more):
                    for j in range(6):
                        if j == 3 and more:
                            hi_parts(g + 1)
                        act.wait_ge(s_q, 6 * g + j + 1)
                        act.wait_ge(s_qst[j % 2], 16 * (3 * g + j // 2) + 16)
                        act.activation(qst[:, j % 2, :], ps[:, 2 + j % 2, :], ACT.Copy).then_inc(s_qe, 1)
                        if not more:
                            composed_hi(j)
                    for t in range(4):
                        act.wait_ge(s_vst[t], 16 * g + 16)
                        for half in range(2):
                            act.wait_ge(s_v, 8 * g + 2 * t + half + 1)
                            act.activation(vst[:, t, 384 * half:384 * half + 384], ps[:, 6 + half, 0:384],
                                           ACT.Copy).then_inc(s_ve, 1)

                group_pairs(act, group)
                act.wait_ge(s_wlo, 2)
                for q in s_vst:
                    act.wait_ge(q, 16 + 16 * G)
                for n in range(0, 3 * NB, 2):
                    read_feature(act, n, s_fa)

            @block.tensor
            def _(pe):

                def compose(j):
                    q, half = divmod(j, 2)
                    if j == 0:
                        pe.wait_ge(s_rk, 1)
                        pe.wait_ge(s_wq, 16)
                    if j >= 2:
                        pe.wait_ge(s_clo, j - 1)
                    for i in range(4):
                        last = pe.matmul(ps[:, j % 2, 128 * i:128 * i + 128], wqt[:, 4 * q + i, 128 * half:128 * half + 128],
                                         rk[:, :], start=True, stop=True)
                    last.then_inc(s_cp, 1)

                pe.wait_ge(s_xn, 1)
                transpose_group(pe, ps, xn, 0, ident, s_tr)
                pe.wait_ge(s_wlo, 2)

                def group(g, r, u, more):
                    cols = bass.ds(2 * g, 2)
                    x = (xhi[:, cols, :], xlo[:, cols, :], xmix[:, cols, :])
                    pe.wait_ge(s_hi, 2 * g + 2)
                    pe.wait_ge(s_lo, 2 * g + 2)
                    for j in range(6):
                        if j == 2 and more:
                            pe.wait_ge(s_xn, g + 2)
                            transpose_group(pe, ps, xn, 1 - u, ident, s_tr)
                        for read, done, bank, off in ((s_qe, s_q, 2, 0), (s_ke, s_k, 4, WQ)):
                            pe.wait_ge(read, 6 * g + j + 1)
                            c = slice(off + 128 * j, off + 128 * j + 128)
                            five_passes(pe, ps[:, bank + j % 2, :], (whi[:, c], wlo[:, c], w2hi[:, c], w2lo[:, c]),
                                        x).then_inc(done, 1)
                        if not more:
                            compose(j)
                    pe.wait_ge(s_vx[u], 48 * (r + 1))
                    for t in range(4):
                        tok = slice(128 * t, 128 * t + 128)
                        for half in range(2):
                            pe.wait_ge(s_ve, 8 * g + 2 * t + half + 1)
                            c = slice(2 * WQ + 384 * half, 2 * WQ + 384 * half + 384)
                            last = five_passes(pe, ps[:, 6 + half, 0:384], (whi[:, c], wlo[:, c], w2hi[:, c], w2lo[:, c]),
                                               (vhi[:, u, tok], vlo[:, u, tok], vmix[:, u, tok]), x_stationary=True)
                            last.then_inc(s_v, 1)
                    pe.sem_inc(s_vused, 1)

                pe.sem_inc(s_vused, 2)
                group_pairs(pe, group)
                pe.wait_ge(s_clo, 6)
                for s, n in ((s_qe, 6 * G + 2), (s_ke, 6 * G + 2), (s_ve, 8 * G + 2), (s_lo, 2 * G)):
                    pe.wait_ge(s, n)
                for n in range(3 * NB):
                    q, (first, count, step, window, _) = n // NB, blocks[n % NB]
                    if n >= 8:
                        pe.wait_ge(s_fd if n % 2 else s_fa, (n - 8) // 2 + 1)
                    tok = slice(first, first + (count - 1) * step + 1, step)
                    rows = [c[:, q, window:window + 32, :].rearrange("p t h -> p (t h)") for c in cq]
                    five_passes(pe, ps[:, n % 8, 0:count * B], rows,
                                [x[:, :, tok].rearrange("p b t -> p t b") for x in (xhi, xlo, xmix)]).then_inc(s_f, 1)


def attend(nc, A, S, h, ident, w):
    SCALE = HD ** -0.5
    with ExitStack() as ctx:
        m = Mem(nc, ctx, "attend")
        qf = m.sb("qf", [128, H, NT])
        kf = m.sb("kf", [128, H, NT])
        vg = m.sb("vg", [128, 2, H, 128])
        prob = m.sb("prob", [128, 3, 2, NT])
        probt = m.sb("probt", [128, 2, 2, NT])
        otp = m.sb("otp", [128, 2, NT])
        wp = m.sb("wp", [128, 6, D])
        mx, nm = m.sb("mx", [128, 2, 2]), m.sb("neg_max", [128, 2, 2])
        den, rden = m.sb("den", [128, 2, 2]), m.sb("rden", [128, 2, 2])
        ps_s = m.psum("ps_scores", [128, 2, 512])
        ps_t = m.psum("ps_probt", [128, 2, 512])
        ps_o = m.psum("ps_out", [128, 2, 512])
        ps_y = m.psum("ps_y", [128, 2, 512])

        s_c = [m.sem(f"indicators_loaded{q}") for q in range(3)]
        s_ci, s_cp = m.sem("value_indicators_loaded"), m.sem("weights_loaded")
        s_ld = [m.sem(f"quad_loaded{q}") for q in range(3)]
        s_z = m.sem("features_zeroed")
        s_s = m.sem("scores")
        s_mx, s_nm = m.sem("max_done"), m.sem("neg_max_done")
        s_e = m.sem("exp_done")
        s_r = m.sem("rden_done")
        s_p0, s_p1 = m.sem("prob_tile0_done"), m.sem("prob_tile1_done")
        s_t = m.sem("prob_transposed")
        s_pt = m.sem("probt_copied")
        s_o = m.sem("head_out")
        s_oe = m.sem("head_out_read")
        s_pr = m.sem("pair_projected")
        s_y = m.sem("y_added")

        def lagged(b, hd, lag):
            n = 12 * b + hd - lag
            if hd - lag < 0:
                return b - 1, hd - lag + H, n
            if hd - lag >= H:
                return b + 1, hd - lag - H, n
            return b, hd - lag, n

        def steps(eng, step):
            for hd in range(H):
                step(0, hd, lambda lag, hd=hd: hd - lag >= 0)
            with eng.Fori(1, B) as b:
                for hd in range(H):
                    step(b, hd, lambda lag: True)
            for hd in range(H, H + 5):
                step(B - 1, hd, lambda lag, hd=hd: hd - lag < H)

        with nc.Block() as block:

            @block.sync
            def _(sp):

                def image(b):
                    cols = bass.ds(b * NT, NT)
                    for q in range(3):
                        sp.wait_ge(s_o, 12 * b + 4 * q + 4)
                        sp.dma_start(qf[0:64, 4 * q:4 * q + 4, :],
                                     S["q"][256 * q:256 * q + 256, cols].rearrange("(h d) t -> d h t", h=4)).then_inc(s_ld[q], 16)
                        sp.dma_start(kf[0:64, 4 * q:4 * q + 4, :],
                                     S["k"][256 * q:256 * q + 256, cols].rearrange("(h d) t -> d h t", h=4)).then_inc(s_ld[q], 16)
                        if isinstance(b, int):
                            sp.dma_start(kf[64:128, 4 * q:4 * q + 4, :], A["ind"].rearrange("f (o t) -> f o t", o=1)
                                         .to_broadcast([64, 4, NT])).then_inc(s_c[q], 16)
                            sp.wait_ge(s_z, q + 1)
                        for k in range(2):
                            sp.dma_start(qf[64 + 32 * k:64 + 32 * k + ROWS, 4 * q:4 * q + 4, :],
                                         S["f"][q, k, :, cols].rearrange("(r h) t -> r h t", h=4)).then_inc(s_ld[q], 16)
                        for j in range(2):
                            sp.dma_start(vg[:, j, 4 * q:4 * q + 4, 0:64],
                                         S["v"][bass.ds(b * NT + 128 * j, 128), 256 * q:256 * q + 256]
                                         .rearrange("p (h d) -> p h d", h=4)).then_inc(s_ld[q], 16)

                image(0)
                with sp.Fori(1, B) as b:
                    image(b)

            @block.vector
            def _(dve):
                for q in range(3):
                    dve.memset(qf[64:128, 4 * q:4 * q + 4, :], 0.0).then_inc(s_z, 1)
                dve.sem_inc(s_pt, 2)
                dve.sem_inc(s_y, 2)

                def step(b, hd, live):
                    if live(1) and hd - 1 < H:
                        _, g, n = lagged(b, hd, 1)
                        dve.wait_ge(s_e, n + 3)
                        dve.reciprocal(rden[:, g % 2, :], den[:, g % 2, :]).then_inc(s_r, 1)
                        dve.wait_ge(s_r, n + 1)
                        dve.tensor_scalar(prob[:, g % 3, 0, :], prob[:, g % 3, 0, :], rden[:, g % 2, 0:1], None,
                                          ALU.mult).then_inc(s_p0, 1)
                    if hd < H:
                        _, _, n = lagged(b, hd, 0)
                        dve.wait_ge(s_s, n + 1)
                        dve.tensor_reduce(mx[:, hd % 2, :], ps_s[:, hd % 2, :].rearrange("p (i j) -> p i j", i=2),
                                          AX.X, ALU.max).then_inc(s_mx, 1)
                        dve.wait_ge(s_mx, n + 1)
                        dve.tensor_scalar(nm[:, hd % 2, :], mx[:, hd % 2, :], -SCALE, None, ALU.mult).then_inc(s_nm, 1)
                    if live(2) and hd - 2 < H:
                        _, g, n = lagged(b, hd, 2)
                        dve.wait_ge(s_t, n + 4)
                        dve.tensor_copy(probt[:, g % 2, :, :].rearrange("p j i -> p (j i)"), ps_t[:, g % 2, :]).then_inc(s_pt, 1)
                    if hd == 4 and live(5):
                        add_y(b - 1)

                def add_y(b):
                    for it in range(2):
                        dve.wait_ge(s_pr, 6 * b + 8)
                        tile = h[:, bass.ds(2 * b + it, 1), :]
                        dve.tensor_tensor(tile, ps_y[:, it, 0:D].rearrange("p (o n) -> p o n", o=1), tile, ALU.add).then_inc(s_y, 1)

                steps(dve, step)
                add_y(B - 1)

            @block.scalar
            def _(act):
                act.sem_inc(s_e, 2)
                act.sem_inc(s_oe, 2)
                act.wait_ge(s_ld[0], 96)
                for j in range(2):
                    act.dma_start(vg[:, j, :, 64:128], A["indt"][:, j:j + 1, :].to_broadcast([128, H, 64])).then_inc(s_ci, 16)
                act.dma_start(wp[:, :, :], A["wproj"].rearrange("(m p) n -> p m n", p=128)).then_inc(s_cp, 16)

                def step(b, hd, live):
                    if live(1) and hd - 1 < H:
                        _, g, n = lagged(b, hd, 1)
                        act.wait_ge(s_r, n + 1)
                        act.activation(prob[:, g % 3, 1, :], prob[:, g % 3, 1, :], ACT.Copy,
                                       scale=rden[:, g % 2, 1:2]).then_inc(s_p1, 1)
                    if hd < H:
                        _, _, n = lagged(b, hd, 0)
                        act.wait_ge(s_nm, n + 1)
                        act.wait_ge(s_t, n + 1)
                        for it in range(2):
                            ins = act.activation(prob[:, hd % 3, it, :], ps_s[:, hd % 2, NT * it:NT * it + NT], ACT.Exp,
                                                 bias=nm[:, hd % 2, it:it + 1], scale=SCALE,
                                                 accum_out=den[:, hd % 2, it:it + 1])
                        ins.then_inc(s_e, 1)
                    if live(3) and hd - 3 < H:
                        gb, g, n = lagged(b, hd, 3)
                        act.wait_ge(s_o, n + 1 + H)
                        act.wait_ge(s_pr, 6 * gb + g // 2 + 1)
                        half = 64 * (g % 2)
                        act.activation(otp[half:half + 64, (g // 2) % 2, :], ps_o[0:64, g % 2, 0:NT], ACT.Copy)
                        q, hq = divmod(g, 4)
                        for kind in range(2):
                            ins = act.activation(w[32 * hq:32 * hq + 32, kind, q, bass.ds(gb, 1), :],
                                                 ps_o[64 + 32 * kind:96 + 32 * kind, g % 2, 0:NT]
                                                 .rearrange("p (o t) -> p o t", o=1), ACT.Copy)
                        ins.then_inc(s_oe, 1)

                steps(act, step)

            @block.tensor
            def _(pe):
                pe.sem_inc(s_t, 3)
                pe.sem_inc(s_o, H)
                pe.sem_inc(s_pr, 2)

                def step(b, hd, live):
                    if hd < H:
                        _, _, n = lagged(b, hd, 0)
                        if hd % 4 == 0:
                            pe.wait_ge(s_ld[hd // 4], 96 * b + 96)
                            if isinstance(b, int) and b == 0:
                                pe.wait_ge(s_c[hd // 4], 16)
                        pe.wait_ge(s_e, n + 1)
                        for it in range(2):
                            last = pe.matmul(ps_s[:, hd % 2, NT * it:NT * it + NT], qf[:, hd, 128 * it:128 * it + 128],
                                             kf[:, hd, :], start=True, stop=True)
                        last.then_inc(s_s, 1)
                    if live(2) and hd - 2 < H:
                        _, g, n = lagged(b, hd, 2)
                        pe.wait_ge(s_p0, n + 1)
                        pe.wait_ge(s_p1, n + 1)
                        pe.wait_ge(s_pt, n + 1)
                        for jt in range(2):
                            for it in range(2):
                                last = pe.transpose(ps_t[:, g % 2, NT * jt + 128 * it:NT * jt + 128 * it + 128],
                                                    prob[:, g % 3, it, 128 * jt:128 * jt + 128], ident[:, :])
                        last.then_inc(s_t, 1)
                    if live(3) and hd - 3 < H:
                        _, g, n = lagged(b, hd, 3)
                        pe.wait_ge(s_pt, n + 3)
                        pe.wait_ge(s_oe, n + 1)
                        if isinstance(n, int) and n == 0:
                            pe.wait_ge(s_ci, 32)
                        for jt in range(2):
                            last = pe.matmul(ps_o[:, g % 2, 0:NT], vg[:, jt, g, :], probt[:, g % 2, jt, :],
                                             start=(jt == 0), stop=(jt == 1))
                        last.then_inc(s_o, 1)
                    if live(4) and hd - 4 < H and hd % 2 == 1:
                        gb, g, n = lagged(b, hd, 4)
                        p = g // 2
                        if p == 0:
                            pe.wait_ge(s_cp, 16)
                            pe.wait_ge(s_y, 2 * gb + 2)
                        pe.wait_ge(s_oe, n + 3)
                        for it in range(2):
                            last = pe.matmul(ps_y[:, it, 0:D], otp[:, p % 2, 128 * it:128 * it + 128], wp[:, p, :],
                                             start=(p == 0), stop=(p == 5))
                        last.then_inc(s_pr, 1)

                steps(pe, step)


def relative(nc, A, S, h, ident, stat, w):
    with ExitStack() as ctx:
        m = Mem(nc, ctx, "relative")
        yt = m.sb("yt", [128, B, NT])
        yt2 = m.sb("yt2", [64, B, NT])
        win = m.sb("rw_window", [128, 4, 3, D])
        bias, bias2 = m.sb("bias", [128, 1]), m.sb("bias2", [64, 1])
        yst = m.sb("y_stage", [128, 4, D])
        raw = m.sb("rel_bn", [128, 2, 6])
        ps = m.psum("ps_rel", [128, 8, 512])

        s_c = m.sem("rel_consts_loaded")
        s_win = [m.sem(f"window_loaded{i}") for i in range(4)]
        s_y, s_ya, s_yc = m.sem("y_product"), m.sem("y_rows_read"), m.sem("y_columns_added")
        s_t, s_ys, s_h = m.sem("y_transposed"), m.sem("y_staged"), m.sem("h_updated")
        s_bn, s_agg = m.sem("bn2_stats_done"), m.sem("bn2_aggregated")

        blocks = [(0, 1, 1, 96, 0)]
        blocks += [(1 + SIDE * a, SIDE, 1, 16 - a, 0) for a in range(ROWS)]
        blocks += [(1 + c, ROWS, SIDE, 48 + 14 - c, 1) for c in range(SIDE)]
        NA = 1 + ROWS
        rows = S["rw"].rearrange("t (h q) n -> t h q n", q=3)

        def tokens(ap, n):
            first, count, step, _, _ = blocks[n]
            return ap[:, :, first:first + (count - 1) * step + 1:step]

        def product(n, part):
            lo, rows = ((0, 128), (1, 64))[part]
            count = blocks[n][1]
            return ps[0:rows, 2 * (n % 4) + lo, 0:B * count].rearrange("p (b t) -> p b t", b=B)

        with nc.Block() as block:

            @block.sync
            def _(sp):
                sp.dma_start(bias[:, :], A["bproj"][0:128].rearrange("(p o) -> p o", o=1)).then_inc(s_c, 16)
                sp.dma_start(bias2[:, :], A["bproj"][128:192].rearrange("(p o) -> p o", o=1)).then_inc(s_c, 16)
                for n in range(len(blocks)):
                    if n >= 4:
                        sp.wait_ge(s_y, n - 3)
                    for hq in range(4):
                        sp.dma_start(win[32 * hq:32 * hq + 32, n % 4, :, :],
                                     rows[blocks[n][3]:blocks[n][3] + 32, hq, :, :]).then_inc(s_win[n % 4], 16)

            @block.scalar
            def _(act):
                act.wait_ge(s_c, 32)
                for n in range(len(blocks)):
                    act.wait_ge(s_y, n + 1)
                    if n < NA:
                        act.activation(tokens(yt, n), product(n, 0), ACT.Identity, bias=bias[:, 0:1])
                        act.activation(tokens(yt2, n), product(n, 1), ACT.Identity, bias=bias2[:, 0:1]).then_inc(s_ya, 1)
                for t in range(NTILE):
                    act.wait_ge(s_t, t + 1)
                    if t >= 4:
                        act.wait_ge(s_h, t - 3)
                    act.activation(yst[:, t % 4, :], ps[:, t % 8, 0:D], ACT.Copy).then_inc(s_ys, 1)

            @block.vector
            def _(dve):
                dve.wait_ge(s_ya, NA)
                for n in range(NA, len(blocks)):
                    dve.wait_ge(s_y, n + 1)
                    dve.tensor_tensor(tokens(yt, n), product(n, 0), tokens(yt, n), ALU.add)
                    dve.tensor_tensor(tokens(yt2, n), product(n, 1), tokens(yt2, n), ALU.add).then_inc(s_yc, 1)
                for t in range(NTILE):
                    norm_stats(dve, h, stat, raw, t, NTILE, s_h, s_bn, s_agg)

            @block.gpsimd
            def _(pool):
                for t in range(NTILE):
                    pool.wait_ge(s_ys, t + 1)
                    pool.tensor_tensor(h[:, t, :], yst[:, t % 4, :], h[:, t, :], ALU.add).then_inc(s_h, 1)

            @block.tensor
            def _(pe):
                for n in range(len(blocks)):
                    if n >= 4:
                        if n - 4 < NA:
                            pe.wait_ge(s_ya, n - 3)
                        else:
                            pe.wait_ge(s_yc, n - 3 - NA)
                    pe.wait_ge(s_win[n % 4], 64 * (n // 4 + 1))
                    for part, c in ((0, slice(0, 128)), (1, slice(128, D))):
                        for q in range(3):
                            last = pe.matmul(product(n, part), win[:, n % 4, q, c], tokens(w[:, blocks[n][4], q], n),
                                             start=(q == 0), stop=(q == 2))
                    last.then_inc(s_y, 1)
                pe.wait_ge(s_yc, SIDE)
                for t in range(NTILE):
                    if t >= 8:
                        pe.wait_ge(s_ys, t - 7)
                    b, i = t // 2, t % 2
                    pe.transpose(ps[:, t % 8, 0:128], yt[:, b, 128 * i:128 * i + 128], ident[:, :])
                    pe.transpose(ps[:, t % 8, 128:D], yt2[:, b, 128 * i:128 * i + 128], ident[0:64, 0:64]).then_inc(s_t, 1)


def pipeline(eng, n, body):
    for u in range(2):
        body(u, 0, u, u > 0, True)
    with eng.Fori(1, n // 2 - 1) as i:
        for u in range(2):
            body(2 * i + u, i, u, True, True)
    for u in range(2):
        body(n - 2 + u, n // 2 - 1, u, True, u == 0)


ROW = 256 + E


def score(nc, A, S, h, ident, stat, epsc, x, scores, raw, parts, consts):
    G = T // 512
    xhi, xlo, xmix = x
    with ExitStack() as ctx:
        m = Mem(nc, ctx, "score")
        s_sw, s_k = m.sem("shared_weights_loaded"), m.sem("constants_loaded")
        s_shi, s_slo = m.sem("shared_hi_made"), m.sem("shared_lo_made")
        rawa, rawb = m.sb("raw_a", [128, E]), m.sb("raw_b", [128, E])
        whi, wlo = m.sb("w_hi", [128, E], F32R), m.sb("w_lo", [128, E], F32R)
        w2hi, w2lo = m.sb("w2_hi", [128, E], F32R), m.sb("w2_lo", [128, E], F32R)
        std = m.sb("std", [128, NTILE])
        xn = m.sb("xn", [128, 2, 4, 256])
        rsc = m.sb("token_scores", [128, 2, 4, E])
        sct = m.sb("scores_t", [E, 2, 512])
        ps = m.psum("ps", [128, 8, 512])

        s_w = m.sem("weights_loaded")
        s_std, s_rstd = m.sem("std_ready"), m.sem("rstd_ready")
        s_whi, s_wlo = m.sem("w_hi_made"), m.sem("w_lo_made")
        s_xn, s_tr = m.sem("normed"), m.sem("x_transposed")
        s_hi, s_lo = m.sem("x_hi_made"), m.sem("x_lo_made")
        s_gt, s_sc = m.sem("gate_product"), m.sem("scores_ready")
        s_st, s_row = m.sem("scores_transposed"), m.sem("row_ready")
        s_go = m.sem("pe_wait_passed")
        s_xd = [m.sem(f"row_stored{i}") for i in range(2)]
        s_rd = [m.sem(f"row_scores_stored{i}") for i in range(2)]
        s_sd = [m.sem(f"scores_stored{i}") for i in range(2)]

        with nc.Block() as block:

            @block.sync
            def _(sp):
                sp.dma_start(rawa[:, :], A["gate"][0:128, :]).then_inc(s_w, 16)
                for half in (0, 64):
                    sp.dma_start(rawb[half:half + 64, :], A["gate"][128:192, :]).then_inc(s_w, 16)
                for dst, name in zip(raw, ("wsgu_a", "wsgu_b", "wsd")):
                    sp.dma_start(dst, A[name]).then_inc(s_sw, 16)
                for name, dst in consts.items():
                    sp.dma_start(dst, A[name]).then_inc(s_k, 16)

                def store_scores(g, u):
                    sp.wait_ge(s_sc, g + 1)
                    sp.dma_start(S["scores"][bass.ds(16 * g, 16), :], sct[:, u, :]).then_inc(s_sd[u], 16)
                    sp.wait_ge(s_row, g + 1)
                    sp.dma_start(rows(g)[:, :, 256:ROW], rsc[:, u, :, :]).then_inc(s_rd[u], 16)

                def rows(g):
                    return S["rows"][bass.ds(g * 512, 512), :].rearrange("(t p) c -> p t c", p=128)

                def body(g, r, u, before, after):
                    sp.wait_ge(s_xn, g + 1)
                    sp.dma_start(rows(g)[:, :, 0:256], xn[:, u, :, :]).then_inc(s_xd[u], 16)
                    if before:
                        store_scores(g - 1, 1 - u)
                    if not after:
                        store_scores(g, u)

                pipeline(sp, G, body)
                for u in range(2):
                    sp.wait_ge(s_sd[u], 16 + 16 * G // 2)
                    sp.wait_ge(s_xd[u], 16 + 16 * G // 2)
                    sp.wait_ge(s_rd[u], 16 + 16 * G // 2)
                sp.dma_start(scores[:, :], S["scores"]).then_inc(s_w, 16)
                sp.wait_ge(s_w, 16 * 4)
                sp.wait_ge(s_k, 16 * len(consts))

            @block.gpsimd
            def _(pool):
                for k, (full, (hi, lo)) in enumerate(zip(raw, parts)):
                    pool.wait_ge(s_shi, k + 1)
                    pool.tensor_tensor(lo, full, hi.bitcast(F32), ALU.subtract).then_inc(s_slo, 1)

            @block.vector
            def _(dve):
                dve.wait_ge(s_std, 1)
                dve.reciprocal(stat[:, :, 1], std[:, :]).then_inc(s_rstd, 1)
                dve.wait_ge(s_rstd, 1)
                dve.wait_ge(s_xd[0], 16)
                normalize_group(dve, h, stat, xn, 0, 0, s_xn)
                for k, (lo, hi, full) in enumerate(((wlo, whi, rawa), (w2lo, w2hi, rawb))):
                    dve.wait_ge(s_whi, k + 1)
                    dve.tensor_tensor(lo[:, :], full[:, :], hi[:, :].bitcast(F32), ALU.subtract).then_inc(s_wlo, 1)

                def body(g, r, u, before, after):
                    if after:
                        dve.wait_ge(s_xd[1 - u], 16 * (r + u) + 16)
                        if before:
                            dve.wait_ge(s_tr, g)
                        normalize_group(dve, h, stat, xn, g + 1, 1 - u, s_xn)
                    cols = bass.ds(g * 512, 512)
                    dve.wait_ge(s_hi, 2 * g + 1)
                    dve.tensor_tensor(xlo[:, cols], ps[:, 2 * u, :], xhi[:, cols].bitcast(F32), ALU.subtract).then_inc(s_lo, 1)
                    dve.wait_ge(s_hi, 2 * g + 2)
                    dve.tensor_tensor(xmix[64:128, cols], ps[64:128, 2 * u + 1, :], xmix[64:128, cols].bitcast(F32),
                                      ALU.subtract).then_inc(s_lo, 1)

                pipeline(dve, G, body)

            @block.scalar
            def _(act):
                for q in s_xd + s_sd + s_rd:
                    act.sem_inc(q, 16)
                act.activation(std[:, :], stat[:, :, 1], ACT.Sqrt, bias=epsc[:, 0:1]).then_inc(s_std, 1)
                act.wait_ge(s_w, 16 * 3)
                for hi, full in ((whi, rawa), (w2hi, rawb)):
                    act.activation(hi[:, :], full[:, :], ACT.Copy).then_inc(s_whi, 1)

                def finish(g, r, u):
                    act.wait_ge(s_gt, g + 1)
                    act.wait_ge(s_sd[u], 16 * r + 16)
                    act.activation(sct[:, u, :], ps[0:E, 4 + u, :], ACT.Sigmoid).then_inc(s_sc, 1)
                    act.wait_ge(s_st, g + 1)
                    act.wait_ge(s_rd[u], 16 * r + 16)
                    act.activation(rsc[:, u, :, :], ps[:, 6 + u, 0:4 * E].rearrange("p (t e) -> p t e", t=4),
                                   ACT.Copy).then_inc(s_row, 1)

                def body(g, r, u, before, after):
                    cols = bass.ds(g * 512, 512)
                    act.wait_ge(s_tr, g + 1)
                    act.activation(xhi[:, cols], ps[:, 2 * u, :], ACT.Copy).then_inc(s_hi, 1)
                    act.activation(xmix[:, cols], ps[:, 2 * u + 1, :], ACT.Copy).then_inc(s_hi, 1)
                    if isinstance(g, int) and g == 1:
                        act.wait_ge(s_sw, 48)
                        for full, (hi, _) in zip(raw, parts):
                            act.activation(hi, full, ACT.Copy).then_inc(s_shi, 1)
                    if before:
                        finish(g - 1, r + u - 1, 1 - u)
                    if not after:
                        finish(g, r, u)

                pipeline(act, G, body)

            @block.tensor
            def _(pe):
                pe.wait_ge(s_wlo, 2)

                def finish(g, r, u):
                    pe.wait_ge(s_lo, 2 * g + 2)
                    cols = bass.ds(g * 512, 512)
                    five_passes(pe, ps[0:E, 4 + u, :], (whi[:, :], wlo[:, :], w2hi[:, :], w2lo[:, :]),
                                (xhi[:, cols], xlo[:, cols], xmix[:, cols])).then_inc(s_gt, 1)

                def turn(g, u):
                    pe.wait_ge(s_sc, g + 1)
                    pe.sem_inc(s_go, 1)
                    for t in range(4):
                        last = pe.transpose(ps[:, 6 + u, E * t:E * t + E], sct[:, u, 128 * t:128 * t + 128], ident[0:E, 0:E])
                    last.then_inc(s_st, 1)

                def body(g, r, u, before, after):
                    if before and not (isinstance(g, int) and g < 2):
                        pe.wait_ge(s_lo, 2 * g - 2)
                        pe.wait_ge(s_row, g - 1)
                    pe.wait_ge(s_xn, g + 1)
                    transpose_group(pe, ps, xn, u, ident, s_tr, 2 * u)
                    if before:
                        finish(g - 1, r, 1 - u)
                        turn(g - 1, 1 - u)
                    if not after:
                        finish(g, r, u)
                        turn(g, u)

                pipeline(pe, G, body)


def share(nc, out, h, x, scores, limit, parts, consts):
    G = T // 512
    NF = FS // 128
    PER_GROUP = 4
    xhi, xlo, xmix = x
    with ExitStack() as ctx:
        m = Mem(nc, ctx, "share")
        (whi, wlo), (w2hi, w2lo), (wdhi, wdlo) = parts
        same, bits = consts["same_expert"], consts["bits"]
        sg = m.sb("silu", [128, 2, 512])
        a = m.sb("act", [128, 2, 512])
        ahi, alo = m.sb("act_hi", [128, 2, NF, 512], F32R), m.sb("act_lo", [128, 2, NF, 512], F32R)
        ost = m.sb("out_stage", [128, 2, 4, D])
        cand, cnt, keep = m.sb("candidate", [128, 1], I32), m.sb("partial_count", [128, 1]), m.sb("kept_candidate", [128, 1])
        mask = m.sb("mask", [128, 512])
        ps = m.psum("ps", [128, 8, 512])

        s_gu, s_sg = m.sem("gate_up_product"), m.sem("silu_done")
        s_a, s_ahi, s_alo = m.sem("act_made"), m.sem("act_hi_made"), m.sem("act_lo_made")
        s_d, s_o = m.sem("down_product"), m.sem("out_made")
        s_os = [m.sem(f"out_stored{i}") for i in range(2)]
        s_v, s_n, s_tot = m.sem("bit_step"), m.sem("counted"), m.sem("total_ready")

        with nc.Block() as block:

            @block.sync
            def _(sp):
                def store_out(g, u):
                    sp.wait_ge(s_o, 4 * g + 6)
                    sp.dma_start(out[bass.ds(g * 512, 512), :].rearrange("(t p) c -> p t c", p=128),
                                 ost[:, u, :, :]).then_inc(s_os[u], 16)

                pipeline(sp, G, lambda g, r, u, before, after: store_out(g, u))
                for u in range(2):
                    sp.wait_ge(s_os[u], 16 + 16 * G // 2)

            @block.vector
            def _(dve):
                dve.sem_inc(s_o, 2)
                dve.memset(limit[:, :], 0).then_inc(s_v, 1)

                def guess(i):
                    dve.wait_ge(s_v, 3 * i + 1)
                    dve.tensor_tensor(cand[:, :], bits[:, bass.ds(i, 1)], limit[:, :], ALU.bitwise_or).then_inc(s_v, 1)
                    dve.wait_ge(s_v, 3 * i + 2)
                    dve.tensor_scalar(mask[:, :], scores[:, :], cand[:, 0:1].bitcast(F32), 0.0, ALU.is_ge, ALU.add,
                                      accum_out=cnt[:, 0:1]).then_inc(s_n, 1)

                def settle(i):
                    dve.wait_ge(s_tot, i + 1)
                    dve.tensor_scalar(keep[:, :], ps[:, 0, 0:1], float(CAP), cand[:, 0:1].bitcast(F32), ALU.is_ge,
                                      ALU.mult).then_inc(s_v, 1)
                    dve.wait_ge(s_v, 3 * i + 3)
                    dve.tensor_tensor(limit[:, :].bitcast(F32), limit[:, :].bitcast(F32), keep[:, :], ALU.max).then_inc(s_v, 1)

                def add_shared(g, u, tiles):
                    for t in tiles:
                        if t == 0:
                            dve.wait_ge(s_os[u], 8 * (g - u) + 16)
                        dve.wait_ge(s_d, 4 * g + t + 1)
                        dve.tensor_tensor(ost[:, u, t:t + 1, :], ps[:, 6 + t % 2, 0:D].rearrange("p (o n) -> p o n", o=1),
                                          h[:, bass.ds(4 * g + t, 1), :], ALU.add).then_inc(s_o, 1)

                def body(g, r, u, before, after):
                    bit = PER_GROUP * g
                    for j in range(NF):
                        k = (u + j) % 2
                        dve.wait_ge(s_sg, NF * g + j + 1)
                        dve.tensor_tensor(a[:, k, :], sg[:, k, :], ps[:, 4 + k, :], ALU.mult).then_inc(s_a, 1)
                        if j == 0 and before:
                            add_shared(g - 1, 1 - u, (0, 1))
                            settle(bit - 1)
                        if j > 0:
                            settle(bit + j)
                        if j < 2:
                            guess(bit + (j + 1 if j else 0))
                        dve.wait_ge(s_ahi, NF * g + j + 1)
                        dve.tensor_tensor(alo[:, u, j, :], a[:, k, :], ahi[:, u, j, :].bitcast(F32), ALU.subtract)\
                            .then_inc(s_alo, 1)
                        if j == 0:
                            if before:
                                add_shared(g - 1, 1 - u, (2, 3))
                            settle(bit)
                            guess(bit + 1)
                        if j == 2:
                            guess(bit + 3)
                    if not after:
                        settle(bit + 3)
                        add_shared(g, u, range(4))

                pipeline(dve, G, body)

            @block.scalar
            def _(act):
                for q in s_os:
                    act.sem_inc(q, 16)

                def body(g, r, u, before, after):
                    for j in range(NF):
                        k = (u + j) % 2
                        act.wait_ge(s_gu, NF * g + j + 1)
                        act.activation(sg[:, k, :], ps[:, 2 + k, :], ACT.Silu).then_inc(s_sg, 1)
                        act.wait_ge(s_a, NF * g + j + 1)
                        act.activation(ahi[:, u, j, :], a[:, k, :], ACT.Copy).then_inc(s_ahi, 1)

                pipeline(act, G, body)

            @block.tensor
            def _(pe):
                def total(i):
                    pe.wait_ge(s_n, i + 1)
                    pe.matmul(ps[:, 0, 0:1], same[:, :], cnt[:, :], start=True, stop=True).then_inc(s_tot, 1)

                def down(g, u, tiles):
                    for t in tiles:
                        tok = slice(128 * t, 128 * t + 128)
                        pe.wait_ge(s_o, 4 * g + t + 1)
                        n = 0
                        for f in range(NF):
                            if t == 0:
                                pe.wait_ge(s_alo, NF * g + f + 1)
                            for v, w in ((ahi, wdhi), (ahi, wdlo), (alo, wdhi)):
                                last = pe.matmul(ps[:, 6 + t % 2, 0:D], v[:, u, f, tok], w[:, f, :],
                                                 start=(n == 0), stop=(n == 3 * NF - 1))
                                n += 1
                        last.then_inc(s_d, 1)

                def body(g, r, u, before, after):
                    cols = bass.ds(g * 512, 512)
                    v = (xhi[:, cols], xlo[:, cols], xmix[:, cols])
                    bit = PER_GROUP * g
                    for j in range(NF):
                        k = (u + j) % 2
                        if not (isinstance(g, int) and NF * g + j < 2):
                            pe.wait_ge(s_a, NF * g + j - 1)
                        for bank, c in ((2, 128 * j), (4, FS + 128 * j)):
                            c = slice(c, c + 128)
                            last = five_passes(pe, ps[:, bank + k, :], (whi[:, c], wlo[:, c], w2hi[:, c], w2lo[:, c]), v)
                        last.then_inc(s_gu, 1)
                        if j > 0:
                            total(bit + j)
                        else:
                            if before:
                                down(g - 1, 1 - u, (0, 1))
                                total(bit - 1)
                                down(g - 1, 1 - u, (2, 3))
                            total(bit)
                    if not after:
                        total(bit + 3)
                        down(g, u, range(4))

                pipeline(pe, G, body)


def select(nc, A, S, ident, scores, limit, weights, consts):
    CH_N = 512
    BF16 = mybir.dt.bfloat16
    with ExitStack() as ctx:
        m = Mem(nc, ctx, "select")
        same, earlier, count, part, tile_no = (consts[k] for k in ("same_expert", "earlier_chunk", "count",
                                                                   "partition", "tile_number"))
        cnt = m.sb("partial_count", [128, 2])
        mask = m.sb("mask", [128, CH_N])
        gt, eq, rank, sel, place = (m.sb(n, [128, CH_N]) for n in ("above", "equal", "rank", "chosen", "place"))
        room = m.sb("room", [128, 1])
        pl, hi, lo = (m.sb(n, [128, CH_N], I32) for n in ("place_int", "place_hi", "place_lo"))
        hif, lof = m.sb("place_hi_f", [128, CH_N]), m.sb("place_lo_f", [128, CH_N])
        hit, lot = m.sb("place_hi_t", [128, E, 32]), m.sb("place_lo_t", [128, E, 32])
        hot = m.sb("one_hot_hi", [128, 4, 32, 32], BF16)
        low = m.sb("one_hot_lo", [128, 4, 32, 16], BF16)
        val = m.sb("values", [128, 4, 2, 32, 16], BF16)
        ids = m.sb("ids", [32, E, 16], I32)
        idf = m.sb("tile_part", [32, E, 16])
        ps_c = m.psum("ps_count", [128, 512])
        ps_t = m.psum("ps_places", [128, 2, 512])
        ps_i = m.psum("ps_ids", [128, 512])

        s_w = m.sem("first_weights_loaded")
        s_v = m.sem("select_step")
        s_n, s_tot = m.sem("counted"), m.sem("total_ready")
        s_pf, s_tr, s_te = m.sem("places_ready"), m.sem("places_transposed"), m.sem("places_read")
        s_hot, s_low = m.sem("hi_ready"), m.sem("lo_ready")
        s_vp, s_vt = m.sem("partition_values_ready"), m.sem("tile_values_ready")
        s_id = m.sem("ids_product")
        s_out, s_st = m.sem("ids_ready"), m.sem("ids_stored")

        with nc.Block() as block:

            @block.sync
            def _(sp):
                for e in range(2):
                    load_gate_up(sp, A, weights, e, e, s_w)
                    load_down(sp, A, weights, e, e, s_w)
                sp.wait_ge(s_w, 2 * 4 * 16)
                sp.wait_ge(s_out, 1)
                sp.dma_start(S["ids"].rearrange("e (a b) -> a e b", b=16), ids[:, :, :]).then_inc(s_st, 16)
                sp.wait_ge(s_st, 16)

            @block.vector
            def _(dve):
                dve.sem_inc(s_id, 4)
                n = 0

                def step(ins):
                    nonlocal n
                    n += 1
                    ins.then_inc(s_v, 1)
                    dve.wait_ge(s_v, n)

                least = limit[:, 0:1].bitcast(F32)
                dve.tensor_scalar(gt[:, :], scores[:, :], least, 0.0, ALU.is_gt, ALU.add, accum_out=cnt[:, 0:1])
                dve.tensor_scalar(eq[:, :], scores[:, :], least, 0.0, ALU.is_equal, ALU.add, accum_out=cnt[:, 1:2]).then_inc(s_n, 1)
                dve.wait_ge(s_n, 1)
                step(dve.tensor_tensor_scan(rank[:, :], eq[:, :], eq[:, :], 0.0, ALU.add, ALU.max))
                dve.wait_ge(s_tot, 1)
                step(dve.tensor_scalar(room[:, :], ps_c[:, 0:1], -1.0, float(CAP), ALU.mult, ALU.add))
                step(dve.scalar_tensor_tensor(mask[:, :], rank[:, :], room[:, 0:1], eq[:, :], ALU.is_le, ALU.mult))
                step(dve.tensor_tensor(sel[:, :], mask[:, :], gt[:, :], ALU.add))
                dve.tensor_tensor_scan(rank[:, :], sel[:, :], sel[:, :], 0.0, ALU.add, ALU.max).then_inc(s_n, 1)
                dve.wait_ge(s_tot, 2)
                step(dve.scalar_tensor_tensor(place[:, :], rank[:, :], ps_c[:, 0:1], sel[:, :], ALU.add, ALU.mult))
                step(dve.tensor_scalar(pl[:, :], place[:, :], -1.0, None, ALU.add))
                dve.tensor_scalar(hi[:, :], pl[:, :], 4, None, ALU.arith_shift_right)
                step(dve.tensor_scalar(lo[:, :], pl[:, :], 15, None, ALU.bitwise_and))
                dve.tensor_copy(hif[:, :], hi[:, :])
                dve.tensor_copy(lof[:, :], lo[:, :]).then_inc(s_pf, 1)
                dve.wait_ge(s_te, 2)

                def pattern(n):
                    return count[:, 0:n].rearrange("p (o n) -> p o n", o=1).to_broadcast([128, 32, n])

                with dve.Fori(0, E // 4) as r:
                    for u in range(4):
                        e = 4 * r + u
                        col = bass.ds(e, 1)
                        dve.wait_ge(s_id, e + 1)
                        dve.tensor_tensor(low[:, u, :, :], lot[:, col, :].rearrange("p o q -> p q o").to_broadcast([128, 32, 16]),
                                          pattern(16), ALU.is_equal).then_inc(s_low, 1)
                        dve.tensor_tensor(hot[:, u, :, :], hit[:, col, :].rearrange("p o q -> p q o").to_broadcast([128, 32, 32]),
                                          pattern(32), ALU.is_equal).then_inc(s_hot, 1)
                dve.wait_ge(s_id, E + 4)
                both = ps_i[0:32, :].rearrange("p (e k b) -> p e k b", k=2, b=16)
                step(dve.tensor_copy(idf[:, :, :], both[:, :, 0, :]))
                dve.scalar_tensor_tensor(ids[:, :, :], both[:, :, 1, :], 128.0, idf[:, :, :], ALU.mult, ALU.add).then_inc(s_out, 1)

            @block.gpsimd
            def _(pool):
                with pool.Fori(0, E // 4) as r:
                    for u in range(4):
                        pool.wait_ge(s_low, 4 * r + u + 1)
                        pool.tensor_tensor(val[:, u, 1, :, :], low[:, u, :, :],
                                           tile_no[:, :].rearrange("p (q o) -> p q o", o=1).to_broadcast([128, 32, 16]),
                                           ALU.mult).then_inc(s_vt, 1)

            @block.scalar
            def _(act):
                for k, (dst, n) in enumerate(((hit, 0), (lot, 1))):
                    act.wait_ge(s_tr, k + 1)
                    act.activation(dst[:, :, :].rearrange("p e (j c) -> p j c e", j=4),
                                   ps_t[:, n, :].rearrange("p (j c e) -> p j c e", j=4, c=8), ACT.Copy).then_inc(s_te, 1)
                with act.Fori(0, E // 4) as r:
                    for u in range(4):
                        act.wait_ge(s_low, 4 * r + u + 1)
                        act.activation(val[:, u, 0, :, :], low[:, u, :, :], ACT.Copy, scale=part[:, 0:1]).then_inc(s_vp, 1)

            @block.tensor
            def _(pe):
                pe.wait_ge(s_n, 1)
                pe.matmul(ps_c[:, 0:1], same[:, :], cnt[:, 0:1], start=True, stop=False)
                pe.matmul(ps_c[:, 0:1], earlier[:, :], cnt[:, 1:2], start=False, stop=True).then_inc(s_tot, 1)
                pe.wait_ge(s_n, 2)
                pe.matmul(ps_c[:, 0:1], earlier[:, :], rank[:, CH_N - 1:CH_N], start=True, stop=True).then_inc(s_tot, 1)
                pe.wait_ge(s_pf, 1)
                for n, src in ((0, hif), (1, lof)):
                    for j in range(4):
                        last = pe.transpose(ps_t[:, n, 128 * j:128 * j + 128], src[:, 128 * j:128 * j + 128], ident[:, :])
                    last.then_inc(s_tr, 1)
                with pe.Fori(0, E // 4) as r:
                    for u in range(4):
                        e = 4 * r + u
                        pe.wait_ge(s_hot, e + 1)
                        pe.wait_ge(s_vp, e + 1)
                        pe.wait_ge(s_vt, e + 1)
                        for q in range(32):
                            last = pe.matmul(ps_i[0:32, bass.ds(32 * e, 32)], hot[:, u, q, :], val[:, u, :, q, :],
                                             start=(q == 0), stop=(q == 31))
                        last.then_inc(s_id, 1)


def load_gate_up(sp, A, weights, e, u, done):
    one = bass.ds(e, 1)
    rawa, rawb, _ = weights
    sp.dma_start(rawa[:, u:u + 1, :], A["wgu"][one, 0:128, :].rearrange("o p f -> p o f")).then_inc(done, 16)
    for half in (0, 64):
        sp.dma_start(rawb[half:half + 64, u:u + 1, :], A["wgu"][one, 128:192, :].rearrange("o p f -> p o f")).then_inc(done, 16)


def load_down(sp, A, weights, e, u, done):
    one = bass.ds(e, 1)
    sp.dma_start(weights[2][:, u:u + 1, :, :], A["wd"][one, :, :, :].rearrange("o p k n -> p o k n")).then_inc(done, 16)


def experts(nc, A, S, out, ident, weights):
    NF = FE // 128
    W = 2 * FE
    NT4 = CAP // 128
    with ExitStack() as ctx:
        m = Mem(nc, ctx, "experts")
        rawa, rawb, rawd = weights
        whi, wlo = m.sb("ewhi", [128, 2, W], F32R), m.sb("ewlo", [128, 2, W], F32R)
        w2hi, w2lo = m.sb("ew2hi", [128, 2, W], F32R), m.sb("ew2lo", [128, 2, W], F32R)
        wdhi, wdlo = m.sb("ewdhi", [128, 2, NF, D], F32R), m.sb("ewdlo", [128, 2, NF, D], F32R)
        idx = m.sb("token_numbers", [128, 2, NT4], I32)
        kept = m.sb("kept_numbers", [128, 2, NT4], I32)
        xg = m.sb("gathered", [128, 2, NT4, ROW])
        xhi, xlo, xmix = (m.sb(n, [128, 2, 512], F32R) for n in ("xghi", "xglo", "xgmix"))
        sc = m.sb("chosen_scores", [128, 2, NT4, 1])
        sg = m.sb("e_silu", [128, 2, 512])
        a = m.sb("e_act", [128, 2, 512])
        ahi, alo = m.sb("e_act_hi", [128, 2, NF, 512], F32R), m.sb("e_act_lo", [128, 2, NF, 512], F32R)
        y = m.sb("y_stage", [128, 2, NT4, D])
        ps = m.psum("ps_experts", [128, 8, 512])

        s_w = [m.sem(f"expert_weights_loaded{i}") for i in range(2)]
        s_wd = [m.sem(f"down_weights_loaded{i}") for i in range(2)]
        s_ix = [m.sem(f"numbers_loaded{i}") for i in range(2)]
        s_g = [m.sem(f"tokens_gathered{i}") for i in range(2)]
        s_whi, s_wlo = m.sem("expert_hi_made"), m.sem("expert_lo_made")
        s_w2lo = m.sem("expert_lo2_made")
        s_wdhi, s_wdlo = m.sem("down_hi_made"), m.sem("down_lo_made")
        s_tr, s_hi, s_lo = m.sem("xg_transposed"), m.sem("xg_hi_made"), m.sem("xg_lo_made")
        s_gu, s_sg = m.sem("e_gate_up_product"), m.sem("e_silu_done")
        s_a, s_ahi, s_alo = m.sem("e_act_made"), m.sem("e_act_hi_made"), m.sem("e_act_lo_made")
        s_sc = m.sem("chosen_scores_ready")
        s_d, s_y = m.sem("e_down_product"), m.sem("y_ready")
        s_kept = m.sem("numbers_kept")
        s_sct = m.sem("y_scattered")
        s_go = m.sem("pool_waits_passed")

        with nc.Block() as block:

            @block.sync
            def _(sp):
                def body(e, r, u, before, after):
                    one = bass.ds(e, 1)
                    if not opening(r):
                        sp.wait_ge(s_g[u], 64 * r)
                        sp.wait_ge(s_kept, e - 1)
                    sp.dma_start(idx[:, u, :].rearrange("p (o k) -> p o k", o=1),
                                 S["ids"][one, :].rearrange("o (p k) -> p o k", p=128)).then_inc(s_ix[u], 16)
                    if not opening(r):
                        sp.wait_ge(s_w2lo, e - 1)
                        sp.wait_ge(s_wlo, e - 1)
                        load_gate_up(sp, A, weights, e, u, s_w[u])
                        sp.wait_ge(s_wdlo, e - 1)
                        load_down(sp, A, weights, e, u, s_wd[u])

                pipeline(sp, E, body)

            @block.gpsimd
            def _(pool):
                def gather(u):
                    for k in range(NT4):
                        pool.indirect_dma_start(
                            out=xg[:, u, k, :], out_offset=None, in_=S["rows"],
                            in_offset=bass.IndirectOffsetOnAxis(ap=idx[:, u, k:k + 1].bitcast(U32), axis=0)).then_inc(s_g[u], 16)

                def scatter(e, u):
                    if not (isinstance(e, int) and e == 0):
                        pool.wait_ge(s_sct, 64 * e)
                    for k in range(NT4):
                        pool.wait_ge(s_y, NT4 * e + k + 3)
                        pool.sem_inc(s_go, 1)
                        pool.indirect_dma_start(
                            out=out, in_=y[:, u, k, :], in_offset=None, compute_op=ALU.add,
                            out_offset=bass.IndirectOffsetOnAxis(ap=kept[:, u, k:k + 1].bitcast(U32), axis=0)).then_inc(s_sct, 16)

                def body(e, r, u, before, after):
                    if after:
                        pool.wait_ge(s_whi, 2 * e + 4)
                        pool.sem_inc(s_go, 1)
                        weights_lo(1 - u, rawb, w2hi, w2lo, s_w2lo)
                    if before:
                        scatter(e - 1, 1 - u)
                    if not opening(r):
                        pool.wait_ge(s_sct, 64 * e - 64)
                    pool.sem_inc(s_go, 1)
                    pool.tensor_copy(kept[:, u, :], idx[:, u, :]).then_inc(s_kept, 1)
                    if not isinstance(e, int) or e + 2 < E:
                        pool.wait_ge(s_ix[u], 16 * r + 32)
                        pool.wait_ge(s_tr, e + 1)
                        pool.wait_ge(s_sc, e + 1)
                        pool.sem_inc(s_go, 1)
                        gather(u)
                    if after:
                        pool.wait_ge(s_wdhi, e + 2)
                        pool.sem_inc(s_go, 1)
                        weights_lo(1 - u, rawd, wdhi, wdlo, s_wdlo)
                    pool.wait_ge(s_kept, e + 1)
                    pool.sem_inc(s_go, 1)
                    if not after:
                        scatter(e, u)

                def weights_lo(u, raw, hi, lo, done):
                    ix = (slice(None), u) + (slice(None),) * (len(raw.shape) - 2)
                    pool.tensor_tensor(lo[ix], raw[ix], hi[ix].bitcast(F32), ALU.subtract).then_inc(done, 1)

                for u in range(2):
                    pool.wait_ge(s_ix[u], 16)
                    gather(u)
                pool.wait_ge(s_wdhi, 1)
                weights_lo(0, rawd, wdhi, wdlo, s_wdlo)
                pipeline(pool, E, body)
                pool.wait_ge(s_sct, 64 * E)

            @block.scalar
            def _(act):
                def weights_hi(u, n, part):
                    if part < 2:
                        if not (isinstance(n, int) and n == 0):
                            act.wait_ge(s_w[u], n * 48)
                        raw, hi = ((rawa, whi), (rawb, w2hi))[part]
                        act.activation(hi[:, u, :], raw[:, u, :], ACT.Copy).then_inc(s_whi, 1)
                    else:
                        if not (isinstance(n, int) and n == 0):
                            act.wait_ge(s_wd[u], n * 16)
                        act.activation(wdhi[:, u, :, :], rawd[:, u, :, :], ACT.Copy).then_inc(s_wdhi, 1)

                def hi_parts(e, u):
                    act.wait_ge(s_tr, e + 1)
                    act.activation(xhi[:, u, :], ps[:, 0, :], ACT.Copy).then_inc(s_hi, 1)
                    act.activation(xmix[:, u, :], ps[:, 1, :], ACT.Copy).then_inc(s_hi, 1)

                weights_hi(0, 0, 0)
                weights_hi(0, 0, 1)
                hi_parts(0, 0)
                weights_hi(0, 0, 2)

                def body(e, r, u, before, after):
                    for j in range(NF):
                        act.wait_ge(s_gu, NF * e + j + 1)
                        act.activation(sg[:, j % 2, :], ps[:, 2 + j % 2, :], ACT.Silu).then_inc(s_sg, 1)
                        act.wait_ge(s_a, NF * e + j + 1)
                        act.activation(ahi[:, u, j, :], a[:, j % 2, :], ACT.Copy).then_inc(s_ahi, 1)
                        if after and j == 1:
                            weights_hi(1 - u, r + u, 0)
                            weights_hi(1 - u, r + u, 1)
                        if after and j == 2:
                            if before:
                                act.wait_ge(s_d, NT4 * e)
                            weights_hi(1 - u, r + u, 2)
                        if after and j == 3:
                            hi_parts(e + 1, 1 - u)

                pipeline(act, E, body)

            @block.vector
            def _(dve):
                dve.sem_inc(s_y, 2)

                def weights_lo(e, u):
                    dve.wait_ge(s_whi, 2 * e + 1)
                    dve.tensor_tensor(wlo[:, u, :], rawa[:, u, :], whi[:, u, :].bitcast(F32), ALU.subtract).then_inc(s_wlo, 1)

                def lo_parts(e, u, n):
                    dve.wait_ge(s_hi, 2 * e + 1)
                    dve.tensor_tensor(xlo[:, u, :], ps[:, 0, :], xhi[:, u, :].bitcast(F32), ALU.subtract).then_inc(s_lo, 1)
                    dve.wait_ge(s_hi, 2 * e + 2)
                    dve.tensor_tensor(xmix[64:128, u, :], ps[64:128, 1, :], xmix[64:128, u, :].bitcast(F32),
                                      ALU.subtract).then_inc(s_lo, 1)
                    dve.wait_ge(s_g[u], 64 * n)
                    dve.tensor_copy(sc[:, u, :, :], xg[:, u, :, bass.ds(256 + e, 1)]).then_inc(s_sc, 1)

                def weigh(e, u):
                    dve.wait_ge(s_sc, e + 1)
                    if not (isinstance(e, int) and e < 2):
                        dve.wait_ge(s_sct, 64 * e - 64)
                    for t in range(NT4):
                        dve.wait_ge(s_d, NT4 * e + t + 1)
                        dve.tensor_scalar(y[:, u, t, :], ps[:, 6 + t % 2, 0:D], sc[:, u, t, 0:1], None,
                                          ALU.mult).then_inc(s_y, 1)

                weights_lo(0, 0)
                dve.wait_ge(s_whi, 2)
                dve.tensor_tensor(w2lo[:, 0, :], rawb[:, 0, :], w2hi[:, 0, :].bitcast(F32), ALU.subtract).then_inc(s_w2lo, 1)
                lo_parts(0, 0, 1)

                def body(e, r, u, before, after):
                    for j in range(NF):
                        dve.wait_ge(s_sg, NF * e + j + 1)
                        dve.tensor_tensor(a[:, j % 2, :], sg[:, j % 2, :], ps[:, 4 + j % 2, :], ALU.mult).then_inc(s_a, 1)
                        dve.wait_ge(s_ahi, NF * e + j + 1)
                        dve.tensor_tensor(alo[:, u, j, :], a[:, j % 2, :], ahi[:, u, j, :].bitcast(F32), ALU.subtract)\
                            .then_inc(s_alo, 1)
                        if j == 1 and before:
                            weigh(e - 1, 1 - u)
                        if after and j == 1:
                            weights_lo(e + 1, 1 - u)
                        if after and j == 3:
                            lo_parts(e + 1, 1 - u, r + u + 1)
                    if not after:
                        weigh(e, u)

                pipeline(dve, E, body)

            @block.tensor
            def _(pe):
                pe.wait_ge(s_g[0], 64)
                transpose_group(pe, ps, xg, 0, ident, s_tr)

                def down(e, u):
                    pe.wait_ge(s_wdlo, e + 1)
                    for t in range(NT4):
                        tok = slice(128 * t, 128 * t + 128)
                        pe.wait_ge(s_y, NT4 * e + t + 1)
                        n = 0
                        for f in range(NF):
                            if t == 0:
                                pe.wait_ge(s_alo, NF * e + f + 1)
                            for x, w in ((ahi, wdhi), (ahi, wdlo), (alo, wdhi)):
                                last = pe.matmul(ps[:, 6 + t % 2, 0:D], x[:, u, f, tok], w[:, u, f, :],
                                                 start=(n == 0), stop=(n == 3 * NF - 1))
                                n += 1
                        last.then_inc(s_d, 1)

                def body(e, r, u, before, after):
                    x = (xhi[:, u, :], xlo[:, u, :], xmix[:, u, :])
                    pe.wait_ge(s_wlo, e + 1)
                    pe.wait_ge(s_w2lo, e + 1)
                    pe.wait_ge(s_hi, 2 * e + 2)
                    pe.wait_ge(s_lo, 2 * e + 2)
                    for j in range(NF):
                        if before or j >= 2:
                            pe.wait_ge(s_a, NF * e + j - 1)
                        for bank, c in ((2, 128 * j), (4, FE + 128 * j)):
                            c = slice(c, c + 128)
                            last = five_passes(pe, ps[:, bank + j % 2, :],
                                               (whi[:, u, c], wlo[:, u, c], w2hi[:, u, c], w2lo[:, u, c]), x)
                        last.then_inc(s_gu, 1)
                        if j == 1 and before:
                            down(e - 1, 1 - u)
                        if j == 3 and after:
                            pe.wait_ge(s_g[1 - u], 64 * (r + u) + 64)
                            transpose_group(pe, ps, xg, 1 - u, ident, s_tr)
                    if not after:
                        down(e, u)

                pipeline(pe, E, body)


def opening(r):
    return isinstance(r, int) and r == 0


def vit_block(nc, A, out):
    def scratch(name, *shape, dt=F32):
        return nc.dram_tensor(name, shape, dt, kind="Internal").ap()

    S = {"q": scratch("q_scratch", H * HD, T), "k": scratch("k_scratch", H * HD, T), "v": scratch("v_scratch", T, H * HD),
         "f": scratch("feature_scratch", 3, 2, 4 * ROWS, T),
         "rw": scratch("value_table_scratch", 128, H, D), "scores": scratch("score_scratch", 128, T // 8),
         "rows": scratch("row_scratch", T, ROW), "ids": scratch("chosen_scratch", E, CAP, dt=I32)}
    Mem.spent.clear()
    with ExitStack() as ctx:
        m = Mem(nc, ctx, "all")
        ident = m.sb("ident", [128, 128])
        epsc = m.sb("eps", [128, 1])
        scores = m.sb("scores", [128, T // 8])
        limit = m.sb("lowest_chosen", [128, 1], I32)
        consts = {name: m.sb(name, A[name].shape, dt)[:, :]
                  for name, dt in (("same_expert", F32), ("bits", I32), ("earlier_chunk", F32), ("count", F32),
                                   ("partition", F32), ("tile_number", F32))}
        s_eps = m.sem("eps_ready")
        with ExitStack() as residual:
            r = Mem(nc, residual, "all")
            h = r.sb("h", [128, NTILE, D])
            stat = r.sb("stat", [128, NTILE, 2])
            with nc.Block() as block:
                @block.vector
                def _(dve):
                    dve.memset(epsc[:, :], EPS).then_inc(s_eps, 1)
            with ExitStack() as features:
                f = Mem(nc, features, "all")
                fbuf = [f.sb(f"f_{k}", [128, B, NT]) for k in "ac"]
                tokenize(nc, A, S, h, ident, stat, raw_weights(fbuf))
                project(nc, A, S, h, ident, stat, epsc, fbuf)
            with ExitStack() as sums:
                w = Mem(nc, sums, "all").sb("block_sums", [128, 2, 3, B, NT])
                attend(nc, A, S, h, ident, w)
                relative(nc, A, S, h, ident, stat, w)
                Mem.reclaim(nc)
            x = tuple(r.sb(name, [128, T], F32R) for name in ("x_hi", "x_lo", "x_mixed"))
            raw = (r.sb("shared_a", [128, 2 * FS])[:, :], r.sb("shared_b", [128, 2 * FS])[:, :],
                   r.sb("shared_down", [128, FS // 128, D])[:, :, :])
            parts = tuple((r.sb(f"shared_hi{k}", [128, *v.shape[1:]], F32R)[(slice(None),) * len(v.shape)],
                           r.sb(f"shared_lo{k}", [128, *v.shape[1:]], F32R)[(slice(None),) * len(v.shape)])
                          for k, v in enumerate(raw))
            score(nc, A, S, h, ident, stat, epsc, x, scores, raw, parts, consts)
            share(nc, out, h, x, scores, limit, parts, consts)
        weights = (m.sb("gate_up_a", [128, 2, 2 * FE]), m.sb("gate_up_b", [128, 2, 2 * FE]),
                   m.sb("down", [128, 2, FE // 128, D]))
        select(nc, A, S, ident, scores, limit, weights, consts)
        experts(nc, A, S, out, ident, weights)


def _layouts(x, L0_tok_W0, L0_tok_b0, L0_tok_W1, L0_tok_b1, L0_tok_W2, L0_tok_b2, L0_tok_Wf, L0_tok_bf,
             L0_tok_idx0, L0_tok_idx1, L0_tok_idx2, L0_attn_wq, L0_attn_wk, L0_attn_wv, L0_attn_wproj,
             L0_attn_bproj, L0_attn_rk_v, L0_attn_rk_h, L0_attn_rv_v, L0_attn_rv_h, L0_ffn_gate_weight,
             L0_ffn_Wg, L0_ffn_Wu, L0_ffn_Wd, L0_ffn_Ws_g, L0_ffn_Ws_u, L0_ffn_Ws_d):
    import numpy as np

    a = {k: np.asarray(v) for k, v in locals().items() if k != "np"}
    x = a["x"]

    def patches(p):
        n = IMG // p
        t = x.reshape(B, CH, n, p, n, p).transpose(2, 4, 0, 3, 5, 1)
        return t.reshape(n * n, B * p * p * CH)

    def rel(tv, th):
        z = np.zeros((HD, 128), np.float32)
        z0 = np.zeros((HD, 32), np.float32)
        for i in range(33):
            z[:, i] = tv[min(max(i - 16, -14), 14) + 15]
        for i in range(29):
            z[:, 48 + i] = th[i + 1]
        for i in range(ROWS):
            z[:, 96 + i] = tv[0]
            z0[:, i] = th[0]
        return z, z0

    rk, rk0 = rel(a["L0_attn_rk_v"], a["L0_attn_rk_h"])
    rv, rv0 = rel(a["L0_attn_rv_v"], a["L0_attn_rv_h"])
    row0 = np.stack([a["L0_attn_rk_v"][0], a["L0_attn_rk_h"][0]])
    rv_row0 = np.stack([np.tile(a["L0_attn_rv_v"][0], H), np.tile(a["L0_attn_rv_h"][0], H)])
    ind = np.zeros((64, NT), np.float32)
    for j in range(1, NT):
        ra, rc = divmod(j - 1, SIDE)
        ind[ra, j] = 1.0
        ind[32 + rc, j] = 1.0

    def rows128(w):
        return w[0:128], np.concatenate([w[128:192], w[128:192]])

    wqkv = np.concatenate([a["L0_attn_wq"], a["L0_attn_wk"], a["L0_attn_wv"]], axis=1)
    wqkv_a, wqkv_b = rows128(wqkv)
    wqt = a["L0_attn_wq"].T.reshape(H, HD, D).transpose(1, 0, 2)
    wqt = np.concatenate([wqt, wqt[:, :, 128:192]], axis=2)
    wsgu = np.concatenate([a["L0_ffn_Ws_g"].T, a["L0_ffn_Ws_u"].T], axis=1)
    wsgu_a, wsgu_b = rows128(wsgu)
    wgu = np.concatenate([a["L0_ffn_Wg"], a["L0_ffn_Wu"]], axis=1).transpose(0, 2, 1)
    gt = a["L0_ffn_gate_weight"].T
    out = {
        "x0": patches(1), "x1": patches(2), "x2": patches(4),
        "idx0t": a["L0_tok_idx0"].reshape(2, 128, GP).transpose(1, 0, 2).reshape(128, 2 * GP),
        "idx1t": a["L0_tok_idx1"].reshape(64, GP),
        "idx2t": a["L0_tok_idx2"].reshape(2, 128).T,
        "w0t": a["L0_tok_W0"].T, "w1t": a["L0_tok_W1"].T,
        "w2t": a["L0_tok_W2"].reshape(EMB, GP, 48).transpose(2, 1, 0),
        "wft": a["L0_tok_Wf"].T,
        "tokb": np.stack([a["L0_tok_b0"], a["L0_tok_b1"], a["L0_tok_b2"]], axis=1),
        "bf": a["L0_tok_bf"],
        "ident": np.eye(128, dtype=np.float32),
        "wqkv_a": wqkv_a, "wqkv_b": wqkv_b, "wqt": wqt,
        "rk": rk, "rk0": rk0, "rv": rv, "rv0": rv0,
        "krow": np.concatenate([row0, row0], axis=1).T,
        "vrow": rv_row0,
        "ind": ind,
        "indt": ind.T.reshape(2, 128, 64).transpose(1, 0, 2),
        "wproj": a["L0_attn_wproj"],
        "wproj_h": a["L0_attn_wproj"].reshape(3, 4, HD, D).transpose(2, 1, 0, 3).reshape(HD, H, D),
        "bproj": a["L0_attn_bproj"],
        "wsgu_a": wsgu_a, "wsgu_b": wsgu_b,
        "wsd": a["L0_ffn_Ws_d"].T.reshape(3, 128, D).transpose(1, 0, 2),
        "wgu": wgu,
        "wd": a["L0_ffn_Wd"].transpose(0, 2, 1).reshape(E, 6, 128, D).transpose(0, 2, 1, 3),
        "gate": gt,
        "same_expert": np.tile(np.eye(E, dtype=np.float32), (8, 8)),
        "earlier_chunk": np.kron(np.triu(np.ones((8, 8), np.float32), 1), np.eye(E, dtype=np.float32)),
        "bits": np.broadcast_to(np.append(1 << np.arange(29, -1, -1), [0, 0]).astype(np.int32), (128, 32)),
        "count": np.broadcast_to(np.arange(32, dtype=np.float32), (128, 32)),
        "partition": np.arange(128, dtype=np.float32)[:, None],
        "tile_number": np.broadcast_to((4 * np.arange(8)[None, :] + np.arange(4)[:, None]).astype(np.float32).reshape(32), (128, 32)),
    }
    return {k: np.ascontiguousarray(v) for k, v in out.items()}


def kernel(**inputs):
    import concourse.bacc as bacc
    from concourse.bass_utils import run_bass_kernel_spmd

    nc = bacc.Bacc("TRN2", target_bir_lowering=False, num_devices=1)
    arrays = _layouts(**inputs)
    A = {k: nc.dram_tensor(f"in_{k}", v.shape, mybir.dt.from_np(v.dtype), kind="ExternalInput").ap()
         for k, v in arrays.items()}
    out = nc.dram_tensor("out_h", (T, D), F32, kind="ExternalOutput").ap()
    vit_block(nc, A, out)
    r = run_bass_kernel_spmd(nc, [{f"in_{k}": v for k, v in arrays.items()}], core_ids=[0])
    return r.results[0]["out_h"].reshape(B, NT, D)
```
